# Optimizing a Trainium2 kernel written in Bass

```python
import numpy as np
import jax
import jax.numpy as jnp

def _softmax(x, axis=-1):
    return jax.nn.softmax(x, axis=axis)
def _gelu(x):
    return jax.nn.gelu(x, approximate=True)
def _silu(x):
    return jax.nn.silu(x)
def _sigmoid(x):
    return jax.nn.sigmoid(x)
def _layernorm(x, axis=-1, eps=1e-5):
    m = jnp.mean(x, axis=axis, keepdims=True)
    v = jnp.var(x, axis=axis, keepdims=True)
    return (x - m) / jnp.sqrt(v + eps)
def _scatter_add(tgt, idx, src, axis=0):
    return tgt.at[idx].add(src)
def _segment_sum(src, seg, n):
    return jax.ops.segment_sum(src, seg, n)

kernel_name = 'mk_conv_attn_hybrid_d2_conv_nchw256_7611d1'

def setup_inputs(seed: int = 0):
    np.random.seed(seed)
    _w = jnp.asarray
    def _rec_inputs():
        import jax
        import jax.numpy as jnp
        _gk = jax.random.key(seed)
        x = -0.0002928 + 1 * jax.random.normal(jax.random.fold_in(_gk, 1), (4, 256, 64, 64), jnp.float32)
        return x
    x = _rec_inputs()
    def _L0_conv_setup():
        import jax, jax.numpy as jnp
        import numpy as np
        BN_EPS = 1e-05
        K = 9

        def _conv3x3(x, w, b=None):
            out = jax.lax.conv_general_dilated(x, w, window_strides=(1, 1), padding=((1, 1), (1, 1)), dimension_numbers=('NCHW', 'OIHW', 'NCHW'))
            if b is not None:
                out = out + b[None, :, None, None]
            return out

        def _bilinear_gather(x, py, px):
            B, C, H, W = x.shape
            y0 = jnp.floor(py)
            x0 = jnp.floor(px)
            y1 = y0 + 1.0
            x1 = x0 + 1.0
            wy1 = py - y0
            wy0 = 1.0 - wy1
            wx1 = px - x0
            wx0 = 1.0 - wx1

            def corner(yc, xc, wgt):
                valid = ((yc >= 0) & (yc < H) & (xc >= 0) & (xc < W)).astype(x.dtype)
                yi = jnp.clip(yc, 0, H - 1).astype(jnp.int32)
                xi = jnp.clip(xc, 0, W - 1).astype(jnp.int32)
                v = jax.vmap(lambda img, a, b_: img[:, a, b_])(x, yi, xi)
                return v * (wgt * valid)[:, None]
            return corner(y0, x0, wy0 * wx0) + corner(y0, x1, wy0 * wx1) + corner(y1, x0, wy1 * wx0) + corner(y1, x1, wy1 * wx1)
        key = jax.random.key(seed)
        k1, k2, k3, k4 = jax.random.split(key, 4)
        B, CHI, CHO, H, W = (4, 256, 256, 64, 64)
        x = jax.random.normal(k1, (B, CHI, H, W), dtype=jnp.float32)
        w_off = jax.random.normal(k2, (2 * K, CHI, 3, 3), dtype=jnp.float32) * 0.01
        b_off = jax.random.normal(k3, (2 * K,), dtype=jnp.float32) * 0.1
        w_conv = jax.random.normal(k4, (CHO, CHI, 3, 3), dtype=jnp.float32) * (2.0 / (CHI * K)) ** 0.5
        gamma = jnp.ones((CHO,), dtype=jnp.float32)
        beta = jnp.zeros((CHO,), dtype=jnp.float32)
        return {'x': x, 'w_off': w_off, 'b_off': b_off, 'w_conv': w_conv, 'gamma': gamma, 'beta': beta}
    _L0_conv_all = _L0_conv_setup()
    _L0_conv_in = {k: v for k, v in _L0_conv_all.items() if k in ('w_off', 'b_off', 'w_conv', 'gamma', 'beta', )}
    del _L0_conv_all

    def _L1_attn_setup():
        import jax, jax.numpy as jnp
        import numpy as np
        INPUT_DIM = 256
        OUTPUT_DIM = 256
        HEAD_DIM = 32
        N_HEADS = INPUT_DIM // HEAD_DIM
        WINDOW = 64
        BLOCK_TYPE = 'SW'

        def _generate_mask(w, p, padding_size, shift, block_type):
            mask = np.zeros((w, p, p), dtype=bool)
            if block_type == 'W':
                s = p - padding_size
                mask[-1, :s, s:] = True
                mask[-1, s:, :s] = True
            elif padding_size + shift <= p:
                s = p - padding_size - shift
                mask[-1, :s, s:] = True
                mask[-1, s:s + padding_size, :s] = True
                mask[-1, s:s + padding_size, s + padding_size:] = True
                mask[-1, s + padding_size:, :s + padding_size] = True
            else:
                t = p - shift
                s = p - (padding_size - t)
                mask[-1, :t, t:] = True
                mask[-1, t:, :t] = True
                mask[-2, :s, s:] = True
                mask[-2, s:, :s] = True
            return mask
        key = jax.random.key(seed)
        ks = jax.random.split(key, 6)
        x = jax.random.normal(ks[0], (8, 16384, INPUT_DIM), dtype=jnp.float32)
        w_qkv = jax.random.normal(ks[1], (3 * INPUT_DIM, INPUT_DIM), dtype=jnp.float32) * 0.02
        b_qkv = jnp.zeros((3 * INPUT_DIM,), dtype=jnp.float32)
        rel_pos = jax.random.normal(ks[2], (N_HEADS, 2 * WINDOW - 1), dtype=jnp.float32) * 0.02
        w_out = jax.random.normal(ks[3], (OUTPUT_DIM, INPUT_DIM), dtype=jnp.float32) * 0.02
        b_out = jnp.zeros((OUTPUT_DIM,), dtype=jnp.float32)
        return {'x': x, 'w_qkv': w_qkv, 'b_qkv': b_qkv, 'rel_pos': rel_pos, 'w_out': w_out, 'b_out': b_out}
    _L1_attn_all = _L1_attn_setup()
    _L1_attn_in = {k: v for k, v in _L1_attn_all.items() if k in ('w_qkv', 'b_qkv', 'rel_pos', 'w_out', 'b_out', )}
    del _L1_attn_all

    def _L1_ffn_setup():
        import jax, jax.numpy as jnp
        import numpy as np
        NUM_EXPERTS = 8
        TOP_K = 2
        B, S, D = (8, 8192, 256)

        def _moe(tokens, router_w, w1, b1, w2, b2):
            N = tokens.shape[0]
            E = router_w.shape[0]
            logits = tokens.astype(jnp.float32) @ router_w.astype(jnp.float32).T
            probs = jax.nn.softmax(logits, axis=-1)
            rw, re = jax.lax.top_k(probs, TOP_K)
            if TOP_K > 1:
                rw = rw / jnp.maximum(rw.sum(-1, keepdims=True), 1e-12)
            rw = rw.astype(tokens.dtype)
            combine = jnp.zeros((N, E), tokens.dtype).at[jnp.arange(N)[:, None], re].set(rw)
            out = tokens
            for e in range(E):
                h = jax.nn.gelu(tokens @ w1[e] + b1[e], approximate=False)
                y = h @ w2[e] + b2[e]
                out = out + combine[:, e:e + 1] * y
            return out
        key = jax.random.key(seed)
        ks = jax.random.split(key, 4)
        scale = 1.0 / np.sqrt(D).astype(np.float32)
        return {'input_embeddings': jax.random.normal(ks[0], (B, S, D), jnp.float32), 'router_w': jax.random.normal(ks[1], (NUM_EXPERTS, D), jnp.float32) * scale, 'w1': jax.random.normal(ks[2], (NUM_EXPERTS, D, D), jnp.float32) * scale, 'b1': jnp.zeros((NUM_EXPERTS, D), jnp.float32), 'w2': jax.random.normal(ks[3], (NUM_EXPERTS, D, D), jnp.float32) * scale, 'b2': jnp.zeros((NUM_EXPERTS, D), jnp.float32)}
    _L1_ffn_all = _L1_ffn_setup()
    _L1_ffn_in = {k: v for k, v in _L1_ffn_all.items() if k in ('router_w', 'w1', 'b1', 'w2', 'b2', )}
    del _L1_ffn_all

    return {
        "x": x,
        "L0_conv_w_off": _L0_conv_in["w_off"],
        "L0_conv_b_off": _L0_conv_in["b_off"],
        "L0_conv_w_conv": _L0_conv_in["w_conv"],
        "L0_conv_gamma": _L0_conv_in["gamma"],
        "L0_conv_beta": _L0_conv_in["beta"],
        "L1_attn_w_qkv": _L1_attn_in["w_qkv"],
        "L1_attn_b_qkv": _L1_attn_in["b_qkv"],
        "L1_attn_rel_pos": _L1_attn_in["rel_pos"],
        "L1_attn_w_out": _L1_attn_in["w_out"],
        "L1_attn_b_out": _L1_attn_in["b_out"],
        "L1_ffn_router_w": _L1_ffn_in["router_w"],
        "L1_ffn_w1": _L1_ffn_in["w1"],
        "L1_ffn_b1": _L1_ffn_in["b1"],
        "L1_ffn_w2": _L1_ffn_in["w2"],
        "L1_ffn_b2": _L1_ffn_in["b2"],
    }

def reference(x, L0_conv_w_off, L0_conv_b_off, L0_conv_w_conv, L0_conv_gamma, L0_conv_beta, L1_attn_w_qkv, L1_attn_b_qkv, L1_attn_rel_pos, L1_attn_w_out, L1_attn_b_out, L1_ffn_router_w, L1_ffn_w1, L1_ffn_b1, L1_ffn_w2, L1_ffn_b2):
    import jax
    import jax.numpy as jnp
    def _L0_conv_ref(x, w_off, b_off, w_conv, gamma, beta):
        import jax, jax.numpy as jnp
        import numpy as np
        BN_EPS = 1e-05
        K = 9

        def _conv3x3(x, w, b=None):
            out = jax.lax.conv_general_dilated(x, w, window_strides=(1, 1), padding=((1, 1), (1, 1)), dimension_numbers=('NCHW', 'OIHW', 'NCHW'))
            if b is not None:
                out = out + b[None, :, None, None]
            return out

        def _bilinear_gather(x, py, px):
            B, C, H, W = x.shape
            y0 = jnp.floor(py)
            x0 = jnp.floor(px)
            y1 = y0 + 1.0
            x1 = x0 + 1.0
            wy1 = py - y0
            wy0 = 1.0 - wy1
            wx1 = px - x0
            wx0 = 1.0 - wx1

            def corner(yc, xc, wgt):
                valid = ((yc >= 0) & (yc < H) & (xc >= 0) & (xc < W)).astype(x.dtype)
                yi = jnp.clip(yc, 0, H - 1).astype(jnp.int32)
                xi = jnp.clip(xc, 0, W - 1).astype(jnp.int32)
                v = jax.vmap(lambda img, a, b_: img[:, a, b_])(x, yi, xi)
                return v * (wgt * valid)[:, None]
            return corner(y0, x0, wy0 * wx0) + corner(y0, x1, wy0 * wx1) + corner(y1, x0, wy1 * wx0) + corner(y1, x1, wy1 * wx1)
        B, C, H, W = x.shape
        CHO = w_conv.shape[0]
        off = _conv3x3(x, w_off, b_off).reshape(B, K, 2, H, W)
        off_y = off[:, :, 0]
        off_x = off[:, :, 1]
        kk = jnp.arange(3, dtype=x.dtype) - 1.0
        ky = jnp.repeat(kk, 3)
        kx = jnp.tile(kk, 3)
        hh = jnp.arange(H, dtype=x.dtype)[:, None]
        ww = jnp.arange(W, dtype=x.dtype)[None, :]
        py = hh[None, None] + ky[None, :, None, None] + off_y
        px = ww[None, None] + kx[None, :, None, None] + off_x
        sampled = _bilinear_gather(x, py, px)
        wk = w_conv.reshape(CHO, C, K)
        out = jnp.einsum('bckhw,ock->bohw', sampled, wk)
        mu = out.mean(axis=(0, 2, 3))
        var = out.var(axis=(0, 2, 3))
        inv = gamma / jnp.sqrt(var + BN_EPS)
        out = out * inv[None, :, None, None] + (beta - mu * inv)[None, :, None, None]
        return jax.nn.relu(out)

    def _L1_attn_ref(x, w_qkv, b_qkv, rel_pos, w_out, b_out):
        import jax, jax.numpy as jnp
        import numpy as np
        INPUT_DIM = 256
        OUTPUT_DIM = 256
        HEAD_DIM = 32
        N_HEADS = INPUT_DIM // HEAD_DIM
        WINDOW = 64
        BLOCK_TYPE = 'SW'

        def _generate_mask(w, p, padding_size, shift, block_type):
            mask = np.zeros((w, p, p), dtype=bool)
            if block_type == 'W':
                s = p - padding_size
                mask[-1, :s, s:] = True
                mask[-1, s:, :s] = True
            elif padding_size + shift <= p:
                s = p - padding_size - shift
                mask[-1, :s, s:] = True
                mask[-1, s:s + padding_size, :s] = True
                mask[-1, s:s + padding_size, s + padding_size:] = True
                mask[-1, s + padding_size:, :s + padding_size] = True
            else:
                t = p - shift
                s = p - (padding_size - t)
                mask[-1, :t, t:] = True
                mask[-1, t:, :t] = True
                mask[-2, :s, s:] = True
                mask[-2, s:, :s] = True
            return mask
        b, n, c = x.shape
        p = WINDOW
        pad = -n % p
        if pad:
            x = jnp.pad(x, ((0, 0), (0, pad), (0, 0)))
        shift = p // 2
        if BLOCK_TYPE != 'W':
            x = jnp.roll(x, -shift, axis=1)
        w = x.shape[1] // p
        xw = x.reshape(b, w, p, c)
        qkv = xw @ w_qkv.T + b_qkv
        qkv = qkv.reshape(b, w, p, 3, N_HEADS, HEAD_DIM)
        q, k, v = (qkv[..., 0, :, :], qkv[..., 1, :, :], qkv[..., 2, :, :])
        scale = HEAD_DIM ** (-0.5)
        sim = jnp.einsum('bwphd,bwqhd->bhwpq', q, k) * scale
        idx = np.arange(p)[:, None] - np.arange(p)[None, :] + p - 1
        sim = sim + rel_pos[:, idx][None, :, None]
        mask = jnp.asarray(_generate_mask(w, p, pad, shift, BLOCK_TYPE))
        sim = jnp.where(mask[None, None], -jnp.inf, sim)
        probs = jax.nn.softmax(sim, axis=-1)
        out = jnp.einsum('bhwpq,bwqhd->bwphd', probs, v)
        out = out.reshape(b, w, p, N_HEADS * HEAD_DIM)
        out = out @ w_out.T + b_out
        out = out.reshape(b, w * p, OUTPUT_DIM)
        if BLOCK_TYPE != 'W':
            out = jnp.roll(out, shift, axis=1)
        return out[:, :n]

    def _L1_ffn_ref(input_embeddings, router_w, w1, b1, w2, b2):
        import jax, jax.numpy as jnp
        import numpy as np
        NUM_EXPERTS = 8
        TOP_K = 2
        B, S, D = (8, 8192, 256)

        def _moe(tokens, router_w, w1, b1, w2, b2):
            N = tokens.shape[0]
            E = router_w.shape[0]
            logits = tokens.astype(jnp.float32) @ router_w.astype(jnp.float32).T
            probs = jax.nn.softmax(logits, axis=-1)
            rw, re = jax.lax.top_k(probs, TOP_K)
            if TOP_K > 1:
                rw = rw / jnp.maximum(rw.sum(-1, keepdims=True), 1e-12)
            rw = rw.astype(tokens.dtype)
            combine = jnp.zeros((N, E), tokens.dtype).at[jnp.arange(N)[:, None], re].set(rw)
            out = tokens
            for e in range(E):
                h = jax.nn.gelu(tokens @ w1[e] + b1[e], approximate=False)
                y = h @ w2[e] + b2[e]
                out = out + combine[:, e:e + 1] * y
            return out
        b, s, d = input_embeddings.shape
        tokens = input_embeddings.reshape(b * s, d)
        return _moe(tokens, router_w, w1, b1, w2, b2).reshape(b, s, d)

    def _gn(v, G=32, eps=1e-5):
        B_, C_, H_, W_ = v.shape
        g = v.reshape(B_, G, C_ // G, H_, W_)
        m = jnp.mean(g, axis=(2, 3, 4), keepdims=True)
        s = jnp.var(g, axis=(2, 3, 4), keepdims=True)
        return ((g - m) / jnp.sqrt(s + eps)).reshape(v.shape)

    def _ln_c(v, eps=1e-6):
        m = jnp.mean(v, axis=1, keepdims=True)
        s = jnp.var(v, axis=1, keepdims=True)
        return (v - m) / jnp.sqrt(s + eps)

    def _ln_t(v, eps=1e-5):
        m = jnp.mean(v, axis=-1, keepdims=True)
        s = jnp.var(v, axis=-1, keepdims=True)
        return (v - m) / jnp.sqrt(s + eps)

    def _to_tokens(v):
        B_, C_, H_, W_ = v.shape
        return v.reshape(B_, C_, H_ * W_).transpose(0, 2, 1)
    def _from_tokens(t, like):
        B_, C_, H_, W_ = like.shape
        return t.transpose(0, 2, 1).reshape(B_, C_, H_, W_)

    x = x + _L0_conv_ref(_gn(x), L0_conv_w_off, L0_conv_b_off, L0_conv_w_conv, L0_conv_gamma, L0_conv_beta)
    t = _to_tokens(x)
    t = t + _L1_attn_ref(_ln_t(t), L1_attn_w_qkv, L1_attn_b_qkv, L1_attn_rel_pos, L1_attn_w_out, L1_attn_b_out)
    t = t + _L1_ffn_ref(_ln_t(t), L1_ffn_router_w, L1_ffn_w1, L1_ffn_b1, L1_ffn_w2, L1_ffn_b2)
    x = _from_tokens(t, x)
    return x


_drawn_inputs = setup_inputs


def setup_inputs(seed=0):
    import zlib

    import numpy as np

    out = dict(_drawn_inputs(seed))
    spreads = {'L0_conv_gamma': (1.0, 0.2),
     'L0_conv_beta': (0.0, 0.1),
     'L1_attn_b_qkv': (0.0, 0.1),
     'L1_attn_b_out': (0.0, 0.1),
     'L1_ffn_b1': (0.0, 0.347),
     'L1_ffn_b2': (0.0, 0.1)}
    factors = {'L1_attn_rel_pos': 64.0}
    for name, (base, spread) in spreads.items():
        noise = np.random.default_rng([zlib.crc32(name.encode()), seed]).standard_normal(out[name].shape)
        drawn = base * np.exp(spread * noise) if base else spread * noise
        out[name] = jnp.asarray(drawn.astype(out[name].dtype))
    for name, factor in factors.items():
        out[name] = (out[name] * factor).astype(out[name].dtype)
    return out
```

```python
from contextlib import ExitStack

import concourse.bass as bass
from concourse import mybir

F32 = mybir.dt.float32
I32 = mybir.dt.int32
ALU = mybir.AluOpType
ACT = mybir.ActivationFunctionType
AX_X = mybir.AxisListType.X

P = 128
B, C, H, W = 4, 256, 64, 64
HALVES = C // P
N = H * W
TAPS = 9
OFFS = 2 * TAPS
OPAD = 32
PADW = W + 2
ENTRIES = PADW * PADW
CORNERS = 4
CHUNK = 512
IMG_CHUNKS = N // CHUNK
TILES = B * IMG_CHUNKS
PXT = CHUNK // P
GN_EPS, BN_EPS, LN_EPS = 1e-5, 1e-5, 1e-5

HEADS, HD, WIN = 8, 32, 64
WINS = CHUNK // WIN
SHIFT = WIN // 2
SCALE = float(HD) ** -0.5
E = 8
HG = 4
PAIRS = HEADS // 2


def upto(value, top):
    return value if isinstance(value, int) else value.with_bounds(min_val=0, max_val=top)


class Tally:

    def __init__(self, per):
        self.per, self.n = per, 0

    def begin(self):
        self.n = 0

    def next(self, i):
        self.n += 1
        return i * self.per + self.n

    def end(self):
        assert self.n == self.per, (self.n, self.per)


def sample_table_stage(nc, x, w_off, b_off, table, keep, const):
    ident, idx_all, wts_all = keep["ident"], keep["idx_all"], keep["wts_all"]
    GROUP_TILES = 8
    GROUPS = N // P // GROUP_TILES
    ROUNDS = 2
    STATS = N // CHUNK
    x_v = x.rearrange("b (h p) y x -> b p h (y x)", p=P)
    table_v = table.rearrange("(b y x) (s c) -> b y x s c", b=B, y=PADW, s=CORNERS)

    with ExitStack() as ctx:
        def sb(name, shape, dt=F32):
            return ctx.enter_context(nc.sbuf_tensor(name, shape, dt))

        def ps(name, shape):
            return ctx.enter_context(nc.psum_tensor(name, shape, F32))

        def sem(name):
            return ctx.enter_context(nc.semaphore(name))

        raw = sb("raw", [P, HALVES, N])
        padded = sb("padded", [P, HALVES, PADW, PADW])
        tok = sb("tok", [P, 2, GROUP_TILES, C])
        zero = sb("zero", [P, CORNERS * C])
        group = sb("group", [P, P])
        base = sb("base", [P, ROUNDS, PXT, 4, OFFS])
        woff = sb("woff", [P, HALVES, TAPS, OPAD])
        boff = sb("boff", [P, 1])
        stats = sb("stats", [P, HALVES, STATS, 6])
        mv = sb("mv", [P, HALVES, 2])
        gmean = sb("gmean", [P, HALVES])
        dev = sb("dev", [P, HALVES])
        spread = sb("spread", [P, HALVES])
        gvar = sb("gvar", [P, HALVES])
        grs = sb("grs", [P, HALVES])
        power = sb("power", [P, HALVES])
        off = sb("off", [P, ROUNDS, CHUNK])
        image_base = sb("image_base", [P, 1])
        pos = sb("pos", [P, PXT, 4, OFFS])
        whole_i = sb("whole_i", [P, PXT, 4, OFFS], I32)
        whole = sb("whole", [P, PXT, 4, OFFS])
        above = sb("above", [P, PXT, 4, OFFS])
        floor = sb("floor", [P, PXT, 4, OFFS])
        frac = sb("frac", [P, 2, PXT, 4, OFFS])
        entry = sb("entry", [P, PXT, 4, TAPS])

        ps_group = ps("ps_group", [P, 2, CHUNK])
        ps_tok = ps("ps_tok", [P, 2, CHUNK])
        ps_off = ps("ps_off", [P, 2, CHUNK])
        ps_pos = ps("ps_pos", [P, 2, CHUNK])

        const_in = sem("const_in")
        boff_zero = sem("boff_zero")
        boff_in = sem("boff_in")
        set_up = sem("set_up")
        base_set = sem("base_set")
        dve_gate, pool_gate, sp_gate = sem("dve_gate"), sem("pool_gate"), sem("sp_gate")
        border_out = sem("border_out")
        raw_in = [sem(f"raw_in{h}") for h in range(HALVES)]
        stat_order = sem("stat_order")
        means_ready = sem("means_ready")
        grouped = sem("grouped")
        var_ready = sem("var_ready")
        rs_ready = sem("rs_ready")
        normed = sem("normed")
        padded_ready = sem("padded_ready")
        turned = sem("turned")
        tok_ready = sem("tok_ready")
        table_out = [sem(f"table_out{i}") for i in range(2)]
        off_ready = sem("off_ready")
        off_kept = sem("off_kept")
        off_turned = sem("off_turned")
        pos_order = sem("pos_order")
        pos_taken = sem("pos_taken")
        block = ctx.enter_context(nc.Block())
        STAT_K, POS_K = 5, 20

        @block.sync
        def _(sp):
            sp.dma_start(ident[:, :], const["ident_c"]).then_inc(const_in, 16)
            sp.dma_start(group[:, :], const["group_c"]).then_inc(const_in, 16)
            sp.dma_start(base[:, :, :, :, :].rearrange("p a b c d -> p (a b c d)"),
                         const["base_c"]).then_inc(const_in, 16)
            for h in range(HALVES):
                sp.dma_start(woff[:, h, :, 0:OFFS], w_off[h * P:(h + 1) * P, :, :]).then_inc(const_in, 16)
                sp.dma_start(raw[:, h, :], x_v[0, :, h, :]).then_inc(raw_in[h], 16)
            sp.wait_ge(boff_zero, 1)
            for j in range(4):
                sp.dma_start(boff[OPAD * j:OPAD * j + OFFS, :],
                             b_off.rearrange("(o a) -> o a", a=1)).then_inc(boff_in, 16)
            sp.wait_ge(set_up, 2)
            rows = ((PADW - 1, 0, 4), (0, 0, 2), (PADW - 2, 2, 4))
            tv = table_v.rearrange("b y x s c -> b y x (s c)")
            for y, s0, s1 in rows:
                for b in range(B):
                    sp.dma_start(tv[b, y, :, s0 * C:s1 * C],
                                 zero[0:PADW, 0:(s1 - s0) * C]).then_inc(border_out, 16)
            for dy in range(2):
                y0 = 1 - dy
                for xx, s0, s1 in ((PADW - 1, 2 * dy, 2 * dy + 2), (0, 2 * dy, 2 * dy + 1),
                                   (PADW - 2, 2 * dy + 1, 2 * dy + 2)):
                    for b in range(B):
                        sp.dma_start(tv[b, y0:y0 + H, xx, s0 * C:s1 * C],
                                     zero[0:H, 0:(s1 - s0) * C]).then_inc(border_out, 16)
            with sp.Fori(0, B) as b:
                image = sp.snap(upto(b, B - 1))
                following = sp.snap(upto((b + 1) & (B - 1), B - 1))
                for g in range(GROUPS):
                    sp.wait_ge(tok_ready, b * (GROUPS * 4) + 4 * (g + 1))
                    sp.sem_inc(sp_gate, 1)
                    for r in range(2):
                        for s in range(CORNERS):
                            dy, dx = s // 2, s % 2
                            y0 = 2 * GROUP_TILES * g + r - dy + 1
                            sp.dma_start(
                                table_v[image, y0:y0 + 2 * GROUP_TILES - 1:2, 1 - dx:1 - dx + W, s, :]
                                .rearrange("y x c -> x y c"),
                                tok[W * r:W * r + W, g % 2, :, :]).then_inc(table_out[g % 2], 16)
                for h in range(HALVES):
                    sp.wait_ge(turned, b * 16 + 16)
                    sp.wait_ge(padded_ready, b * HALVES + HALVES)
                    sp.sem_inc(sp_gate, 1)
                    sp.dma_start(raw[:, h, :], x_v[following, :, h, :]).then_inc(raw_in[h], 16)
            for i in range(2):
                sp.wait_ge(table_out[i], 16 * 8 * 2 * B)
            sp.wait_ge(border_out, 16 * 9 * B)
            for h in range(HALVES):
                sp.wait_ge(raw_in[h], 16 * (B + 1))
            sp.wait_ge(boff_in, 64)

        @block.gpsimd
        def _(pool):
            pool.memset(boff[:, :], 0.0).then_inc(boff_zero, 1)
            pool.memset(power[:, :], -0.5).then_inc(set_up, 1)
            pool.memset(zero[:, :], 0.0).then_inc(set_up, 1)
            pool.memset(woff[:, :, :, OFFS:OPAD], 0.0).then_inc(set_up, 1)
            pool.memset(padded[:, :, :, :], 0.0).then_inc(set_up, 1)
            pool.wait_ge(set_up, 4)
            with pool.Fori(0, B) as b:
                pool.wait_ge(var_ready, b + 1)
                pool.tensor_tensor(grs[:, :], gvar[:, :], power[:, :], ALU.pow).then_inc(rs_ready, 1)
                pool.wait_ge(off_ready, b * 2)
                for h in range(HALVES):
                    pool.wait_ge(normed, b * 2 + h + 1)
                    pool.sem_inc(pool_gate, 1)
                    pool.tensor_copy(padded[:, h, 1:H + 1, 1:W + 1],
                                     raw[:, h, :].rearrange("p (y x) -> p y x", x=W)).then_inc(padded_ready, 1)

        @block.vector
        def _(dve):
            st, po = Tally(STAT_K), Tally(POS_K)
            dve.memset(image_base[:, :], float(PADW + 1 - ENTRIES)).then_inc(base_set, 1)
            dve.wait_ge(base_set, 1)
            dve.wait_ge(const_in, 80)
            with dve.Fori(0, B) as b:
                st.begin()
                for h in range(HALVES):
                    dve.wait_ge(raw_in[h], (b + 1) * 16)
                    for c in range(STATS):
                        last = dve.bn_stats(stats[:, h, c, :], raw[:, h, c * CHUNK:(c + 1) * CHUNK])
                last.then_inc(stat_order, 1)
                dve.wait_ge(stat_order, st.next(b))
                dve.sem_inc(dve_gate, 1)
                for h in range(HALVES):
                    last = dve.bn_aggr(mv[:, h, :], stats[:, h, :, :].rearrange("p a b -> p (a b)"))
                last.then_inc(means_ready, 1)
                dve.wait_ge(grouped, b * 2 + 1)
                dve.tensor_copy(gmean[:, :], ps_group[:, 0, 0:HALVES]).then_inc(stat_order, 1)
                dve.wait_ge(means_ready, b * 2 + 1)
                dve.wait_ge(stat_order, st.next(b))
                dve.tensor_tensor(dev[:, :], mv[:, :, 0], gmean[:, :], ALU.subtract).then_inc(stat_order, 1)
                dve.wait_ge(stat_order, st.next(b))
                dve.tensor_tensor(dev[:, :], dev[:, :], dev[:, :], ALU.mult).then_inc(stat_order, 1)
                dve.wait_ge(stat_order, st.next(b))
                dve.tensor_tensor(spread[:, :], dev[:, :], mv[:, :, 1], ALU.add).then_inc(means_ready, 1)
                dve.wait_ge(grouped, b * 2 + 2)
                dve.tensor_scalar(gvar[:, :], ps_group[:, 1, 0:HALVES], GN_EPS, None, ALU.add).then_inc(var_ready, 1)
                dve.wait_ge(rs_ready, b + 1)
                for h in range(HALVES):
                    dve.tensor_scalar(raw[:, h, :], raw[:, h, :], gmean[:, h:h + 1], grs[:, h:h + 1],
                                      ALU.subtract, ALU.mult).then_inc(normed, 1)
                dve.tensor_scalar(image_base[:, :], image_base[:, :], float(ENTRIES), None,
                                  ALU.add).then_inc(stat_order, 1)
                dve.wait_ge(stat_order, st.next(b))
                st.end()
                po.begin()
                image = upto(b, B - 1)
                for r in range(ROUNDS):
                    here = ps_pos[:, r, :].rearrange("p (q j o) -> p q j o", q=PXT, j=4)[:, :, :, 0:OFFS]
                    dve.wait_ge(off_turned, b * 2 + r + 1)

                    def chained(ins):
                        ins.then_inc(pos_order, 1)
                        dve.wait_ge(pos_order, po.next(b))

                    dve.tensor_tensor(pos[:, :, :, :], here, base[:, r, :, :, :], ALU.add).then_inc(pos_taken, 1)
                    dve.wait_ge(pos_taken, b * 2 + r + 1)
                    chained(dve.tensor_scalar(pos[:, :, :, :], pos[:, :, :, :], -1.0, float(H),
                                              ALU.max, ALU.min))
                    chained(dve.tensor_copy(whole_i[:, :, :, :], pos[:, :, :, :]))
                    chained(dve.tensor_copy(whole[:, :, :, :], whole_i[:, :, :, :]))
                    chained(dve.tensor_tensor(above[:, :, :, :], whole[:, :, :, :], pos[:, :, :, :], ALU.is_gt))
                    chained(dve.tensor_tensor(floor[:, :, :, :], whole[:, :, :, :], above[:, :, :, :],
                                              ALU.subtract))
                    chained(dve.tensor_tensor(frac[:, 1, :, :, :], pos[:, :, :, :], floor[:, :, :, :],
                                              ALU.subtract))
                    chained(dve.tensor_scalar(frac[:, 0, :, :, :], frac[:, 1, :, :, :], -1.0, 1.0,
                                              ALU.mult, ALU.add))
                    f = floor[:, :, :, :].rearrange("p q j (t a) -> p q j t a", a=2)
                    for j in range(4):
                        last = dve.scalar_tensor_tensor(entry[:, :, j, :], f[:, :, j, :, 0], float(PADW),
                                                        f[:, :, j, :, 1], ALU.mult, ALU.add)
                    chained(last)
                    chained(dve.tensor_scalar(
                        idx_all[:, image, r, :, :, :].rearrange("p j q t -> p q j t"),
                        entry[:, :, :, :], image_base[:, 0:1], None, ALU.add))
                    fr = frac[:, :, :, :, :].rearrange("p n q j (t a) -> p n q j t a", a=2)
                    for s in range(CORNERS):
                        dy, dx = s // 2, s % 2
                        for j in range(4):
                            last = dve.tensor_tensor(wts_all[:, image, r, j, :, :, s],
                                                     fr[:, dy, :, j, :, 0], fr[:, dx, :, j, :, 1], ALU.mult)
                    chained(last)
                po.end()

        @block.scalar
        def _(act):
            act.wait_ge(boff_in, 64)
            with act.Fori(0, B) as b:
                for g in range(GROUPS):
                    act.wait_ge(table_out[g % 2], (b * 2 + g // 2) * 128)
                    for k in range(4):
                        n = 4 * g + k
                        act.wait_ge(turned, b * 16 + n + 1)
                        act.activation(tok[:, g % 2, 2 * k:2 * k + 2, :].rearrange("p t c -> p (t c)"),
                                       ps_tok[:, n % 2, :], ACT.Copy).then_inc(tok_ready, 1)
                for r in range(ROUNDS):
                    act.wait_ge(off_ready, b * 2 + r + 1)
                    act.activation(off[:, r, :], ps_off[:, r, :], ACT.Identity,
                                   bias=boff[:, 0:1]).then_inc(off_kept, 1)

        @block.tensor
        def _(pe):
            pe.wait_ge(const_in, 80)
            pe.wait_ge(set_up, 4)
            with pe.Fori(0, B) as b:
                for k, src in enumerate((mv[:, :, 0], spread[:, :])):
                    pe.wait_ge(means_ready, b * 2 + k + 1)
                    pe.matmul(ps_group[:, k, 0:HALVES], group[:, :], src, start=True, stop=True).then_inc(grouped, 1)
                pe.wait_ge(normed, b * 2 + 2)
                for n in range(N // P // 2):
                    if n >= 2:
                        pe.wait_ge(tok_ready, b * 16 + n - 1)
                    else:
                        pe.wait_ge(tok_ready, b * 16)
                    for t in range(2):
                        px = P * (2 * n + t)
                        for h in range(HALVES):
                            at = (t * HALVES + h) * P
                            last = pe.matmul(ps_tok[:, n % 2, at:at + P], raw[:, h, px:px + P],
                                             ident[:, :], is_transpose=True, start=True, stop=True)
                    last.then_inc(turned, 1)
                for r in range(ROUNDS):
                    pe.wait_ge(off_kept, b * 2)
                    pe.wait_ge(padded_ready, b * 2 + 2)
                    for h in range(HALVES):
                        for t in range(TAPS):
                            ky, kx = t // 3, t % 3
                            for j in range(4):
                                y = 8 * (4 * r + j) + ky
                                last = pe.matmul(ps_off[OPAD * j:OPAD * (j + 1), r, :], woff[:, h, t, :],
                                                 padded[:, h, y:y + 8, kx:kx + W],
                                                 start=(h == 0 and t == 0),
                                                 stop=(h == HALVES - 1 and t == TAPS - 1))
                    last.then_inc(off_ready, 1)
                for r in range(ROUNDS):
                    pe.wait_ge(off_kept, b * 2 + r + 1)
                    pe.wait_ge(pos_taken, b * 2)
                    for q in range(PXT):
                        last = pe.matmul(ps_pos[:, r, q * P:(q + 1) * P], off[:, r, q * P:(q + 1) * P],
                                         ident[:, :], is_transpose=True, start=True, stop=True)
                    last.then_inc(off_turned, 1)


def conv_stage(nc, w_conv, gamma, beta, table, conv, keep):
    ident, idx_all, wts_all = keep["ident"], keep["idx_all"], keep["wts_all"]
    bn_scale, bn_shift = keep["bn_scale"], keep["bn_shift"]
    ROW = CORNERS * C
    GATHERS = PXT * TAPS
    NPAIR = GATHERS // 2
    RING = 12
    MIX = 3
    KC = TAPS * HALVES
    idx_v = idx_all[:, :, :, :, :, :].rearrange("p b r j q t -> p (b r j) (q t)")
    wts_v = wts_all[:, :, :, :, :, :, :].rearrange("p b r j q t s -> p (b r j) (q t s)")
    conv_v = conv.rearrange("(m p) n -> p m n", p=P)

    with ExitStack() as ctx:
        def sb(name, shape, dt=F32):
            return ctx.enter_context(nc.sbuf_tensor(name, shape, dt))

        def ps(name, shape):
            return ctx.enter_context(nc.psum_tensor(name, shape, F32))

        def sem(name):
            return ctx.enter_context(nc.semaphore(name))

        weights = sb("weights", [P, TAPS, HALVES, C])
        rows = sb("rows", [P, RING, ROW])
        mixed_sb = sb("mixed_sb", [P, 2 * MIX, C])
        sampled = sb("sampled", [P, 2, KC, CHUNK])
        conv_sb = sb("conv_sb", [P, 2, HALVES, CHUNK])
        idx = sb("idx", [P, 2, GATHERS], I32)
        wts = sb("wts", [P, 2, GATHERS * CORNERS])
        stats = sb("bn_stats", [P, HALVES, TILES, 6])
        mv = sb("bn_mv", [P, HALVES, 2])
        aff = sb("aff", [P, 2, HALVES])
        power = sb("bn_power", [P, HALVES])
        rs = sb("bn_rs", [P, HALVES])
        ps_turn = ps("ps_turn", [P, MIX, CHUNK])
        ps_conv = ps("ps_conv", [P, 2, HALVES, CHUNK])

        weights_in = sem("weights_in")
        sp_gate = sem("conv_sp_gate")
        pool_gate = sem("conv_pool_gate")
        idx_ready = sem("idx_ready")
        rows_in = [sem(f"rows_in{i}") for i in range(RING)]
        scaled = sem("scaled")
        mix_order = sem("mix_order")
        mixed = sem("mixed")
        turned = sem("pair_turned")
        filed = sem("filed")
        conv_ready = sem("conv_ready")
        conv_kept = sem("conv_kept")
        counted = sem("counted")
        conv_out = [sem(f"conv_out{i}") for i in range(2)]
        bn_step = sem("bn_step")
        pow_ready = sem("pow_ready")
        block = ctx.enter_context(nc.Block())

        def slot_of(g):
            pair, side = g // 2, g % 2
            return 2 * (pair // TAPS) + side, pair % TAPS

        def tiles(eng, step):
            step(0, 0, 0)
            step(1, 1, 0)
            with eng.Fori(1, TILES // 2) as k:
                step(k * 2, 0, k)
                step(k * 2 + 1, 1, k)

        @block.sync
        def _(sp):
            for t in range(TAPS):
                sp.dma_start(weights[:, t, :, :], w_conv[:, t, :].rearrange("(h p) o -> p h o", p=P))\
                  .then_inc(weights_in, 16)
            sp.dma_start(aff[:, 0, :], gamma.rearrange("(m p) -> p m", p=P),
                         allow_slow_non_contiguous=True).then_inc(weights_in, 16)
            sp.dma_start(aff[:, 1, :], beta.rearrange("(m p) -> p m", p=P),
                         allow_slow_non_contiguous=True).then_inc(weights_in, 16)
            with sp.Fori(0, TILES // 2) as k:
                for par in range(2):
                    at = sp.snap(k * (2 * CHUNK) + par * CHUNK)
                    sp.wait_ge(conv_kept, k * 2 + par + 1)
                    sp.sem_inc(sp_gate, 1)
                    sp.dma_start(conv_v[:, :, bass.ds(at, CHUNK)], conv_sb[:, par, :, :])\
                      .then_inc(conv_out[par], 16)
            for par in range(2):
                sp.wait_ge(conv_out[par], 16 * (TILES // 2))

        @block.gpsimd
        def _(pool):
            pool.memset(power[:, :], -0.5).then_inc(bn_step, 1)

            def step(s, par, k):
                pool.wait_ge(idx_ready, s + 1)
                for g in range(GATHERS):
                    if not isinstance(s, int) or s * GATHERS + g >= RING:
                        pool.wait_ge(mixed, s * GATHERS + g - RING + 1)
                        pool.sem_inc(pool_gate, 1)
                    q, t = slot_of(g)
                    pool.indirect_dma_start(rows[:, g % RING, :], None, table,
                                            bass.IndirectOffsetOnAxis(idx[:, par, q * TAPS + t:q * TAPS + t + 1], 0))\
                        .then_inc(rows_in[g % RING], 16)

            tiles(pool, step)
            pool.wait_ge(bn_step, 2)
            pool.tensor_tensor(rs[:, :], mv[:, :, 1], power[:, :], ALU.pow).then_inc(pow_ready, 1)

        @block.scalar
        def _(act):
            def conv_copy(par, n):
                act.wait_ge(conv_ready, n + 1)
                if not isinstance(n, int) or n >= 2:
                    act.wait_ge(conv_out[par], (n // 2) * 16 if isinstance(n, int) else upto(n >> 1, TILES) * 16)
                act.activation(conv_sb[:, par, :, :].rearrange("p m n -> p (m n)"),
                               ps_conv[:, par, :, :].rearrange("p m n -> p (m n)"), ACT.Copy).then_inc(conv_kept, 1)

            def step(s, par, k):
                act.wait_ge(idx_ready, s + 1)

                def file(n):
                    act.wait_ge(turned, s * NPAIR + n + 1)
                    half, t = n // TAPS, n % TAPS
                    if n == 0 and (not isinstance(s, int) or s >= 2):
                        act.wait_ge(conv_ready, s - 1)
                    act.activation(sampled[:, par, 2 * t:2 * t + 2, half * 256:half * 256 + 256],
                                   ps_turn[:, n % MIX, :].rearrange("p (h n) -> p h n", h=HALVES),
                                   ACT.Copy).then_inc(filed, 1)

                for n in range(NPAIR):
                    for g in (2 * n, 2 * n + 1):
                        q, t = slot_of(g)
                        act.wait_ge(rows_in[g % RING], (s * (GATHERS // RING) + g // RING + 1) * 16)
                        if not isinstance(s, int) or s * NPAIR + n >= MIX:
                            act.wait_ge(turned, s * NPAIR + n - MIX + 1)
                        at = (q * TAPS + t) * CORNERS
                        act.activation(mixed_sb[:, g % (2 * MIX), :], rows[:, g % RING, 0:C], ACT.Copy,
                                       scale=wts[:, par, at:at + 1]).then_inc(scaled, 1)
                    if n >= 2:
                        file(n - 2)
                    if n == 4 and (not isinstance(s, int) or s >= 2):
                        conv_copy(par, s - 2)
                file(NPAIR - 2)
                file(NPAIR - 1)

            tiles(act, step)
            conv_copy(0, TILES - 2)
            conv_copy(1, TILES - 1)

        @block.vector
        def _(dve):
            def load_indices(s, par):
                dve.tensor_copy(idx[:, par, :], idx_v[:, s, :])
                dve.tensor_copy(wts[:, par, :], wts_v[:, s, :]).then_inc(idx_ready, 1)

            def count(s, par, n):
                dve.wait_ge(conv_kept, s + 1)
                for m in range(HALVES):
                    last = dve.bn_stats(stats[:, m, n, :], conv_sb[:, par, m, :])
                last.then_inc(counted, 1)

            load_indices(0, 0)

            def step(s, par, k):
                for n in range(NPAIR):
                    for corner in range(1, CORNERS):
                        for side in range(2):
                            g = 2 * n + side
                            q, t = slot_of(g)
                            done = s * (4 * NPAIR) + 4 * n + 2 * (corner - 2) + side + 1
                            if corner == 1:
                                dve.wait_ge(rows_in[g % RING], (s * (GATHERS // RING) + g // RING + 1) * 16)
                                dve.wait_ge(scaled, s * GATHERS + g + 1)
                            else:
                                dve.wait_ge(mix_order, done)
                            at = (q * TAPS + t) * CORNERS + corner
                            ins = dve.scalar_tensor_tensor(
                                mixed_sb[:, g % (2 * MIX), :], rows[:, g % RING, corner * C:(corner + 1) * C],
                                wts[:, par, at:at + 1], mixed_sb[:, g % (2 * MIX), :], ALU.mult, ALU.add)
                            if corner < CORNERS - 1:
                                ins.then_inc(mix_order, 1)
                            else:
                                ins.then_inc(mixed, 1)
                    if n == 2:
                        load_indices(upto((s + 1) & (TILES - 1), TILES - 1) if not isinstance(s, int) else s + 1,
                                     1 - par)
                    if n == 6 and (not isinstance(s, int) or s >= 2):
                        count(s - 2, par, s - 2 if isinstance(s, int) else upto(s - 2, TILES - 1))

            tiles(dve, step)
            count(TILES - 2, 0, TILES - 2)
            count(TILES - 1, 1, TILES - 1)
            dve.wait_ge(counted, TILES)
            for m in range(HALVES):
                last = dve.bn_aggr(mv[:, m, :], stats[:, m, :, :].rearrange("p a b -> p (a b)"))
            last.then_inc(counted, 1)
            dve.wait_ge(counted, TILES + 1)
            dve.tensor_scalar(mv[:, :, 1], mv[:, :, 1], BN_EPS, None, ALU.add).then_inc(bn_step, 1)
            dve.wait_ge(weights_in, 16 * (TAPS + 2))
            dve.wait_ge(pow_ready, 1)
            dve.tensor_tensor(bn_scale[:, :], aff[:, 0, :], rs[:, :], ALU.mult).then_inc(bn_step, 1)
            dve.wait_ge(bn_step, 3)
            dve.tensor_tensor(mv[:, :, 0], mv[:, :, 0], bn_scale[:, :], ALU.mult).then_inc(bn_step, 1)
            dve.wait_ge(bn_step, 4)
            dve.tensor_tensor(bn_shift[:, :], aff[:, 1, :], mv[:, :, 0], ALU.subtract).then_inc(bn_step, 1)

        @block.tensor
        def _(pe):
            pe.wait_ge(weights_in, 16 * (TAPS + 2))

            def product(s, par, kc):
                t, h = kc // HALVES, kc % HALVES
                pe.wait_ge(filed, s * NPAIR + TAPS + t + 1)
                if kc == 0 and (not isinstance(s, int) or s >= 2):
                    pe.wait_ge(conv_kept, s - 1)
                for m in range(HALVES):
                    last = pe.matmul(ps_conv[:, par, m, :], weights[:, t, h, m * P:(m + 1) * P],
                                     sampled[:, par, kc, :], start=(kc == 0), stop=(kc == KC - 1))
                if kc == KC - 1:
                    last.then_inc(conv_ready, 1)

            def step(s, par, k):
                for n in range(NPAIR):
                    pe.wait_ge(mixed, s * GATHERS + 2 * n + 2)
                    if not isinstance(s, int) or s * NPAIR + n >= MIX:
                        pe.wait_ge(filed, s * NPAIR + n - MIX + 1)
                    for h in range(HALVES):
                        for side in range(2):
                            g = 2 * n + side
                            at = h * 256 + side * P
                            last = pe.matmul(ps_turn[:, n % MIX, at:at + P],
                                             mixed_sb[:, g % (2 * MIX), h * P:(h + 1) * P],
                                             ident[:, :], is_transpose=True, start=True, stop=True)
                    last.then_inc(turned, 1)
                    if not isinstance(s, int) or s >= 1:
                        product(s - 1, 1 - par, n)

            tiles(pe, step)
            for kc in range(KC):
                product(TILES - 1, 1, kc)


def token_stage(nc, x, conv, d, out, keep):
    ident, bn_scale, bn_shift = keep["ident"], keep["bn_scale"], keep["bn_shift"]
    SUBS = CHUNK // P
    x_v = x.rearrange("b (h p) y x -> b p h (y x)", p=P)
    conv_v = conv.rearrange("(h p) (b n) -> b p h n", p=P, b=B)
    out_v = out.rearrange("b (h p) y x -> b p h (y x)", p=P)
    BODY, REST = CHUNK - SHIFT, SHIFT

    with ExitStack() as ctx:
        def sb(name, shape, dt=F32):
            return ctx.enter_context(nc.sbuf_tensor(name, shape, dt))

        def ps(name, shape):
            return ctx.enter_context(nc.psum_tensor(name, shape, F32))

        def sem(name):
            return ctx.enter_context(nc.semaphore(name))

        wqk = sb("wqk", [P, HALVES, 2 * C])
        wv = sb("wv", [P, HALVES, 2, P])
        wo = sb("wo", [P, HALVES, C])
        wr = sb("wr", [P, HALVES, E])
        w1 = sb("w1", [P, HALVES, E, C])
        w2 = sb("w2", [P, HALVES, E, C])
        b1 = sb("b1", [P, E, HALVES])
        b2 = sb("b2", [E, C])
        bqk = sb("bqk", [P, 4])
        bv = sb("bv", [P, P])
        bo = sb("bo", [P, C])
        bias = sb("bias", [P, 2, HEADS * WIN])
        rel = sb("rel", [WIN, HEADS * WIN])
        flip = sb("flip", [WIN, P])
        lower = sb("lower", [P, E * E])
        power = sb("c_power", [P, 4])
        euler = sb("euler", [P, SUBS * E])
        xl = sb("xl", [P, 2, HALVES, CHUNK])
        yl = sb("yl", [P, 2, HALVES, CHUNK])
        res = sb("res", [P, SUBS, C])
        nrm = sb("nrm", [P, SUBS, C])
        nrm_t = sb("nrm_t", [P, HALVES, CHUNK])
        qt = sb("qt", [P, HALVES, CHUNK])
        kdiag = sb("kdiag", [P, HALVES, HG, CHUNK])
        vdiag = sb("vdiag", [P, WINS, PAIRS, 2 * HD])
        prob = sb("prob", [P, SUBS, HEADS * WIN])
        prob_t = sb("prob_t", [P, SUBS, HEADS * WIN])
        att_t = sb("att_t", [P, HALVES, CHUNK])
        tok_t = sb("tok_t", [P, 2, HALVES, CHUNK])
        acc = sb("acc", [P, 2, SUBS, C])
        hid = sb("hid", [P, 2, HALVES, CHUNK])
        final = sb("final", [P, HALVES, CHUNK])
        stats = sb("ln_stats", [P, SUBS, 6])
        mv = sb("ln_mv", [P, SUBS, 2])
        var = sb("ln_var", [P, SUBS])
        rs = sb("ln_rs", [P, SUBS])
        top = sb("top", [P, SUBS * HEADS])
        total = sb("total", [P, SUBS * HEADS])
        inverse = sb("inverse", [P, SUBS * HEADS])
        rmax = sb("rmax", [P, SUBS])
        rexp = sb("rexp", [P, SUBS, E])
        rsum = sb("rsum", [P, SUBS])
        rprob = sb("rprob", [P, SUBS, E])
        more = sb("more", [P, SUBS, E, E])
        same = sb("same", [P, SUBS, E, E])
        rank = sb("rank", [P, SUBS, E])
        chosen = sb("chosen", [P, SUBS, E])
        comb = sb("comb", [P, 2, SUBS, E])
        comb_t = sb("comb_t", [E, CHUNK])

        pa = ps("pa", [P, 4, CHUNK])
        ph = ps("ph", [P, HALVES, CHUNK])
        py = ps("py", [P, 2, CHUNK])
        pa_all = pa[:, :, :].rearrange("p a n -> p (a n)")

        weights_in = sem("c_weights_in")
        experts_in = sem("experts_in")
        tables = sem("tables")
        bias_turned = sem("bias_turned")
        bias_kept = sem("bias_kept")
        loads_in = [sem(f"loads_in{i}") for i in range(2)]
        relued = sem("relued")
        summed = sem("summed")
        x_turned = sem("x_turned")
        att_order = sem("att_order")
        var_ready = sem("c_var_ready")
        rs_ready = sem("c_rs_ready")
        n1_ready = sem("n1_ready")
        bo_added = sem("bo_added")
        n1_turned = sem("n1_turned")
        n1_kept = sem("n1_kept")
        q_ready = sem("q_ready")
        k_ready = sem("k_ready")
        q_kept = sem("q_kept")
        k_kept_act = sem("k_kept_act")
        k_kept_dve = sem("k_kept_dve")
        v_ready = sem("v_ready")
        v_kept = sem("v_kept")
        scored = sem("scored")
        shifted = sem("shifted")
        exped = sem("exped")
        probs_ready = sem("probs_ready")
        p_turned = sem("p_turned")
        p_kept = sem("p_kept")
        mixed_v = sem("mixed_v")
        att_kept = sem("att_kept")
        projected = sem("projected")
        n2_ready = sem("n2_ready")
        acc_begun = sem("acc_begun")
        n2_turned = sem("n2_turned")
        n2_kept = sem("n2_kept")
        routed = sem("routed")
        route_in = sem("route_in")
        route_exp = sem("route_exp")
        comb_ready = sem("comb_ready")
        comb_turned = sem("comb_turned")
        comb_kept = sem("comb_kept")
        hid_ready = sem("hid_ready")
        hid_kept = sem("hid_kept")
        y_ready = sem("y_ready")
        y_used = sem("y_used")
        out_turned = sem("out_turned")
        out_kept = sem("out_kept")
        stored = sem("stored")
        sp_gate, dve_gate, pool_gate = sem("c_sp_gate"), sem("c_dve_gate"), sem("c_pool_gate")
        block = ctx.enter_context(nc.Block())
        WEIGHTS = 18
        H_K, Y_K = 2 * E, 2 * (E + 1)
        ATT_K = 22

        def steps(eng, step):
            step(0, 0, True, False)
            step(1, 1, True, True)
            with eng.Fori(1, TILES // 2) as k:
                step(k * 2, 0, True, True)
                step(k * 2 + 1, 1, True, True)
            step(TILES, 0, False, True)

        def at_least(eng, semaphore, value):
            if not isinstance(value, int) or value > 0:
                eng.wait_ge(semaphore, value)

        def image_of(i):
            return i // IMG_CHUNKS if isinstance(i, int) else upto(i >> 3, B - 1)

        def columns(i):
            j = i % IMG_CHUNKS if isinstance(i, int) else i & (IMG_CHUNKS - 1)
            nxt = (i + 1) % IMG_CHUNKS if isinstance(i, int) else (i + 1) & (IMG_CHUNKS - 1)
            return j * CHUNK + SHIFT, nxt * CHUNK

        @block.sync
        def _(sp):
            def load(nxt, par, turned):
                img, (body, rest) = image_of(nxt), columns(nxt)
                if not isinstance(nxt, int):
                    img, body, rest = upto(sp.snap(img), B - 1), sp.snap(body), sp.snap(rest)
                at_least(sp, x_turned, turned)
                sp.sem_inc(sp_gate, 1)
                for src, dst in ((x_v, xl), (conv_v, yl)):
                    sp.dma_start(dst[:, par, :, 0:BODY], src[img, :, :, bass.ds(body, BODY)])\
                      .then_inc(loads_in[par], 16)
                    sp.dma_start(dst[:, par, :, BODY:CHUNK], src[img, :, :, bass.ds(rest, REST)])\
                      .then_inc(loads_in[par], 16)

            load(0, 0, 0)
            for h in range(HALVES):
                rows = slice(h * P, (h + 1) * P)
                sp.dma_start(wqk[:, h, :], d["w_qk"][rows, :]).then_inc(weights_in, 16)
                sp.dma_start(wv[:, h, :, :].rearrange("p a n -> p (a n)"), d["w_v"][rows, :]).then_inc(weights_in, 16)
                sp.dma_start(wo[:, h, :], d["w_out"][rows, :]).then_inc(weights_in, 16)
                sp.dma_start(wr[:, h, :], d["w_router"][rows, :]).then_inc(weights_in, 16)
                sp.dma_start(bv[64 * h:64 * h + 64, :], d["b_v"][h:h + 1, :].partition_broadcast(64)
                             .rearrange("p a n -> p (a n)")).then_inc(weights_in, 16)
            sp.dma_start(rel[:, :].rearrange("p (h k) -> p h k", k=WIN),
                         bass.AP(d["rel_rev"].tensor, 0, [[1, WIN], [2 * WIN - 1, HEADS], [1, WIN]]))\
              .then_inc(weights_in, 16)
            sp.dma_start(flip[:, :], d["flip_c"]).then_inc(weights_in, 16)
            sp.dma_start(bqk[:, :], d["b_qk"]).then_inc(weights_in, 16)
            sp.dma_start(b1[:, :, :].rearrange("p a b -> p (a b)"), d["b_1"]).then_inc(weights_in, 16)
            sp.dma_start(b2[:, :], d["b_2"]).then_inc(weights_in, 16)
            sp.dma_start(bo[:, :], d["b_out"].partition_broadcast(P)).then_inc(weights_in, 16)
            sp.dma_start(lower[:, :], d["lower_c"]).then_inc(weights_in, 16)
            sp.dma_start(bias[:, 1, :], d["apart_c"]).then_inc(weights_in, 16)
            load(1, 1, 0)
            for h in range(HALVES):
                rows = slice(h * P, (h + 1) * P)
                sp.dma_start(w1[:, h, :, :], d["w_1"][:, rows, :].rearrange("e p n -> p e n")).then_inc(experts_in, 16)
                sp.dma_start(w2[:, h, :, :], d["w_2"][:, rows, :].rearrange("e p n -> p e n")).then_inc(experts_in, 16)

            def step(i, par, att, moe):
                m = i - 1
                if att:
                    nxt = i + 2 if isinstance(i, int) else (i + 2) & (TILES - 1)
                    load(nxt, par, i + 1)
                if moe:
                    img, (body, rest) = image_of(m), columns(m)
                    if not isinstance(m, int):
                        img, body, rest = upto(sp.snap(img), B - 1), sp.snap(body), sp.snap(rest)
                    sp.wait_ge(out_kept, m + 1)
                    sp.sem_inc(sp_gate, 1)
                    sp.dma_start(out_v[img, :, :, bass.ds(body, BODY)], final[:, :, 0:BODY]).then_inc(stored, 16)
                    sp.dma_start(out_v[img, :, :, bass.ds(rest, REST)], final[:, :, BODY:CHUNK]).then_inc(stored, 16)

            steps(sp, step)
            sp.wait_ge(stored, 32 * TILES)
            for par in range(2):
                sp.wait_ge(loads_in[par], 64 * (TILES // 2 + 1))

        @block.gpsimd
        def _(pool):
            pool.memset(power[:, :], -0.5).then_inc(tables, 1)
            pool.memset(euler[:, :], 2.718281828459045).then_inc(tables, 1)
            pool.memset(kdiag[:, :, :, :], 0.0).then_inc(tables, 1)
            pool.memset(vdiag[:, :, :, :], 0.0).then_inc(tables, 1)
            pool.wait_ge(weights_in, 16 * WEIGHTS)
            pool.wait_ge(bias_kept, 1)
            pool.tensor_tensor(bias[:, 1, :], bias[:, 1, :], bias[:, 0, :], ALU.add).then_inc(tables, 1)
            pool.wait_ge(tables, 5)

            def add_x(i, par):
                pool.wait_ge(relued, i + 1)
                pool.tensor_tensor(xl[:, par, :, :], xl[:, par, :, :], yl[:, par, :, :], ALU.add).then_inc(summed, 1)

            add_x(0, 0)

            def step(i, par, att, moe):
                if not att:
                    return
                pool.wait_ge(var_ready, 2 * i + 1)
                pool.tensor_tensor(rs[:, :], var[:, :], power[:, :], ALU.pow).then_inc(rs_ready, 1)
                add_x(i + 1, 1 - par)
                pool.wait_ge(n1_ready, i + 1)
                for u in range(SUBS):
                    last = pool.tensor_tensor(res[:, u, :], res[:, u, :], bo[:, :], ALU.add)
                last.then_inc(bo_added, 1)
                pool.wait_ge(var_ready, 2 * i + 2)
                pool.tensor_tensor(rs[:, :], var[:, :], power[:, :], ALU.pow).then_inc(rs_ready, 1)
                pool.wait_ge(n2_ready, i + 1)
                at_least(pool, out_turned, i - 1)
                pool.tensor_tensor(acc[:, par, :, :], res[:, :, :], nrm[:, :, :], ALU.add).then_inc(acc_begun, 1)
                pool.wait_ge(route_in, i + 1)
                pool.tensor_tensor(rexp[:, :, :].rearrange("p u e -> p (u e)"), euler[:, :],
                                   rexp[:, :, :].rearrange("p u e -> p (u e)"), ALU.pow).then_inc(route_exp, 1)

            steps(pool, step)

        @block.scalar
        def _(act):
            act.wait_ge(weights_in, 16 * WEIGHTS)
            act.wait_ge(bias_turned, 1)
            act.activation(bias[:, 0, :], pa[:, 0, :], ACT.Copy).then_inc(bias_kept, 1)
            act.wait_ge(tables, 5)

            def relu(i, par):
                use = i // 2 if isinstance(i, int) else i >> 1
                act.wait_ge(loads_in[par], (use + 1) * 64)
                for h in range(HALVES):
                    last = act.activation(yl[:, par, h, :], yl[:, par, h, :], ACT.Relu,
                                          bias=bn_shift[:, h:h + 1], scale=bn_scale[:, h:h + 1])
                last.then_inc(relued, 1)

            relu(0, 0)

            def step(i, par, att, moe):
                m, mp = i - 1, 1 - par

                def gelu(e):
                    if not moe:
                        return
                    for f in range(HALVES):
                        act.wait_ge(hid_ready, m * H_K + 2 * e + f + 1)
                        at_least(act, y_ready, m * Y_K + 2 * e - (2 if e >= 2 else 4))
                        act.activation(hid[:, e % 2, f, :], ph[:, f, :], ACT.Gelu,
                                       bias=b1[:, e, f:f + 1]).then_inc(hid_kept, 1)

                gelu(0)
                if moe:
                    act.wait_ge(comb_turned, m + 1)
                    act.activation(comb_t[:, :], pa[0:E, 3, :], ACT.Copy).then_inc(comb_kept, 1)
                if att:
                    relu(i + 1, 1 - par)
                gelu(1)
                if att:
                    act.wait_ge(n1_turned, i + 1)
                    act.activation(nrm_t[:, :, :].rearrange("p h n -> p (h n)"), pa_all[:, 2 * CHUNK:4 * CHUNK],
                                   ACT.Copy).then_inc(n1_kept, 1)
                gelu(2)
                if att:
                    act.wait_ge(q_ready, i + 1)
                    for h in range(HALVES):
                        last = act.activation(qt[:, h, :], pa[:, h, :], ACT.Identity, bias=bqk[:, h:h + 1])
                    last.then_inc(q_kept, 1)
                    act.wait_ge(k_ready, i + 1)
                    for n in range(HG):
                        rows = slice(HD * n, HD * (n + 1))
                        last = act.activation(kdiag[rows, 0, n, :], pa[rows, 2, :], ACT.Identity,
                                              bias=bqk[rows, 2:3])
                    last.then_inc(k_kept_act, 1)
                gelu(3)
                gelu(4)
                if att:
                    act.wait_ge(shifted, i + 1)
                    act.activation(prob[:, :, :], prob[:, :, :], ACT.Exp).then_inc(exped, 1)
                gelu(5)
                if att:
                    for u in range(SUBS):
                        act.wait_ge(p_turned, i * SUBS + u + 1)
                        act.activation(prob_t[:, u, :], pa[:, u, :], ACT.Copy).then_inc(p_kept, 1)
                gelu(6)
                if att:
                    act.wait_ge(mixed_v, i + 1)
                    act.activation(att_t[:, :, :].rearrange("p h n -> p (h n)"), pa_all[:, 0:2 * CHUNK],
                                   ACT.Copy).then_inc(att_kept, 1)
                gelu(7)
                if att:
                    act.wait_ge(n2_turned, i + 1)
                    act.activation(tok_t[:, par, :, :].rearrange("p h n -> p (h n)"), pa_all[:, 0:2 * CHUNK],
                                   ACT.Copy).then_inc(n2_kept, 1)
                if moe:
                    act.wait_ge(out_turned, m + 1)
                    at_least(act, stored, m * 32)
                    act.activation(final[:, :, :].rearrange("p h n -> p (h n)"),
                                   py[:, :, :].rearrange("p h n -> p (h n)"), ACT.Copy).then_inc(out_kept, 1)

            steps(act, step)

        @block.vector
        def _(dve):
            dve.wait_ge(weights_in, 16 * WEIGHTS)
            dve.wait_ge(tables, 5)
            order = Tally(ATT_K)

            def step(i, par, att, moe):
                m, mp = i - 1, 1 - par

                def chained(ins):
                    ins.then_inc(att_order, 1)
                    dve.wait_ge(att_order, order.next(i))

                def layer_norm(nth, done):
                    for u in range(SUBS):
                        last = dve.bn_stats(stats[:, u, :], res[:, u, :])
                    chained(last)
                    dve.sem_inc(dve_gate, 1)
                    for u in range(SUBS):
                        last = dve.bn_aggr(mv[:, u, :], stats[:, u, :])
                    chained(last)
                    dve.tensor_scalar(var[:, :], mv[:, :, 1], LN_EPS, None, ALU.add).then_inc(var_ready, 1)
                    dve.wait_ge(rs_ready, 2 * i + nth)
                    for u in range(SUBS):
                        last = dve.tensor_scalar(nrm[:, u, :], res[:, u, :], mv[:, u, 0:1], rs[:, u:u + 1],
                                                 ALU.subtract, ALU.mult)
                    last.then_inc(done, 1)

                def weigh(e):
                    if not moe:
                        return
                    for v in range(2):
                        dve.wait_ge(y_ready, m * Y_K + 2 * e + v + 1)
                        if e == 0:
                            dve.wait_ge(acc_begun, m + 1)
                            dve.wait_ge(comb_ready, m + 1)
                        else:
                            dve.wait_ge(y_used, m * Y_K + 2 * e + v - 1)
                        for u in (2 * v, 2 * v + 1):
                            last = dve.scalar_tensor_tensor(
                                acc[:, mp, u, :], py[:, v, (u % 2) * C:(u % 2) * C + C], comb[:, mp, u, e:e + 1],
                                acc[:, mp, u, :], ALU.mult, ALU.add)
                        last.then_inc(y_used, 1)

                order.begin()
                if att:
                    dve.wait_ge(x_turned, i + 1)
                    at_least(dve, acc_begun, i)
                    chained(dve.tensor_copy(res[:, :, :].rearrange("p u c -> p (u c)"), pa_all[:, 0:2 * CHUNK]))
                    layer_norm(1, n1_ready)
                weigh(0)
                weigh(1)
                if att:
                    dve.wait_ge(k_ready, i + 1)
                    for n in range(HG):
                        rows = slice(HD * n, HD * (n + 1))
                        last = dve.tensor_scalar(kdiag[rows, 1, n, :], pa[rows, 3, :], bqk[rows, 3:4], None, ALU.add)
                    last.then_inc(k_kept_dve, 1)
                    dve.wait_ge(v_ready, i + 1)
                    for h in range(2):
                        rows = slice(64 * h, 64 * h + 64)
                        for w2_ in range(2):
                            ws = slice(4 * w2_, 4 * w2_ + 4)
                            last = dve.tensor_tensor(
                                vdiag[rows, ws, :, HD * h:HD * h + HD],
                                pa[rows, w2_, :].rearrange("p (w g d) -> p w g d", w=4, d=HD),
                                bv[rows, :].rearrange("p (g d) -> p g d", d=HD).unsqueeze(1)
                                .broadcast_to([64, 4, PAIRS, HD]), ALU.add)
                    last.then_inc(v_kept, 1)
                weigh(2)
                if att:
                    last_tile = (i + 1) // IMG_CHUNKS - i // IMG_CHUNKS if isinstance(i, int) else \
                        upto(((i & (IMG_CHUNKS - 1)) + 1) >> 3, 1)
                    for u in range(SUBS):
                        dve.wait_ge(scored, i * SUBS + u + 1)
                        table = bias[:, last_tile, :] if u == SUBS - 1 else bias[:, 0, :]
                        ins = dve.scalar_tensor_tensor(prob[:, u, :], pa[:, u, :], SCALE, table, ALU.mult, ALU.add)
                    chained(ins)
                    grid = prob[:, :, :].rearrange("p u (h k) -> p (u h) k", k=WIN)

                    def wide(a):
                        return a[:, :].unsqueeze(2).broadcast_to([P, SUBS * HEADS, WIN])

                    chained(dve.tensor_reduce(top[:, :], grid, AX_X, ALU.max))
                    dve.tensor_tensor(grid, grid, wide(top), ALU.subtract).then_inc(shifted, 1)
                weigh(3)
                if att:
                    dve.wait_ge(exped, i + 1)
                    chained(dve.tensor_reduce(total[:, :], grid, AX_X, ALU.add))
                    chained(dve.reciprocal(inverse[:, :], total[:, :]))
                    dve.tensor_tensor(grid, grid, wide(inverse), ALU.mult).then_inc(probs_ready, 1)
                weigh(4)
                weigh(5)
                weigh(6)
                if att:
                    dve.wait_ge(projected, i + 1)
                    dve.wait_ge(bo_added, i + 1)
                    chained(dve.tensor_tensor(res[:, :, :].rearrange("p u c -> p (u c)"), pa_all[:, 2 * CHUNK:4 * CHUNK],
                                              res[:, :, :].rearrange("p u c -> p (u c)"), ALU.add))
                    layer_norm(2, n2_ready)
                weigh(7)
                if moe:
                    for v in range(2):
                        dve.wait_ge(y_ready, m * Y_K + 2 * E + v + 1)
                        dve.wait_ge(y_used, m * Y_K + 2 * E + v - 1)
                        dve.tensor_tensor(acc[:, mp, 2 * v:2 * v + 2, :].rearrange("p u c -> p (u c)"), py[:, v, :],
                                          acc[:, mp, 2 * v:2 * v + 2, :].rearrange("p u c -> p (u c)"),
                                          ALU.add).then_inc(y_used, 1)
                if att:
                    dve.wait_ge(routed, i + 1)
                    logits = pa[:, 2, 0:SUBS * E].rearrange("p (u e) -> p u e", e=E)

                    def over_e(a):
                        return a[:, :].unsqueeze(2).broadcast_to([P, SUBS, E])

                    chained(dve.tensor_reduce(rmax[:, :], logits, AX_X, ALU.max))
                    dve.tensor_tensor(rexp[:, :, :], logits, over_e(rmax), ALU.subtract).then_inc(route_in, 1)
                    dve.wait_ge(route_exp, i + 1)
                    chained(dve.tensor_reduce(rsum[:, :], rexp[:, :, :], AX_X, ALU.add))
                    chained(dve.reciprocal(rsum[:, :], rsum[:, :]))
                    chained(dve.tensor_tensor(rprob[:, :, :], rexp[:, :, :], over_e(rsum), ALU.mult))
                    mine = rprob[:, :, :].unsqueeze(3).broadcast_to([P, SUBS, E, E])
                    other = rprob[:, :, :].unsqueeze(2).broadcast_to([P, SUBS, E, E])
                    before = lower[:, :].rearrange("p (e f) -> p e f", f=E).unsqueeze(1).broadcast_to([P, SUBS, E, E])
                    chained(dve.tensor_tensor(same[:, :, :, :], other, mine, ALU.is_equal))
                    dve.tensor_tensor(more[:, :, :, :], other, mine, ALU.is_gt)
                    chained(dve.tensor_tensor(same[:, :, :, :], same[:, :, :, :], before, ALU.mult))
                    chained(dve.tensor_tensor(more[:, :, :, :], more[:, :, :, :], same[:, :, :, :], ALU.add))
                    chained(dve.tensor_reduce(rank[:, :, :], more[:, :, :, :], AX_X, ALU.add))
                    chained(dve.scalar_tensor_tensor(chosen[:, :, :], rank[:, :, :], 1.5, rprob[:, :, :],
                                                     ALU.is_lt, ALU.mult))
                    chained(dve.tensor_reduce(rsum[:, :], chosen[:, :, :], AX_X, ALU.add))
                    chained(dve.tensor_scalar(rsum[:, :], rsum[:, :], 1e-12, None, ALU.max))
                    chained(dve.reciprocal(rsum[:, :], rsum[:, :]))
                    dve.tensor_tensor(comb[:, par, :, :], chosen[:, :, :], over_e(rsum), ALU.mult).then_inc(comb_ready, 1)
                    order.end()

            steps(dve, step)

        @block.tensor
        def _(pe):
            pe.wait_ge(weights_in, 16 * WEIGHTS)
            pe.matmul(pa[:, 0, :], flip[:, :], rel[:, :], start=True, stop=True).then_inc(bias_turned, 1)
            pe.wait_ge(tables, 5)
            pe.wait_ge(experts_in, 64)

            def turn(dst, src):
                return pe.matmul(dst, src, ident[:, :], is_transpose=True, start=True, stop=True)

            def step(i, par, att, moe):
                m, mp = i - 1, 1 - par

                def hidden(e):
                    if not moe:
                        return
                    if e == 0:
                        pe.wait_ge(n2_kept, m + 1)
                    for f in range(HALVES):
                        at_least(pe, hid_kept, m * H_K + 2 * e + f - 1)
                        for h in range(HALVES):
                            last = pe.matmul(ph[:, f, :], w1[:, h, e, f * P:(f + 1) * P], tok_t[:, mp, h, :],
                                             start=(h == 0), stop=(h == HALVES - 1))
                        last.then_inc(hid_ready, 1)

                def output(e):
                    if not moe:
                        return
                    if e == 0:
                        at_least(pe, out_kept, m)
                    pe.wait_ge(hid_kept, m * H_K + 2 * e + 2)
                    for v in range(2):
                        at_least(pe, y_used, m * Y_K + 2 * e + v - 1)
                        for u in (2 * v, 2 * v + 1):
                            for f in range(HALVES):
                                last = pe.matmul(py[:, v, (u % 2) * C:(u % 2) * C + C],
                                                 hid[:, e % 2, f, u * P:(u + 1) * P], w2[:, f, e, :],
                                                 start=(f == 0), stop=(f == HALVES - 1))
                        last.then_inc(y_ready, 1)

                hidden(0)
                if moe:
                    pe.wait_ge(comb_ready, m + 1)
                    for u in range(SUBS):
                        last = turn(pa[0:E, 3, u * P:(u + 1) * P], comb[:, mp, u, :])
                    last.then_inc(comb_turned, 1)
                if att:
                    pe.wait_ge(summed, i + 1)
                    at_least(pe, n2_kept, i)
                    for u in range(SUBS):
                        for h in range(HALVES):
                            at = (2 * (u % 2) + h) * P
                            last = turn(pa[:, u // 2, at:at + P], xl[:, par, h, u * P:(u + 1) * P])
                    last.then_inc(x_turned, 1)
                hidden(1)
                output(0)
                if att:
                    pe.wait_ge(n1_ready, i + 1)
                    at_least(pe, comb_kept, m + 1)
                    at_least(pe, comb_ready, m + 1)
                    for h in range(HALVES):
                        for u in range(SUBS):
                            last = turn(pa[:, 2 + h, u * P:(u + 1) * P], nrm[:, u, h * P:(h + 1) * P])
                    last.then_inc(n1_turned, 1)
                hidden(2)
                output(1)
                if att:
                    pe.wait_ge(n1_kept, i + 1)
                    for n in range(4):
                        for h in range(HALVES):
                            last = pe.matmul(pa[:, n, :], wqk[:, h, n * P:(n + 1) * P], nrm_t[:, h, :],
                                             start=(h == 0), stop=(h == HALVES - 1))
                        if n == 1:
                            last.then_inc(q_ready, 1)
                    last.then_inc(k_ready, 1)
                    pe.wait_ge(q_kept, i + 1)
                    for w in range(WINS):
                        for parity in range(2):
                            for h in range(HALVES):
                                last = pe.matmul(pa[64 * parity:64 * parity + 64, w // 4, (w % 4) * P:(w % 4 + 1) * P],
                                                 nrm_t[:, h, w * WIN:(w + 1) * WIN], wv[:, h, parity, :],
                                                 start=(h == 0), stop=(h == HALVES - 1))
                    last.then_inc(v_ready, 1)
                hidden(3)
                output(2)
                if att:
                    pe.wait_ge(k_kept_act, i + 1)
                    pe.wait_ge(k_kept_dve, i + 1)
                    pe.wait_ge(v_kept, i + 1)
                    for u in range(SUBS):
                        for side in range(2):
                            cols = slice((2 * u + side) * WIN, (2 * u + side + 1) * WIN)
                            for g in range(HALVES):
                                last = pe.matmul(pa[64 * side:64 * side + 64, u, g * 256:g * 256 + 256],
                                                 qt[:, g, cols], kdiag[:, g, :, cols], start=True, stop=True)
                        last.then_inc(scored, 1)
                hidden(4)
                output(3)
                hidden(5)
                output(4)
                if att:
                    pe.wait_ge(probs_ready, i + 1)
                    for u in range(SUBS):
                        for g in range(PAIRS):
                            last = turn(pa[:, u, g * P:(g + 1) * P], prob[:, u, g * P:(g + 1) * P])
                        last.then_inc(p_turned, 1)
                hidden(6)
                output(5)
                if att:
                    pe.wait_ge(p_kept, (i + 1) * SUBS)
                    for w in range(WINS):
                        for g in range(PAIRS):
                            at = g * P + (w % 2) * WIN
                            rows = slice(64 * (g % 2), 64 * (g % 2) + 64)
                            last = pe.matmul(pa[rows, g // 2, w * WIN:(w + 1) * WIN], vdiag[:, w, g, :],
                                             prob_t[:, w // 2, at:at + WIN], start=True, stop=True)
                    last.then_inc(mixed_v, 1)
                hidden(7)
                output(6)
                if att:
                    pe.wait_ge(att_kept, i + 1)
                    for u in range(SUBS):
                        for h in range(HALVES):
                            last = pe.matmul(pa[:, 2 + u // 2, (u % 2) * C:(u % 2) * C + C],
                                             att_t[:, h, u * P:(u + 1) * P], wo[:, h, :],
                                             start=(h == 0), stop=(h == HALVES - 1))
                    last.then_inc(projected, 1)
                output(7)
                if moe:
                    pe.wait_ge(comb_kept, m + 1)
                    for v in range(2):
                        pe.wait_ge(y_used, m * Y_K + 2 * E + v - 1)
                        for u in (2 * v, 2 * v + 1):
                            last = pe.matmul(py[:, v, (u % 2) * C:(u % 2) * C + C], comb_t[:, u * P:(u + 1) * P],
                                             b2[:, :], start=True, stop=True)
                        last.then_inc(y_ready, 1)
                if att:
                    pe.wait_ge(n2_ready, i + 1)
                    for h in range(HALVES):
                        for u in range(SUBS):
                            last = turn(pa[:, h, u * P:(u + 1) * P], nrm[:, u, h * P:(h + 1) * P])
                    last.then_inc(n2_turned, 1)
                if moe:
                    pe.wait_ge(y_used, (m + 1) * Y_K)
                    for h in range(HALVES):
                        for u in range(SUBS):
                            last = turn(py[:, h, u * P:(u + 1) * P], acc[:, mp, u, h * P:(h + 1) * P])
                    last.then_inc(out_turned, 1)
                if att:
                    pe.wait_ge(n2_kept, i + 1)
                    for u in range(SUBS):
                        for h in range(HALVES):
                            last = pe.matmul(pa[:, 2, u * E:(u + 1) * E], tok_t[:, par, h, u * P:(u + 1) * P],
                                             wr[:, h, :], start=(h == 0), stop=(h == HALVES - 1))
                    last.then_inc(routed, 1)

            steps(pe, step)


def keep_buffers(nc, ctx):
    def sb(name, shape, dt=F32):
        return ctx.enter_context(nc.sbuf_tensor(name, shape, dt))

    return {
        "ident": sb("ident", [P, P]),
        "idx_all": sb("idx_all", [P, B, 2, 4, PXT, TAPS], I32),
        "wts_all": sb("wts_all", [P, B, 2, 4, PXT, TAPS, CORNERS]),
        "bn_scale": sb("bn_scale", [P, HALVES]),
        "bn_shift": sb("bn_shift", [P, HALVES]),
    }


def constants():
    import numpy as np

    chan = np.arange(P)
    group = (chan[:, None] // (C // 32) == chan[None, :] // (C // 32)).astype(np.float32) / (C // 32)
    p, r, q, j, t = np.ogrid[0:P, 0:2, 0:PXT, 0:4, 0:TAPS]
    base = np.zeros((P, 2, PXT, 4, TAPS, 2), np.float32)
    base[..., 0] = 2 * (16 * r + 4 * j + q) + p // W + t // 3 - 1
    base[..., 1] = p % W + t % 3 - 1 + 0 * (r + q + j)
    here = np.zeros((P, HEADS, WIN), np.float32)
    first = np.arange(P)[:, None] % WIN < SHIFT
    apart = (first != (np.arange(WIN)[None, :] < SHIFT)) & (np.arange(P)[:, None] >= WIN)
    here[:] = np.where(apart, np.float32(-1e30), np.float32(0))[:, None, :]
    flip = (np.arange(WIN)[:, None] == WIN - 1 - np.arange(P)[None, :] % WIN).astype(np.float32)
    lower = (np.arange(E)[None, :] < np.arange(E)[:, None]).astype(np.float32)
    return {
        "ident_c": np.eye(P, dtype=np.float32),
        "group_c": group,
        "base_c": base.reshape(P, -1),
        "flip_c": flip,
        "apart_c": here.reshape(P, -1),
        "lower_c": np.broadcast_to(lower.reshape(1, -1), (P, E * E)).copy(),
    }


def build(nc, d, out):
    with ExitStack() as ctx:
        table = nc.dram_tensor("table", (B * ENTRIES, CORNERS * C), F32, kind="Internal").ap()
        conv = nc.dram_tensor("conv_raw", (C, B * N), F32, kind="Internal").ap()
        keep = keep_buffers(nc, ctx)
        sample_table_stage(nc, d["x"], d["w_off"], d["b_off"], table, keep, d)
        conv_stage(nc, d["w_conv"], d["gamma"], d["beta"], table, conv, keep)
        token_stage(nc, d["x"], conv, d, out, keep)


def laid_out(inputs):
    import numpy as np

    def a(name):
        return np.asarray(inputs[name])

    w_qkv, b_qkv = a("L1_attn_w_qkv"), a("L1_attn_b_qkv")
    even_odd = (PAIRS, 2, HD)
    d = {
        "x": a("x"),
        "w_off": a("L0_conv_w_off").reshape(OFFS, C, TAPS).transpose(1, 2, 0),
        "b_off": a("L0_conv_b_off"),
        "w_conv": a("L0_conv_w_conv").reshape(C, C, TAPS).transpose(1, 2, 0),
        "gamma": a("L0_conv_gamma"),
        "beta": a("L0_conv_beta"),
        "w_qk": w_qkv[:2 * C].T,
        "w_v": w_qkv[2 * C:].T.reshape(C, *even_odd).transpose(0, 2, 1, 3).reshape(C, C),
        "b_qk": b_qkv[:2 * C].reshape(4, P).T,
        "b_v": b_qkv[2 * C:].reshape(even_odd).transpose(1, 0, 2).reshape(2, P),
        "rel_rev": a("L1_attn_rel_pos")[:, ::-1],
        "w_out": a("L1_attn_w_out").T,
        "b_out": a("L1_attn_b_out"),
        "w_router": a("L1_ffn_router_w").T,
        "w_1": a("L1_ffn_w1"),
        "b_1": a("L1_ffn_b1").reshape(E, HALVES, P).transpose(2, 0, 1).reshape(P, E * HALVES),
        "w_2": a("L1_ffn_w2"),
        "b_2": a("L1_ffn_b2"),
        **constants(),
    }
    return {name: np.ascontiguousarray(v) for name, v in d.items()}


def kernel(**inputs):
    import concourse.bacc as bacc
    from concourse.bass_utils import run_bass_kernel_spmd

    nc = bacc.Bacc("TRN2", target_bir_lowering=False, num_devices=1)
    arrays = laid_out(inputs)
    d = {name: nc.dram_tensor("in_" + name, v.shape, mybir.dt.from_np(v.dtype), kind="ExternalInput").ap()
         for name, v in arrays.items()}
    out = nc.dram_tensor("out", (B, C, H, W), F32, kind="ExternalOutput").ap()
    build(nc, d, out)
    r = run_bass_kernel_spmd(nc, [{"in_" + name: v for name, v in arrays.items()}], core_ids=[0])
    return r.results[0]["out"]
```

```python
from contextlib import ExitStack

import concourse.bass as bass
from concourse import mybir

F32 = mybir.dt.float32
I32 = mybir.dt.int32
ALU = mybir.AluOpType
ACT = mybir.ActivationFunctionType
AX_X = mybir.AxisListType.X

P = 128
B, C, H, W = 4, 256, 64, 64
HALVES = C // P
N = H * W
TAPS = 9
OFFS = 2 * TAPS
OPAD = 32
PADW = W + 2
ENTRIES = PADW * PADW
CORNERS = 4
CHUNK = 512
IMG_CHUNKS = N // CHUNK
TILES = B * IMG_CHUNKS
PXT = CHUNK // P
GN_EPS, BN_EPS, LN_EPS = 1e-5, 1e-5, 1e-5

HEADS, HD, WIN = 8, 32, 64
WINS = CHUNK // WIN
SHIFT = WIN // 2
SCALE = float(HD) ** -0.5
E = 8
HG = 4
PAIRS = HEADS // 2
TOP_K = 2
STEP_TILES = -(-(TOP_K * N + E * (P - 1)) // (P * IMG_CHUNKS))
EXPERT_TILES = STEP_TILES * IMG_CHUNKS


def upto(value, top):
    return value if isinstance(value, int) else value.with_bounds(min_val=0, max_val=top)


class Tally:

    def __init__(self, per):
        self.per, self.n = per, 0

    def begin(self):
        self.n = 0

    def next(self, i):
        self.n += 1
        return i * self.per + self.n

    def end(self):
        assert self.n == self.per, (self.n, self.per)


def sample_table_stage(nc, x, w_off, b_off, table, keep, const):
    ident, idx_all, wts_all = keep["ident"], keep["idx_all"], keep["wts_all"]
    GROUP_TILES = 8
    GROUPS = N // P // GROUP_TILES
    ROUNDS = 2
    STATS = N // CHUNK
    x_v = x.rearrange("b (h p) y x -> b p h (y x)", p=P)
    table_v = table.rearrange("(b y x) (s c) -> b y x s c", b=B, y=PADW, s=CORNERS)

    with ExitStack() as ctx:
        def sb(name, shape, dt=F32):
            return ctx.enter_context(nc.sbuf_tensor(name, shape, dt))

        def ps(name, shape):
            return ctx.enter_context(nc.psum_tensor(name, shape, F32))

        def sem(name):
            return ctx.enter_context(nc.semaphore(name))

        raw = sb("raw", [P, HALVES, N])
        padded = sb("padded", [P, HALVES, PADW, PADW])
        tok = sb("tok", [P, 2, GROUP_TILES, C])
        zero = sb("zero", [P, CORNERS * C])
        group = sb("group", [P, P])
        base = sb("base", [P, ROUNDS, PXT, 4, OFFS])
        woff = sb("woff", [P, HALVES, TAPS, OPAD])
        boff = sb("boff", [P, 1])
        stats = sb("stats", [P, HALVES, STATS, 6])
        mv = sb("mv", [P, HALVES, 2])
        gmean = sb("gmean", [P, HALVES])
        dev = sb("dev", [P, HALVES])
        spread = sb("spread", [P, HALVES])
        gvar = sb("gvar", [P, HALVES])
        grs = sb("grs", [P, HALVES])
        power = sb("power", [P, HALVES])
        off = sb("off", [P, ROUNDS, CHUNK])
        image_base = sb("image_base", [P, 1])
        pos = sb("pos", [P, PXT, 4, OFFS])
        whole_i = sb("whole_i", [P, PXT, 4, OFFS], I32)
        whole = sb("whole", [P, PXT, 4, OFFS])
        above = sb("above", [P, PXT, 4, OFFS])
        floor = sb("floor", [P, PXT, 4, OFFS])
        frac = sb("frac", [P, 2, PXT, 4, OFFS])
        entry = sb("entry", [P, PXT, 4, TAPS])

        ps_group = ps("ps_group", [P, 2, CHUNK])
        ps_tok = ps("ps_tok", [P, 2, CHUNK])
        ps_off = ps("ps_off", [P, 2, CHUNK])
        ps_pos = ps("ps_pos", [P, 2, CHUNK])

        const_in = sem("const_in")
        boff_zero = sem("boff_zero")
        boff_in = sem("boff_in")
        set_up = sem("set_up")
        base_set = sem("base_set")
        dve_gate, pool_gate, sp_gate = sem("dve_gate"), sem("pool_gate"), sem("sp_gate")
        border_out = sem("border_out")
        raw_in = [sem(f"raw_in{h}") for h in range(HALVES)]
        stat_order = sem("stat_order")
        means_ready = sem("means_ready")
        grouped = sem("grouped")
        var_ready = sem("var_ready")
        rs_ready = sem("rs_ready")
        normed = sem("normed")
        padded_ready = sem("padded_ready")
        turned = sem("turned")
        tok_ready = sem("tok_ready")
        table_out = [sem(f"table_out{i}") for i in range(2)]
        off_ready = sem("off_ready")
        off_kept = sem("off_kept")
        off_turned = sem("off_turned")
        pos_order = sem("pos_order")
        pos_taken = sem("pos_taken")
        block = ctx.enter_context(nc.Block())
        STAT_K, POS_K = 5, 20

        @block.sync
        def _(sp):
            sp.dma_start(ident[:, :], const["ident_c"]).then_inc(const_in, 16)
            sp.dma_start(group[:, :], const["group_c"]).then_inc(const_in, 16)
            sp.dma_start(base[:, :, :, :, :].rearrange("p a b c d -> p (a b c d)"),
                         const["base_c"]).then_inc(const_in, 16)
            for h in range(HALVES):
                sp.dma_start(woff[:, h, :, 0:OFFS], w_off[h * P:(h + 1) * P, :, :]).then_inc(const_in, 16)
                sp.dma_start(raw[:, h, :], x_v[0, :, h, :]).then_inc(raw_in[h], 16)
            sp.wait_ge(boff_zero, 1)
            for j in range(4):
                sp.dma_start(boff[OPAD * j:OPAD * j + OFFS, :],
                             b_off.rearrange("(o a) -> o a", a=1)).then_inc(boff_in, 16)
            sp.wait_ge(set_up, 2)
            rows = ((PADW - 1, 0, 4), (0, 0, 2), (PADW - 2, 2, 4))
            tv = table_v.rearrange("b y x s c -> b y x (s c)")
            for y, s0, s1 in rows:
                for b in range(B):
                    sp.dma_start(tv[b, y, :, s0 * C:s1 * C],
                                 zero[0:PADW, 0:(s1 - s0) * C]).then_inc(border_out, 16)
            for dy in range(2):
                y0 = 1 - dy
                for xx, s0, s1 in ((PADW - 1, 2 * dy, 2 * dy + 2), (0, 2 * dy, 2 * dy + 1),
                                   (PADW - 2, 2 * dy + 1, 2 * dy + 2)):
                    for b in range(B):
                        sp.dma_start(tv[b, y0:y0 + H, xx, s0 * C:s1 * C],
                                     zero[0:H, 0:(s1 - s0) * C]).then_inc(border_out, 16)
            with sp.Fori(0, B) as b:
                image = sp.snap(upto(b, B - 1))
                following = sp.snap(upto((b + 1) & (B - 1), B - 1))
                for g in range(GROUPS):
                    sp.wait_ge(tok_ready, b * (GROUPS * 4) + 4 * (g + 1))
                    sp.sem_inc(sp_gate, 1)
                    for r in range(2):
                        for s in range(CORNERS):
                            dy, dx = s // 2, s % 2
                            y0 = 2 * GROUP_TILES * g + r - dy + 1
                            sp.dma_start(
                                table_v[image, y0:y0 + 2 * GROUP_TILES - 1:2, 1 - dx:1 - dx + W, s, :]
                                .rearrange("y x c -> x y c"),
                                tok[W * r:W * r + W, g % 2, :, :]).then_inc(table_out[g % 2], 16)
                for h in range(HALVES):
                    sp.wait_ge(turned, b * 16 + 16)
                    sp.wait_ge(padded_ready, b * HALVES + HALVES)
                    sp.sem_inc(sp_gate, 1)
                    sp.dma_start(raw[:, h, :], x_v[following, :, h, :]).then_inc(raw_in[h], 16)
            for i in range(2):
                sp.wait_ge(table_out[i], 16 * 8 * 2 * B)
            sp.wait_ge(border_out, 16 * 9 * B)
            for h in range(HALVES):
                sp.wait_ge(raw_in[h], 16 * (B + 1))
            sp.wait_ge(boff_in, 64)

        @block.gpsimd
        def _(pool):
            pool.memset(boff[:, :], 0.0).then_inc(boff_zero, 1)
            pool.memset(power[:, :], -0.5).then_inc(set_up, 1)
            pool.memset(zero[:, :], 0.0).then_inc(set_up, 1)
            pool.memset(woff[:, :, :, OFFS:OPAD], 0.0).then_inc(set_up, 1)
            pool.memset(padded[:, :, :, :], 0.0).then_inc(set_up, 1)
            pool.wait_ge(set_up, 4)
            with pool.Fori(0, B) as b:
                pool.wait_ge(var_ready, b + 1)
                pool.tensor_tensor(grs[:, :], gvar[:, :], power[:, :], ALU.pow).then_inc(rs_ready, 1)
                pool.wait_ge(off_ready, b * 2)
                for h in range(HALVES):
                    pool.wait_ge(normed, b * 2 + h + 1)
                    pool.sem_inc(pool_gate, 1)
                    pool.tensor_copy(padded[:, h, 1:H + 1, 1:W + 1],
                                     raw[:, h, :].rearrange("p (y x) -> p y x", x=W)).then_inc(padded_ready, 1)

        @block.vector
        def _(dve):
            st, po = Tally(STAT_K), Tally(POS_K)
            dve.memset(image_base[:, :], float(PADW + 1 - ENTRIES)).then_inc(base_set, 1)
            dve.wait_ge(base_set, 1)
            dve.wait_ge(const_in, 80)
            with dve.Fori(0, B) as b:
                st.begin()
                for h in range(HALVES):
                    dve.wait_ge(raw_in[h], (b + 1) * 16)
                    for c in range(STATS):
                        last = dve.bn_stats(stats[:, h, c, :], raw[:, h, c * CHUNK:(c + 1) * CHUNK])
                last.then_inc(stat_order, 1)
                dve.wait_ge(stat_order, st.next(b))
                dve.sem_inc(dve_gate, 1)
                for h in range(HALVES):
                    last = dve.bn_aggr(mv[:, h, :], stats[:, h, :, :].rearrange("p a b -> p (a b)"))
                last.then_inc(means_ready, 1)
                dve.wait_ge(grouped, b * 2 + 1)
                dve.tensor_copy(gmean[:, :], ps_group[:, 0, 0:HALVES]).then_inc(stat_order, 1)
                dve.wait_ge(means_ready, b * 2 + 1)
                dve.wait_ge(stat_order, st.next(b))
                dve.tensor_tensor(dev[:, :], mv[:, :, 0], gmean[:, :], ALU.subtract).then_inc(stat_order, 1)
                dve.wait_ge(stat_order, st.next(b))
                dve.tensor_tensor(dev[:, :], dev[:, :], dev[:, :], ALU.mult).then_inc(stat_order, 1)
                dve.wait_ge(stat_order, st.next(b))
                dve.tensor_tensor(spread[:, :], dev[:, :], mv[:, :, 1], ALU.add).then_inc(means_ready, 1)
                dve.wait_ge(grouped, b * 2 + 2)
                dve.tensor_scalar(gvar[:, :], ps_group[:, 1, 0:HALVES], GN_EPS, None, ALU.add).then_inc(var_ready, 1)
                dve.wait_ge(rs_ready, b + 1)
                for h in range(HALVES):
                    dve.tensor_scalar(raw[:, h, :], raw[:, h, :], gmean[:, h:h + 1], grs[:, h:h + 1],
                                      ALU.subtract, ALU.mult).then_inc(normed, 1)
                dve.tensor_scalar(image_base[:, :], image_base[:, :], float(ENTRIES), None,
                                  ALU.add).then_inc(stat_order, 1)
                dve.wait_ge(stat_order, st.next(b))
                st.end()
                po.begin()
                image = upto(b, B - 1)
                for r in range(ROUNDS):
                    here = ps_pos[:, r, :].rearrange("p (q j o) -> p q j o", q=PXT, j=4)[:, :, :, 0:OFFS]
                    dve.wait_ge(off_turned, b * 2 + r + 1)

                    def chained(ins):
                        ins.then_inc(pos_order, 1)
                        dve.wait_ge(pos_order, po.next(b))

                    dve.tensor_tensor(pos[:, :, :, :], here, base[:, r, :, :, :], ALU.add).then_inc(pos_taken, 1)
                    dve.wait_ge(pos_taken, b * 2 + r + 1)
                    chained(dve.tensor_scalar(pos[:, :, :, :], pos[:, :, :, :], -1.0, float(H),
                                              ALU.max, ALU.min))
                    chained(dve.tensor_copy(whole_i[:, :, :, :], pos[:, :, :, :]))
                    chained(dve.tensor_copy(whole[:, :, :, :], whole_i[:, :, :, :]))
                    chained(dve.tensor_tensor(above[:, :, :, :], whole[:, :, :, :], pos[:, :, :, :], ALU.is_gt))
                    chained(dve.tensor_tensor(floor[:, :, :, :], whole[:, :, :, :], above[:, :, :, :],
                                              ALU.subtract))
                    chained(dve.tensor_tensor(frac[:, 1, :, :, :], pos[:, :, :, :], floor[:, :, :, :],
                                              ALU.subtract))
                    chained(dve.tensor_scalar(frac[:, 0, :, :, :], frac[:, 1, :, :, :], -1.0, 1.0,
                                              ALU.mult, ALU.add))
                    f = floor[:, :, :, :].rearrange("p q j (t a) -> p q j t a", a=2)
                    for j in range(4):
                        last = dve.scalar_tensor_tensor(entry[:, :, j, :], f[:, :, j, :, 0], float(PADW),
                                                        f[:, :, j, :, 1], ALU.mult, ALU.add)
                    chained(last)
                    chained(dve.tensor_scalar(
                        idx_all[:, image, r, :, :, :].rearrange("p j q t -> p q j t"),
                        entry[:, :, :, :], image_base[:, 0:1], None, ALU.add))
                    fr = frac[:, :, :, :, :].rearrange("p n q j (t a) -> p n q j t a", a=2)
                    for s in range(CORNERS):
                        dy, dx = s // 2, s % 2
                        for j in range(4):
                            last = dve.tensor_tensor(wts_all[:, image, r, j, :, :, s],
                                                     fr[:, dy, :, j, :, 0], fr[:, dx, :, j, :, 1], ALU.mult)
                    chained(last)
                po.end()

        @block.scalar
        def _(act):
            act.wait_ge(boff_in, 64)
            with act.Fori(0, B) as b:
                for g in range(GROUPS):
                    act.wait_ge(table_out[g % 2], (b * 2 + g // 2) * 128)
                    for k in range(4):
                        n = 4 * g + k
                        act.wait_ge(turned, b * 16 + n + 1)
                        act.activation(tok[:, g % 2, 2 * k:2 * k + 2, :].rearrange("p t c -> p (t c)"),
                                       ps_tok[:, n % 2, :], ACT.Copy).then_inc(tok_ready, 1)
                for r in range(ROUNDS):
                    act.wait_ge(off_ready, b * 2 + r + 1)
                    act.activation(off[:, r, :], ps_off[:, r, :], ACT.Identity,
                                   bias=boff[:, 0:1]).then_inc(off_kept, 1)

        @block.tensor
        def _(pe):
            pe.wait_ge(const_in, 80)
            pe.wait_ge(set_up, 4)
            with pe.Fori(0, B) as b:
                for k, src in enumerate((mv[:, :, 0], spread[:, :])):
                    pe.wait_ge(means_ready, b * 2 + k + 1)
                    pe.matmul(ps_group[:, k, 0:HALVES], group[:, :], src, start=True, stop=True).then_inc(grouped, 1)
                pe.wait_ge(normed, b * 2 + 2)
                for n in range(N // P // 2):
                    if n >= 2:
                        pe.wait_ge(tok_ready, b * 16 + n - 1)
                    else:
                        pe.wait_ge(tok_ready, b * 16)
                    for t in range(2):
                        px = P * (2 * n + t)
                        for h in range(HALVES):
                            at = (t * HALVES + h) * P
                            last = pe.matmul(ps_tok[:, n % 2, at:at + P], raw[:, h, px:px + P],
                                             ident[:, :], is_transpose=True, start=True, stop=True)
                    last.then_inc(turned, 1)
                for r in range(ROUNDS):
                    pe.wait_ge(off_kept, b * 2)
                    pe.wait_ge(padded_ready, b * 2 + 2)
                    for h in range(HALVES):
                        for t in range(TAPS):
                            ky, kx = t // 3, t % 3
                            for j in range(4):
                                y = 8 * (4 * r + j) + ky
                                last = pe.matmul(ps_off[OPAD * j:OPAD * (j + 1), r, :], woff[:, h, t, :],
                                                 padded[:, h, y:y + 8, kx:kx + W],
                                                 start=(h == 0 and t == 0),
                                                 stop=(h == HALVES - 1 and t == TAPS - 1))
                    last.then_inc(off_ready, 1)
                for r in range(ROUNDS):
                    pe.wait_ge(off_kept, b * 2 + r + 1)
                    pe.wait_ge(pos_taken, b * 2)
                    for q in range(PXT):
                        last = pe.matmul(ps_pos[:, r, q * P:(q + 1) * P], off[:, r, q * P:(q + 1) * P],
                                         ident[:, :], is_transpose=True, start=True, stop=True)
                    last.then_inc(off_turned, 1)


def conv_stage(nc, w_conv, gamma, beta, table, conv, keep):
    ident, idx_all, wts_all = keep["ident"], keep["idx_all"], keep["wts_all"]
    bn_scale, bn_shift = keep["bn_scale"], keep["bn_shift"]
    ROW = CORNERS * C
    GATHERS = PXT * TAPS
    NPAIR = GATHERS // 2
    RING = 12
    MIX = 3
    KC = TAPS * HALVES
    idx_v = idx_all[:, :, :, :, :, :].rearrange("p b r j q t -> p (b r j) (q t)")
    wts_v = wts_all[:, :, :, :, :, :, :].rearrange("p b r j q t s -> p (b r j) (q t s)")
    conv_v = conv.rearrange("(m p) n -> p m n", p=P)

    with ExitStack() as ctx:
        def sb(name, shape, dt=F32):
            return ctx.enter_context(nc.sbuf_tensor(name, shape, dt))

        def ps(name, shape):
            return ctx.enter_context(nc.psum_tensor(name, shape, F32))

        def sem(name):
            return ctx.enter_context(nc.semaphore(name))

        weights = sb("weights", [P, TAPS, HALVES, C])
        rows = sb("rows", [P, RING, ROW])
        mixed_sb = sb("mixed_sb", [P, 2 * MIX, C])
        sampled = sb("sampled", [P, 2, KC, CHUNK])
        conv_sb = sb("conv_sb", [P, 2, HALVES, CHUNK])
        idx = sb("idx", [P, 2, GATHERS], I32)
        wts = sb("wts", [P, 2, GATHERS * CORNERS])
        stats = sb("bn_stats", [P, HALVES, TILES, 6])
        mv = sb("bn_mv", [P, HALVES, 2])
        aff = sb("aff", [P, 2, HALVES])
        power = sb("bn_power", [P, HALVES])
        rs = sb("bn_rs", [P, HALVES])
        ps_turn = ps("ps_turn", [P, MIX, CHUNK])
        ps_conv = ps("ps_conv", [P, 2, HALVES, CHUNK])

        weights_in = sem("weights_in")
        sp_gate = sem("conv_sp_gate")
        pool_gate = sem("conv_pool_gate")
        idx_ready = sem("idx_ready")
        rows_in = [sem(f"rows_in{i}") for i in range(RING)]
        scaled = sem("scaled")
        mix_order = sem("mix_order")
        mixed = sem("mixed")
        turned = sem("pair_turned")
        filed = sem("filed")
        conv_ready = sem("conv_ready")
        conv_kept = sem("conv_kept")
        counted = sem("counted")
        conv_out = [sem(f"conv_out{i}") for i in range(2)]
        bn_step = sem("bn_step")
        pow_ready = sem("pow_ready")
        block = ctx.enter_context(nc.Block())

        def slot_of(g):
            pair, side = g // 2, g % 2
            return 2 * (pair // TAPS) + side, pair % TAPS

        def tiles(eng, step):
            step(0, 0, 0)
            step(1, 1, 0)
            with eng.Fori(1, TILES // 2) as k:
                step(k * 2, 0, k)
                step(k * 2 + 1, 1, k)

        @block.sync
        def _(sp):
            for t in range(TAPS):
                sp.dma_start(weights[:, t, :, :], w_conv[:, t, :].rearrange("(h p) o -> p h o", p=P))\
                  .then_inc(weights_in, 16)
            sp.dma_start(aff[:, 0, :], gamma.rearrange("(m p) -> p m", p=P),
                         allow_slow_non_contiguous=True).then_inc(weights_in, 16)
            sp.dma_start(aff[:, 1, :], beta.rearrange("(m p) -> p m", p=P),
                         allow_slow_non_contiguous=True).then_inc(weights_in, 16)
            with sp.Fori(0, TILES // 2) as k:
                for par in range(2):
                    at = sp.snap(k * (2 * CHUNK) + par * CHUNK)
                    sp.wait_ge(conv_kept, k * 2 + par + 1)
                    sp.sem_inc(sp_gate, 1)
                    sp.dma_start(conv_v[:, :, bass.ds(at, CHUNK)], conv_sb[:, par, :, :])\
                      .then_inc(conv_out[par], 16)
            for par in range(2):
                sp.wait_ge(conv_out[par], 16 * (TILES // 2))

        @block.gpsimd
        def _(pool):
            pool.memset(power[:, :], -0.5).then_inc(bn_step, 1)

            def step(s, par, k):
                pool.wait_ge(idx_ready, s + 1)
                for g in range(GATHERS):
                    if not isinstance(s, int) or s * GATHERS + g >= RING:
                        pool.wait_ge(mixed, s * GATHERS + g - RING + 1)
                        pool.sem_inc(pool_gate, 1)
                    q, t = slot_of(g)
                    pool.indirect_dma_start(rows[:, g % RING, :], None, table,
                                            bass.IndirectOffsetOnAxis(idx[:, par, q * TAPS + t:q * TAPS + t + 1], 0))\
                        .then_inc(rows_in[g % RING], 16)

            tiles(pool, step)
            pool.wait_ge(bn_step, 2)
            pool.tensor_tensor(rs[:, :], mv[:, :, 1], power[:, :], ALU.pow).then_inc(pow_ready, 1)

        @block.scalar
        def _(act):
            def conv_copy(par, n):
                act.wait_ge(conv_ready, n + 1)
                if not isinstance(n, int) or n >= 2:
                    act.wait_ge(conv_out[par], (n // 2) * 16 if isinstance(n, int) else upto(n >> 1, TILES) * 16)
                act.activation(conv_sb[:, par, :, :].rearrange("p m n -> p (m n)"),
                               ps_conv[:, par, :, :].rearrange("p m n -> p (m n)"), ACT.Copy).then_inc(conv_kept, 1)

            def step(s, par, k):
                act.wait_ge(idx_ready, s + 1)

                def file(n):
                    act.wait_ge(turned, s * NPAIR + n + 1)
                    half, t = n // TAPS, n % TAPS
                    if n == 0 and (not isinstance(s, int) or s >= 2):
                        act.wait_ge(conv_ready, s - 1)
                    act.activation(sampled[:, par, 2 * t:2 * t + 2, half * 256:half * 256 + 256],
                                   ps_turn[:, n % MIX, :].rearrange("p (h n) -> p h n", h=HALVES),
                                   ACT.Copy).then_inc(filed, 1)

                for n in range(NPAIR):
                    for g in (2 * n, 2 * n + 1):
                        q, t = slot_of(g)
                        act.wait_ge(rows_in[g % RING], (s * (GATHERS // RING) + g // RING + 1) * 16)
                        if not isinstance(s, int) or s * NPAIR + n >= MIX:
                            act.wait_ge(turned, s * NPAIR + n - MIX + 1)
                        at = (q * TAPS + t) * CORNERS
                        act.activation(mixed_sb[:, g % (2 * MIX), :], rows[:, g % RING, 0:C], ACT.Copy,
                                       scale=wts[:, par, at:at + 1]).then_inc(scaled, 1)
                    if n >= 2:
                        file(n - 2)
                    if n == 4 and (not isinstance(s, int) or s >= 2):
                        conv_copy(par, s - 2)
                file(NPAIR - 2)
                file(NPAIR - 1)

            tiles(act, step)
            conv_copy(0, TILES - 2)
            conv_copy(1, TILES - 1)

        @block.vector
        def _(dve):
            def load_indices(s, par):
                dve.tensor_copy(idx[:, par, :], idx_v[:, s, :])
                dve.tensor_copy(wts[:, par, :], wts_v[:, s, :]).then_inc(idx_ready, 1)

            def count(s, par, n):
                dve.wait_ge(conv_kept, s + 1)
                for m in range(HALVES):
                    last = dve.bn_stats(stats[:, m, n, :], conv_sb[:, par, m, :])
                last.then_inc(counted, 1)

            load_indices(0, 0)

            def step(s, par, k):
                for n in range(NPAIR):
                    for corner in range(1, CORNERS):
                        for side in range(2):
                            g = 2 * n + side
                            q, t = slot_of(g)
                            done = s * (4 * NPAIR) + 4 * n + 2 * (corner - 2) + side + 1
                            if corner == 1:
                                dve.wait_ge(rows_in[g % RING], (s * (GATHERS // RING) + g // RING + 1) * 16)
                                dve.wait_ge(scaled, s * GATHERS + g + 1)
                            else:
                                dve.wait_ge(mix_order, done)
                            at = (q * TAPS + t) * CORNERS + corner
                            ins = dve.scalar_tensor_tensor(
                                mixed_sb[:, g % (2 * MIX), :], rows[:, g % RING, corner * C:(corner + 1) * C],
                                wts[:, par, at:at + 1], mixed_sb[:, g % (2 * MIX), :], ALU.mult, ALU.add)
                            if corner < CORNERS - 1:
                                ins.then_inc(mix_order, 1)
                            else:
                                ins.then_inc(mixed, 1)
                    if n == 2:
                        load_indices(upto((s + 1) & (TILES - 1), TILES - 1) if not isinstance(s, int) else s + 1,
                                     1 - par)
                    if n == 6 and (not isinstance(s, int) or s >= 2):
                        count(s - 2, par, s - 2 if isinstance(s, int) else upto(s - 2, TILES - 1))

            tiles(dve, step)
            count(TILES - 2, 0, TILES - 2)
            count(TILES - 1, 1, TILES - 1)
            dve.wait_ge(counted, TILES)
            for m in range(HALVES):
                last = dve.bn_aggr(mv[:, m, :], stats[:, m, :, :].rearrange("p a b -> p (a b)"))
            last.then_inc(counted, 1)
            dve.wait_ge(counted, TILES + 1)
            dve.tensor_scalar(mv[:, :, 1], mv[:, :, 1], BN_EPS, None, ALU.add).then_inc(bn_step, 1)
            dve.wait_ge(weights_in, 16 * (TAPS + 2))
            dve.wait_ge(pow_ready, 1)
            dve.tensor_tensor(bn_scale[:, :], aff[:, 0, :], rs[:, :], ALU.mult).then_inc(bn_step, 1)
            dve.wait_ge(bn_step, 3)
            dve.tensor_tensor(mv[:, :, 0], mv[:, :, 0], bn_scale[:, :], ALU.mult).then_inc(bn_step, 1)
            dve.wait_ge(bn_step, 4)
            dve.tensor_tensor(bn_shift[:, :], aff[:, 1, :], mv[:, :, 0], ALU.subtract).then_inc(bn_step, 1)

        @block.tensor
        def _(pe):
            pe.wait_ge(weights_in, 16 * (TAPS + 2))

            def product(s, par, kc):
                t, h = kc // HALVES, kc % HALVES
                pe.wait_ge(filed, s * NPAIR + TAPS + t + 1)
                if kc == 0 and (not isinstance(s, int) or s >= 2):
                    pe.wait_ge(conv_kept, s - 1)
                for m in range(HALVES):
                    last = pe.matmul(ps_conv[:, par, m, :], weights[:, t, h, m * P:(m + 1) * P],
                                     sampled[:, par, kc, :], start=(kc == 0), stop=(kc == KC - 1))
                if kc == KC - 1:
                    last.then_inc(conv_ready, 1)

            def step(s, par, k):
                for n in range(NPAIR):
                    pe.wait_ge(mixed, s * GATHERS + 2 * n + 2)
                    if not isinstance(s, int) or s * NPAIR + n >= MIX:
                        pe.wait_ge(filed, s * NPAIR + n - MIX + 1)
                    for h in range(HALVES):
                        for side in range(2):
                            g = 2 * n + side
                            at = h * 256 + side * P
                            last = pe.matmul(ps_turn[:, n % MIX, at:at + P],
                                             mixed_sb[:, g % (2 * MIX), h * P:(h + 1) * P],
                                             ident[:, :], is_transpose=True, start=True, stop=True)
                    last.then_inc(turned, 1)
                    if not isinstance(s, int) or s >= 1:
                        product(s - 1, 1 - par, n)

            tiles(pe, step)
            for kc in range(KC):
                product(TILES - 1, 1, kc)


def token_stage(nc, x, conv, d, out, keep):
    ident, bn_scale, bn_shift = keep["ident"], keep["bn_scale"], keep["bn_shift"]
    SUBS = CHUNK // P
    STEPS = TILES
    T_STEP, T_IMG = STEP_TILES, EXPERT_TILES
    T_ALL = T_IMG * B
    RING = 3
    assert T_STEP % RING == 0
    HID_LAG, TURN_LAG, OUT_LAG, STORE_LAG = 1, 2, 3, 5
    SCATTER = 16 * TOP_K * SUBS
    REGION = N + P
    BUFFER = E * REGION
    x_v = x.rearrange("b (h p) y x -> b p h (y x)", p=P)
    conv_v = conv.rearrange("(h p) (b n) -> b p h n", p=P, b=B)
    out_v = out.rearrange("b (h p) y x -> b p h (y x)", p=P)
    BODY, REST = CHUNK - SHIFT, SHIFT
    slots = nc.dram_tensor("slots", (2 * BUFFER, C), F32, kind="Internal").ap()
    results = [nc.dram_tensor(f"results{i}", (T_IMG * P, C), F32, kind="Internal").ap() for i in range(2)]
    base = nc.dram_tensor("firsts", (STEPS, P, SUBS * C), F32, kind="Internal").ap()

    with ExitStack() as ctx:
        def sb(name, shape, dt=F32):
            return ctx.enter_context(nc.sbuf_tensor(name, shape, dt))

        def ps(name, shape):
            return ctx.enter_context(nc.psum_tensor(name, shape, F32))

        def sem(name):
            return ctx.enter_context(nc.semaphore(name))

        wqk = sb("wqk", [P, HALVES, 2 * C])
        wv = sb("wv", [P, HALVES, 2, P])
        wo = sb("wo", [P, HALVES, C])
        wr = sb("wr", [P, HALVES, E])
        w1 = sb("w1", [P, HALVES, E, C])
        w2 = sb("w2", [P, HALVES, E, C])
        b1 = sb("b1", [P, E, C])
        b2 = sb("b2", [P, E, C])
        bqk = sb("bqk", [P, 4])
        bv = sb("bv", [P, P])
        bo = sb("bo", [P, C])
        bias = sb("bias", [P, 2, HEADS * WIN])
        lower = sb("lower", [P, E * E])
        strict = sb("strict", [P, P])
        ones = sb("ones", [P, P])
        region = sb("region", [P, 2, E])
        row_id = sb("row_id", [P, E])
        octal = sb("octal", [1, E])
        tile_id = sb("tile_id", [1, T_IMG])
        power = sb("c_power", [P, 4])
        euler = sb("euler", [P, SUBS * E])
        zero = sb("c_zero", [P, C])
        xl = sb("xl", [P, 2, HALVES, CHUNK])
        yl = sb("yl", [P, 2, HALVES, CHUNK])
        res = sb("res", [P, 2, SUBS, C])
        nrm = sb("nrm", [P, SUBS, C])
        tok = sb("ctok", [P, 2, SUBS, C])
        nrm_t = sb("nrm_t", [P, HALVES, CHUNK])
        qt = sb("qt", [P, HALVES, CHUNK])
        kdiag = sb("kdiag", [P, HALVES, HG, CHUNK])
        vdiag = sb("vdiag", [P, WINS, PAIRS, 2 * HD])
        prob = sb("prob", [P, SUBS, HEADS * WIN])
        prob_t = sb("prob_t", [P, SUBS, HEADS * WIN])
        att_t = sb("att_t", [P, HALVES, CHUNK])
        tok_t = sb("tok_t", [P, HALVES, CHUNK])
        first = sb("first", [P, SUBS * C])
        stats = sb("ln_stats", [P, SUBS, 6])
        mv = sb("ln_mv", [P, SUBS, 2])
        var = sb("ln_var", [P, SUBS])
        rs = sb("ln_rs", [P, SUBS])
        top = sb("top", [P, SUBS * HEADS])
        total = sb("total", [P, SUBS * HEADS])
        inverse = sb("inverse", [P, SUBS * HEADS])
        rmax = sb("rmax", [P, SUBS])
        rexp = sb("rexp", [P, SUBS, E])
        rsum = sb("rsum", [P, SUBS])
        rprob = sb("rprob", [P, SUBS, E])
        more = sb("more", [P, SUBS, E, E])
        same = sb("same", [P, SUBS, E, E])
        rank = sb("rank", [P, SUBS, E])
        sel = sb("sel", [P, SUBS, E])
        chosen = sb("chosen", [P, SUBS, E])
        comb = sb("comb", [P, SUBS, E])
        filled = sb("filled", [P, E])
        place = sb("place", [P, SUBS, E])
        high = sb("high", [P, SUBS])
        both = sb("both", [P, SUBS])
        is_high = sb("is_high", [P, SUBS, E])
        weighed = sb("weighed", [P, SUBS, E])
        scat_idx = sb("scat_idx", [P, 2, TOP_K, SUBS], I32)
        row_hist = sb("row_hist", [P, STEPS, TOP_K * SUBS])
        gate_hist = sb("gate_hist", [P, STEPS, TOP_K * SUBS])
        pad_f = sb("pad_f", [P, E])
        pad_idx = sb("pad_idx", [P, E], I32)
        need_i = sb("need_i", [P, E], I32)
        need = sb("need", [P, E])
        gap = sb("gap", [P, E])
        shrink = sb("shrink", [P, 2, E])
        start = sb("start", [1, 3, E])
        beyond = sb("beyond", [1, T_IMG, E])
        scratch = sb("scratch", [1, T_IMG, E])
        rows_f = sb("rows_f", [1, 3, T_IMG])
        ids = sb("ids", [1, OUT_LAG + T_ALL + T_STEP + E])
        packing = sb("packing", [1, 2, IMG_CHUNKS + 1, E])
        words_f = sb("words_f", [1, 2, IMG_CHUNKS + 1])
        words = sb("words", [1, 2, STEPS + 1], I32)
        row_in = sb("row_in", [1, T_ALL], I32)
        xs = sb("xs", [P, RING, C])
        xs_t = sb("xs_t", [P, 2, HALVES, P])
        hid = sb("hid", [P, 2, C])
        hid_t = sb("hid_t", [P, 2, HALVES, P])
        ys = sb("ys", [P, RING, C])
        region_of = sb("region_of", [P, TOP_K * SUBS, E])
        shift_by = sb("shift_by", [P, TOP_K * SUBS])
        cidx = sb("cidx", [P, 2, TOP_K * SUBS], I32)
        cgate = sb("cgate", [P, 2, TOP_K * SUBS])
        got = sb("got", [P, TOP_K, SUBS, C])
        acc = sb("acc", [P, SUBS, C])
        final = sb("final", [P, HALVES, CHUNK])
        rel, flip = final[0:WIN, 0, :], final[0:WIN, 1, 0:P]

        fa = ps("fa", [P, 2, CHUNK])
        ga = ps("ga", [P, 2, CHUNK])
        pt = ps("pt", [P, 2, HALVES, P])
        ph = ps("ph", [P, CHUNK])
        py = ps("py", [P, CHUNK])
        pf = ps("pf", [P, CHUNK])
        fa_all = fa[:, :, :].rearrange("p a n -> p (a n)")
        ga_all = ga[:, :, :].rearrange("p a n -> p (a n)")

        weights_in = sem("c_weights_in")
        experts_in = sem("experts_in")
        tables = sem("tables")
        bias_turned = sem("bias_turned")
        bias_kept = sem("bias_kept")
        loads_in = [sem(f"loads_in{i}") for i in range(2)]
        relued = sem("relued")
        summed = sem("summed")
        x_turned = sem("x_turned")
        front_order = sem("front_order")
        back_order = sem("back_order")
        var_ready = [sem(f"var_ready{n}") for n in (1, 2)]
        rs_ready = [sem(f"rs_ready{n}") for n in (1, 2)]
        n1_ready = sem("n1_ready")
        bo_added = sem("bo_added")
        n1_turned = sem("n1_turned")
        n1_kept = sem("n1_kept")
        q_ready = sem("q_ready")
        k_ready = sem("k_ready")
        q_kept = sem("q_kept")
        k_kept_act = sem("k_kept_act")
        k_kept_dve = sem("k_kept_dve")
        v_ready = sem("v_ready")
        v_kept = sem("v_kept")
        scored = sem("scored")
        shifted = sem("shifted")
        exped = sem("exped")
        probs_ready = sem("probs_ready")
        p_turned = sem("p_turned")
        p_kept = sem("p_kept")
        mixed_v = sem("mixed_v")
        att_kept = sem("att_kept")
        projected = sem("projected")
        n2_ready = sem("n2_ready")
        first_ready = sem("first_ready")
        first_out = sem("first_out")
        n2_turned = sem("n2_turned")
        n2_kept = sem("n2_kept")
        routed = sem("routed")
        route_in = sem("route_in")
        route_exp = sem("route_exp")
        comb_ready = sem("comb_ready")
        ranked = sem("ranked")
        place_order = sem("place_order")
        placed = sem("placed")
        scattered = [sem(f"scattered{i}") for i in range(2)]
        padded = sem("padded")
        pads_out = sem("pads_out")
        table_order = sem("table_order")
        table_ready = sem("table_ready")
        xs_in = [sem(f"xs_in{i}") for i in range(RING)]
        xs_turned = sem("xs_turned")
        xs_kept = sem("xs_kept")
        hid_ready = sem("hid_ready")
        hid_biased = sem("hid_biased")
        hid_done = sem("hid_done")
        hid_turned = sem("hid_turned")
        hid_kept = sem("hid_kept")
        y_ready = sem("y_ready")
        y_kept = sem("y_kept")
        ys_out = [sem(f"ys_out{i}") for i in range(RING)]
        cidx_order = sem("cidx_order")
        cidx_ready = sem("cidx_ready")
        got_in = [sem(f"got_in{u}") for u in range(SUBS)]
        acc_in = sem("acc_in")
        acc_half = sem("acc_half")
        acc_done = sem("acc_done")
        out_turned = sem("out_turned")
        out_kept = sem("out_kept")
        stored = sem("stored")
        sp_gate, dve_gate, pool_gate, pe_gate = sem("c_sp_gate"), sem("c_dve_gate"), sem("c_pool_gate"), sem("c_pe_gate")
        block = ctx.enter_context(nc.Block())
        WEIGHTS, TABLES, EXPERTS = 21, 9, 6
        FRONT_K, BACK_K, PLACE_K, TABLE_K = 3, 24, 7, 15

        def steps(eng, step, flush=None):
            for img in range(B + 2):
                i0 = img * IMG_CHUNKS
                if img == B + 1 and flush is not None:
                    flush()
                step(i0, 0, img)
                with eng.Fori(0, IMG_CHUNKS // 2 - 1) as k:
                    step(k * 2 + (i0 + 1), 1, img)
                    step(k * 2 + (i0 + 2), 0, img)
                step(i0 + IMG_CHUNKS - 1, 1, img)

        def has_front(i):
            return not isinstance(i, int) or i + 1 < STEPS

        def expert_of(eng, m):
            at = m if isinstance(m, int) else upto(m, STEPS)
            loaded = {}

            def who(t, lag):
                w, j = divmod(t - lag + OUT_LAG, E)
                if w not in loaded:
                    at_ap = words[0:1, w, at:at + 1] if isinstance(at, int) else words[0:1, w, bass.ds(at, 1)]
                    loaded[w] = eng.value_load(at_ap, min_val=0, max_val=8 ** E - 1)
                return upto((loaded[w] >> (3 * j)) & (E - 1), E - 1)

            return who

        def stages(img):
            return img < B, 1 <= img <= B, img >= 2

        def at_least(eng, semaphore, value):
            if not isinstance(value, int) or value > 0:
                eng.wait_ge(semaphore, value)

        def columns(eng, i):
            if isinstance(i, int):
                return i % IMG_CHUNKS * CHUNK + SHIFT, (i + 1) % IMG_CHUNKS * CHUNK
            return (eng.snap(upto((i & (IMG_CHUNKS - 1)) * CHUNK + SHIFT, N - BODY)),
                    eng.snap(upto(((i + 1) & (IMG_CHUNKS - 1)) * CHUNK, N - REST)))

        def half_of(i):
            return i // 2 if isinstance(i, int) else upto(i >> 1, STEPS)

        def tile(m, t, lag):
            g = m * T_STEP + t - lag
            if isinstance(m, int) and not 0 <= g < T_ALL:
                return None
            return g

        @block.sync
        def _(sp):
            def load(nxt, par, turned):
                body, rest = columns(sp, nxt)
                image = nxt // IMG_CHUNKS if isinstance(nxt, int) else sp.snap(upto(nxt >> 3, B - 1))
                at_least(sp, x_turned, turned)
                sp.sem_inc(sp_gate, 1)
                for src, dst in ((x_v, xl), (conv_v, yl)):
                    sp.dma_start(dst[:, par, :, 0:BODY], src[image, :, :, bass.ds(body, BODY)])\
                      .then_inc(loads_in[par], 16)
                    sp.dma_start(dst[:, par, :, BODY:CHUNK], src[image, :, :, bass.ds(rest, REST)])\
                      .then_inc(loads_in[par], 16)

            load(0, 0, 0)
            for h in range(HALVES):
                rows = slice(h * P, (h + 1) * P)
                sp.dma_start(wqk[:, h, :], d["w_qk"][rows, :]).then_inc(weights_in, 16)
                sp.dma_start(wv[:, h, :, :].rearrange("p a n -> p (a n)"), d["w_v"][rows, :]).then_inc(weights_in, 16)
                sp.dma_start(wo[:, h, :], d["w_out"][rows, :]).then_inc(weights_in, 16)
                sp.dma_start(wr[:, h, :], d["w_router"][rows, :]).then_inc(weights_in, 16)
                sp.dma_start(bv[64 * h:64 * h + 64, :], d["b_v"][h:h + 1, :].partition_broadcast(64)
                             .rearrange("p a n -> p (a n)")).then_inc(weights_in, 16)
            sp.dma_start(rel.rearrange("p (h k) -> p h k", k=WIN),
                         bass.AP(d["rel_rev"].tensor, 0, [[1, WIN], [2 * WIN - 1, HEADS], [1, WIN]]))\
              .then_inc(weights_in, 16)
            sp.dma_start(flip, d["flip_c"]).then_inc(weights_in, 16)
            sp.dma_start(bqk[:, :], d["b_qk"]).then_inc(weights_in, 16)
            sp.dma_start(bo[:, :], d["b_out"].partition_broadcast(P)).then_inc(weights_in, 16)
            sp.dma_start(lower[:, :], d["lower_c"]).then_inc(weights_in, 16)
            sp.dma_start(bias[:, 1, :], d["apart_c"]).then_inc(weights_in, 16)
            sp.dma_start(strict[:, :], d["strict_c"]).then_inc(weights_in, 16)
            sp.dma_start(region[:, :, :].rearrange("p a e -> p (a e)"), d["region_c"]).then_inc(weights_in, 16)
            sp.dma_start(row_id[:, :], d["row_id_c"]).then_inc(weights_in, 16)
            sp.dma_start(octal[:, :], d["octal_c"]).then_inc(weights_in, 16)
            sp.dma_start(tile_id[:, :], d["tile_id_c"]).then_inc(weights_in, 16)
            load(1, 1, 0)
            for h in range(HALVES):
                rows = slice(h * P, (h + 1) * P)
                sp.dma_start(w1[:, h, :, :], d["w_1"][:, rows, :].rearrange("e p n -> p e n")).then_inc(experts_in, 16)
                sp.dma_start(w2[:, h, :, :], d["w_2"][:, rows, :].rearrange("e p n -> p e n")).then_inc(experts_in, 16)
            sp.dma_start(b1[:, :, :].rearrange("p e n -> p (e n)"), d["b_1"].partition_broadcast(P))\
              .then_inc(experts_in, 16)
            sp.dma_start(b2[:, :, :].rearrange("p e n -> p (e n)"), d["b_2"].partition_broadcast(P))\
              .then_inc(experts_in, 16)

            load(2, 0, 1)

            def expert_slot(m, t, img):
                g = tile(m, t, 0)
                if g is not None:
                    entry = slice(g, g + 1) if isinstance(g, int) else bass.ds(upto(g, T_ALL - 1), 1)
                    row = sp.value_load(row_in[0:1, entry], min_val=0, max_val=2 * BUFFER - P)
                    at_least(sp, xs_turned, g - RING + 1)
                    sp.sem_inc(sp_gate, 1)
                    sp.dma_start(xs[:, t % RING, :], slots[bass.ds(row, P), :]).then_inc(xs_in[t % RING], 16)
                g = tile(m, t, STORE_LAG)
                if g is not None:
                    if isinstance(g, int):
                        image, row = g // T_IMG, g % T_IMG * P
                    else:
                        image = img - 1
                        row = sp.snap(upto((g - image * T_IMG) * P, (T_IMG - 1) * P))
                    sp.wait_ge(y_kept, g + 1)
                    sp.sem_inc(sp_gate, 1)
                    r = (t - STORE_LAG) % RING
                    sp.dma_start(results[image % 2][bass.ds(row, P), :], ys[:, r, :]).then_inc(ys_out[r], 16)

            def step(i, par, img):
                att, exp, com = stages(img)
                m, c = i - IMG_CHUNKS, i - 2 * IMG_CHUNKS
                if exp and isinstance(m, int) and m % IMG_CHUNKS == 0:
                    sp.wait_ge(table_ready, img)
                    for half in range(2):
                        sp.wait_ge(scattered[half], SCATTER * (IMG_CHUNKS // 2) * img)
                    sp.wait_ge(pads_out, 16 * E * img)
                    sp.sem_inc(sp_gate, 1)
                if com:
                    which = c if isinstance(c, int) else sp.snap(upto(c, STEPS - 1))
                    at_least(sp, out_turned, c * 2)
                    sp.sem_inc(sp_gate, 1)
                    sp.dma_start(acc[:, :, :].rearrange("p u c -> p (u c)"), base[which, :, :]).then_inc(acc_in, 16)
                for t in range(T_STEP):
                    if exp:
                        expert_slot(m, t, img)
                    if t == 1 and att and has_front(i):
                        load(i + 3 if isinstance(i, int) else (i + 3) & (STEPS - 1), 1 - par, i + 2)
                if att:
                    which = i if isinstance(i, int) else sp.snap(upto(i, STEPS - 1))
                    sp.wait_ge(first_ready, i + 1)
                    sp.sem_inc(sp_gate, 1)
                    sp.dma_start(base[which, :, :], first[:, :]).then_inc(first_out, 16)
                if com:
                    body, rest = columns(sp, c)
                    sp.wait_ge(out_kept, (c + 1) * 2)
                    sp.sem_inc(sp_gate, 1)
                    sp.dma_start(out_v[img - 2, :, :, bass.ds(body, BODY)], final[:, :, 0:BODY]).then_inc(stored, 16)
                    sp.dma_start(out_v[img - 2, :, :, bass.ds(rest, REST)], final[:, :, BODY:CHUNK]).then_inc(stored, 16)

            def flush():
                for t in range(STORE_LAG):
                    expert_slot(STEPS, t, B + 1)

            steps(sp, step, flush)
            sp.wait_ge(stored, 32 * STEPS)
            for par in range(2):
                sp.wait_ge(loads_in[par], 64 * (STEPS // 2 + 1))
            sp.wait_ge(first_out, 16 * STEPS)
            for r in range(RING):
                sp.wait_ge(ys_out[r], 16 * (T_ALL // RING))

        @block.gpsimd
        def _(pool):
            pool.memset(power[:, :], -0.5).then_inc(tables, 1)
            pool.memset(euler[:, :], 2.718281828459045).then_inc(tables, 1)
            pool.memset(kdiag[:, :, :, :], 0.0).then_inc(tables, 1)
            pool.memset(vdiag[:, :, :, :], 0.0).then_inc(tables, 1)
            pool.memset(ones[:, :], 1.0).then_inc(tables, 1)
            pool.memset(zero[:, :], 0.0).then_inc(tables, 1)
            pool.memset(ids[:, :], 0.0).then_inc(tables, 1)
            pool.memset(filled[:, :], 0.0).then_inc(tables, 1)
            pool.wait_ge(weights_in, 16 * WEIGHTS)
            pool.wait_ge(bias_kept, 1)
            pool.tensor_tensor(bias[:, 1, :], bias[:, 1, :], bias[:, 0, :], ALU.add).then_inc(tables, 1)
            pool.wait_ge(tables, TABLES)

            def add_x(i, par):
                pool.wait_ge(relued, i + 1)
                pool.tensor_tensor(xl[:, par, :, :], xl[:, par, :, :], yl[:, par, :, :], ALU.add).then_inc(summed, 1)

            def scatter(i, par):
                pool.wait_ge(placed, i + 1)
                pool.sem_inc(pool_gate, 1)
                for u in range(SUBS):
                    for k in range(TOP_K):
                        pool.indirect_dma_start(
                            slots, bass.IndirectOffsetOnAxis(scat_idx[:, par, k, u:u + 1], 0),
                            tok[:, par, u, :], None).then_inc(scattered[par], 16)

            def all_results(images):
                for r in range(RING):
                    pool.wait_ge(ys_out[r], 16 * (T_IMG // RING) * images)

            def all_results(images):
                for r in range(RING):
                    pool.wait_ge(ys_out[r], 16 * (T_IMG // RING) * images)

            def inverse_root(nth, j):
                pool.wait_ge(var_ready[nth], j + 1)
                pool.tensor_tensor(rs[:, :], var[:, :], power[:, :], ALU.pow).then_inc(rs_ready[nth], 1)

            def add_bo(j, par):
                pool.wait_ge(n1_ready, j + 1)
                for u in range(SUBS):
                    last = pool.tensor_tensor(res[:, par, u, :], res[:, par, u, :], bo[:, :], ALU.add)
                last.then_inc(bo_added, 1)

            add_x(0, 0)
            inverse_root(0, 0)
            add_x(1, 1)
            add_bo(0, 0)

            def step(i, par, img):
                att, exp, com = stages(img)
                c = i - 2 * IMG_CHUNKS
                if att and has_front(i):
                    inverse_root(0, i + 1)
                if (att and not (isinstance(i, int) and i == 0)) or (isinstance(i, int) and i == STEPS):
                    scatter(i - 1, 1 - par)
                if exp and isinstance(i, int) and i % IMG_CHUNKS == 0:
                    pool.wait_ge(padded, img)
                    for e in range(E):
                        pool.indirect_dma_start(slots, bass.IndirectOffsetOnAxis(pad_idx[:, e:e + 1], 0),
                                                zero[:, :], None).then_inc(pads_out, 16)
                if att and has_front(i):
                    add_x(i + 2, par)
                    add_bo(i + 1, 1 - par)
                if com:
                    if isinstance(c, int) and c % IMG_CHUNKS == 0:
                        all_results(img - 1)
                    pool.wait_ge(cidx_ready, c + 1)
                    pool.sem_inc(pool_gate, 1)
                    for u in range(SUBS):
                        for k in range(TOP_K):
                            pool.indirect_dma_start(got[:, k, u, :], None, results[img % 2],
                                                    bass.IndirectOffsetOnAxis(cidx[:, par, k * SUBS + u:k * SUBS + u + 1], 0))\
                                .then_inc(got_in[u], 16)
                if att:
                    inverse_root(1, i)
                    pool.wait_ge(n2_ready, i + 1)
                    at_least(pool, first_out, i * 16)
                    pool.tensor_tensor(first[:, :], res[:, par, :, :].rearrange("p u c -> p (u c)"),
                                       tok[:, par, :, :].rearrange("p u c -> p (u c)"), ALU.add)\
                        .then_inc(first_ready, 1)
                    pool.wait_ge(route_in, i + 1)
                    pool.tensor_tensor(rexp[:, :, :].rearrange("p u e -> p (u e)"), euler[:, :],
                                       rexp[:, :, :].rearrange("p u e -> p (u e)"), ALU.pow).then_inc(route_exp, 1)

            steps(pool, step)
            for par in range(2):
                pool.wait_ge(scattered[par], SCATTER * (STEPS // 2))
            pool.wait_ge(pads_out, 16 * E * B)

        @block.scalar
        def _(act):
            act.wait_ge(weights_in, 16 * WEIGHTS)
            act.wait_ge(bias_turned, 1)
            act.activation(bias[:, 0, :], ga[:, 0, :], ACT.Copy).then_inc(bias_kept, 1)
            act.wait_ge(tables, TABLES)

            def relu(i, par):
                act.wait_ge(loads_in[par], (half_of(i) + 1) * 64)
                for h in range(HALVES):
                    last = act.activation(yl[:, par, h, :], yl[:, par, h, :], ACT.Relu,
                                          bias=bn_shift[:, h:h + 1], scale=bn_scale[:, h:h + 1])
                last.then_inc(relued, 1)

            def expert_slot(m, t, par):
                g = tile(m, t, 0)
                if g is not None:
                    act.wait_ge(xs_turned, g + 1)
                    at_least(act, hid_ready, g - 1)
                    act.activation(xs_t[:, (par + t) % 2, :, :], pt[:, 0, :, :], ACT.Copy).then_inc(xs_kept, 1)
                g = tile(m, t, TURN_LAG)
                if g is not None:
                    act.wait_ge(hid_turned, g + 1)
                    at_least(act, y_ready, g - 1)
                    act.activation(hid_t[:, (par + t) % 2, :, :], pt[:, 1, :, :], ACT.Copy).then_inc(hid_kept, 1)
                g = tile(m, t, HID_LAG)
                if g is not None:
                    act.wait_ge(hid_biased, g + 1)
                    at = hid[:, (par + t + 1) % 2, :]
                    act.activation(at, at, ACT.Gelu).then_inc(hid_done, 1)

            def keep_normed(j):
                act.wait_ge(n1_turned, j + 1)
                act.activation(nrm_t[:, :, :].rearrange("p h n -> p (h n)"), fa_all, ACT.Copy).then_inc(n1_kept, 1)

            def keep_q(j):
                act.wait_ge(q_ready, j + 1)
                for h in range(HALVES):
                    last = act.activation(qt[:, h, :], fa[:, h, :], ACT.Identity, bias=bqk[:, h:h + 1])
                last.then_inc(q_kept, 1)

            def keep_k(j):
                act.wait_ge(k_ready, j + 1)
                for n in range(HG):
                    rows = slice(HD * n, HD * (n + 1))
                    last = act.activation(kdiag[rows, 0, n, :], fa[rows, 0, :], ACT.Identity, bias=bqk[rows, 2:3])
                last.then_inc(k_kept_act, 1)

            def exp_scores(i, v):
                act.wait_ge(shifted, 2 * i + v + 1)
                act.activation(prob[:, 2 * v:2 * v + 2, :], prob[:, 2 * v:2 * v + 2, :], ACT.Exp).then_inc(exped, 1)

            def keep_probs(i, v):
                for u in (2 * v, 2 * v + 1):
                    act.wait_ge(p_turned, i * SUBS + u + 1)
                    act.activation(prob_t[:, u, :], ga[:, u % 2, :], ACT.Copy).then_inc(p_kept, 1)

            relu(0, 0)
            relu(1, 1)
            keep_normed(0)
            keep_q(0)
            keep_k(0)

            def step(i, par, img):
                att, exp, com = stages(img)
                front = att and has_front(i)
                m, c = i - IMG_CHUNKS, i - 2 * IMG_CHUNKS

                def slot(t):
                    if exp:
                        expert_slot(m, t, par)

                if front:
                    relu(i + 2, par)
                if att:
                    exp_scores(i, 0)
                slot(0)
                slot(1)
                if att:
                    exp_scores(i, 1)
                slot(2)
                if att:
                    keep_probs(i, 0)
                if front:
                    keep_normed(i + 1)
                slot(3)
                if att:
                    keep_probs(i, 1)
                if front:
                    keep_q(i + 1)
                slot(4)
                if att:
                    act.wait_ge(mixed_v, i + 1)
                    act.activation(att_t[:, :, :].rearrange("p h n -> p (h n)"), ga_all, ACT.Copy).then_inc(att_kept, 1)
                if front:
                    keep_k(i + 1)
                slot(5)
                slot(6)
                slot(7)
                if com:
                    for v in range(2):
                        act.wait_ge(out_turned, c * 2 + v + 1)
                        at_least(act, stored, c * 32)
                        act.activation(final[:, :, 256 * v:256 * v + 256],
                                       pf[:, :].rearrange("p (h n) -> p h n", h=HALVES), ACT.Copy)\
                           .then_inc(out_kept, 1)
                if att:
                    act.wait_ge(n2_turned, i + 1)
                    act.activation(tok_t[:, :, :].rearrange("p h n -> p (h n)"), ga_all, ACT.Copy).then_inc(n2_kept, 1)
                slot(8)

            def flush():
                for t in range(OUT_LAG):
                    expert_slot(STEPS, t, 0)

            steps(act, step, flush)

        @block.vector
        def _(dve):
            dve.wait_ge(weights_in, 16 * WEIGHTS)
            dve.wait_ge(tables, TABLES)
            dve.wait_ge(experts_in, 16 * EXPERTS)
            forder, border = Tally(FRONT_K), Tally(BACK_K)
            porder, torder = Tally(PLACE_K), Tally(TABLE_K)

            def expert_slot(m, t, par, who):
                g = tile(m, t, HID_LAG)
                if g is not None:
                    dve.wait_ge(hid_ready, g + 1)
                    at_least(dve, hid_turned, g - 1)
                    at = (par + t + 1) % 2
                    dve.tensor_tensor(hid[:, at, :], ph[:, 0:C], b1[:, who(t, HID_LAG), :], ALU.add)\
                       .then_inc(hid_biased, 1)
                g = tile(m, t, OUT_LAG)
                if g is not None:
                    dve.wait_ge(y_ready, g + 1)
                    at_least(dve, ys_out[t % RING], (m * (T_STEP // RING) + t // RING - 1) * 16)
                    dve.tensor_tensor(ys[:, t % RING, :], py[:, 0:C], b2[:, who(t, OUT_LAG), :], ALU.add)\
                       .then_inc(y_kept, 1)

            def places(i, par, img):
                def chained(ins):
                    ins.then_inc(place_order, 1)
                    dve.wait_ge(place_order, porder.next(i))

                def over_u(a):
                    return a.unsqueeze(1).broadcast_to([P, SUBS, E])

                def over_e(a):
                    return a[:, :].unsqueeze(2).broadcast_to([P, SUBS, E])

                porder.begin()
                dve.wait_ge(ranked, i + 1)
                before_ = pf[:, 0:SUBS * E].rearrange("p (u e) -> p u e", e=E)
                chained(dve.tensor_tensor(place[:, :, :], before_, over_u(filled[:, :]), ALU.add))
                dve.tensor_tensor(filled[:, :], filled[:, :], pf[:, 64:64 + E], ALU.add)
                chained(dve.tensor_tensor(place[:, :, :], place[:, :, :], over_u(region[:, img % 2, :]), ALU.add))
                chained(dve.tensor_tensor(place[:, :, :], place[:, :, :], sel[:, :, :], ALU.mult))
                dve.tensor_reduce(high[:, :], place[:, :, :], AX_X, ALU.max)
                chained(dve.tensor_reduce(both[:, :], place[:, :, :], AX_X, ALU.add))
                dve.tensor_tensor(is_high[:, :, :], place[:, :, :], over_e(high), ALU.is_equal)
                chained(dve.tensor_tensor(both[:, :], both[:, :], high[:, :], ALU.subtract))
                chained(dve.tensor_tensor(sel[:, :, :], sel[:, :, :], is_high[:, :, :], ALU.subtract))
                hist = i if isinstance(i, int) else upto(i, STEPS - 1)
                dve.tensor_tensor(weighed[:, :, :], is_high[:, :, :], comb[:, :, :], ALU.mult)
                chained(dve.tensor_tensor(comb[:, :, :], sel[:, :, :], comb[:, :, :], ALU.mult))
                dve.tensor_reduce(gate_hist[:, hist, 0:SUBS], weighed[:, :, :], AX_X, ALU.add)
                dve.tensor_reduce(gate_hist[:, hist, SUBS:2 * SUBS], comb[:, :, :], AX_X, ALU.add)
                at_least(dve, scattered[par], half_of(i) * SCATTER)
                for k, rows in enumerate((high, both)):
                    dve.tensor_copy(row_hist[:, hist, k * SUBS:(k + 1) * SUBS], rows[:, :])
                    last = dve.tensor_scalar(scat_idx[:, par, k, :], rows[:, :], -1.0, None, ALU.add)
                last.then_inc(placed, 1)
                porder.end()

            def tile_table(img):
                def chained(ins):
                    ins.then_inc(table_order, 1)
                    dve.wait_ge(table_order, torder.next(img))

                torder.begin()
                one = slice(0, 1)
                first_row = float((img % 2) * BUFFER)
                at_least(dve, pads_out, 16 * E * img)
                dve.tensor_tensor(pad_f[:, :], filled[:, :], row_id[:, :], ALU.add)
                chained(dve.tensor_scalar(gap[:, :], filled[:, :], float(P - 1), None, ALU.add))
                dve.tensor_scalar(pad_idx[:, :], pad_f[:, :], first_row, None, ALU.add).then_inc(padded, 1)
                dve.memset(filled[:, :], 0.0)
                chained(dve.tensor_copy(need_i[:, :], gap[:, :]))
                chained(dve.tensor_scalar(need_i[:, :], need_i[:, :], 7, None, ALU.arith_shift_right))
                chained(dve.tensor_copy(need[:, :], need_i[:, :]))
                dve.tensor_scalar(gap[:, :], need[:, :], -float(P), float(REGION), ALU.mult, ALU.add)
                chained(dve.tensor_copy(start[:, 0, :], need[one, :]))
                src = 0
                for n, dist in enumerate((1, 2, 4)):
                    dst = n + 1 if n < 2 else 0
                    dve.tensor_copy(start[:, dst, 0:dist], start[:, src, 0:dist])
                    chained(dve.tensor_tensor(start[:, dst, dist:E], start[:, src, dist:E],
                                              start[:, src, 0:E - dist], ALU.add))
                    src = dst
                dve.memset(shrink[:, img % 2, 0:1], first_row + 1)
                dve.tensor_copy(shrink[:, img % 2, 1:E], gap[:, 0:E - 1])
                upto_e = start[:, src, :].unsqueeze(1).broadcast_to([1, T_IMG, E])
                t_of = tile_id[:, :].unsqueeze(2).broadcast_to([1, T_IMG, E])
                chained(dve.tensor_tensor(beyond[:, :, :], t_of, upto_e, ALU.is_ge))
                own = ids[:, OUT_LAG + img * T_IMG:OUT_LAG + (img + 1) * T_IMG]
                dve.tensor_reduce(own, beyond[:, :, 0:E - 1], AX_X, ALU.add)
                chained(dve.tensor_tensor(scratch[:, :, :], beyond[:, :, :],
                                          gap[one, :].unsqueeze(1).broadcast_to([1, T_IMG, E]), ALU.mult))
                dve.tensor_reduce(rows_f[:, 0, :], scratch[:, :, 0:E - 1], AX_X, ALU.add)
                chained(dve.tensor_scalar(rows_f[:, 1, :], beyond[:, :, E - 1], -1.0, 1.0, ALU.mult, ALU.add))
                chained(dve.scalar_tensor_tensor(rows_f[:, 2, :], tile_id[:, :], float(P), rows_f[:, 0, :],
                                                 ALU.mult, ALU.add))
                chained(dve.tensor_tensor(rows_f[:, 2, :], rows_f[:, 2, :], rows_f[:, 1, :], ALU.mult))
                at = slice(img * T_IMG, (img + 1) * T_IMG)
                dve.tensor_scalar(row_in[:, at], rows_f[:, 2, :], first_row, None, ALU.add)
                for w in range(2):
                    for j in range(IMG_CHUNKS + 1):
                        a = img * T_IMG + j * T_STEP + E * w
                        last = dve.tensor_tensor(packing[:, w, j, :], ids[:, a:a + E], octal[:, :], ALU.mult)
                chained(last)
                chained(dve.tensor_reduce(words_f[:, :, :], packing[:, :, :, :], AX_X, ALU.add))
                n = img * IMG_CHUNKS
                dve.tensor_copy(words[:, :, n:n + IMG_CHUNKS + 1], words_f[:, :, :]).then_inc(table_ready, 1)
                torder.end()

            def fronted(j, ins):
                ins.then_inc(front_order, 1)
                dve.wait_ge(front_order, forder.next(j))

            def backed(i, ins):
                ins.then_inc(back_order, 1)
                dve.wait_ge(back_order, border.next(i))

            def norm_stats(nth, j, par, ordered):
                for u in range(SUBS):
                    last = dve.bn_stats(stats[:, u, :], res[:, par, u, :])
                ordered(j, last)
                dve.sem_inc(dve_gate, 1)
                for u in range(SUBS):
                    last = dve.bn_aggr(mv[:, u, :], stats[:, u, :])
                ordered(j, last)
                dve.tensor_scalar(var[:, :], mv[:, :, 1], LN_EPS, None, ALU.add).then_inc(var_ready[nth], 1)

            def normalize(nth, j, par, dst, done):
                dve.wait_ge(rs_ready[nth], j + 1)
                for u in range(SUBS):
                    last = dve.tensor_scalar(dst(u), res[:, par, u, :], mv[:, u, 0:1], rs[:, u:u + 1],
                                             ALU.subtract, ALU.mult)
                last.then_inc(done, 1)

            def keep_residual(j, par):
                forder.begin()
                dve.wait_ge(x_turned, j + 1)
                at_least(dve, first_ready, j - 1)
                fronted(j, dve.tensor_copy(res[:, par, :, :].rearrange("p u c -> p (u c)"), fa_all))
                norm_stats(0, j, par, fronted)
                forder.end()

            def first_norm(j, par):
                normalize(0, j, par, lambda u: nrm[:, u, :], n1_ready)

            def keep_k(j):
                dve.wait_ge(k_ready, j + 1)
                for n in range(HG):
                    rows = slice(HD * n, HD * (n + 1))
                    last = dve.tensor_scalar(kdiag[rows, 1, n, :], fa[rows, 1, :], bqk[rows, 3:4], None, ALU.add)
                last.then_inc(k_kept_dve, 1)

            def keep_v(j):
                dve.wait_ge(v_ready, j + 1)
                for h in range(2):
                    rows = slice(64 * h, 64 * h + 64)
                    for bank in range(2):
                        ws = slice(4 * bank, 4 * bank + 4)
                        last = dve.tensor_tensor(
                            vdiag[rows, ws, :, HD * h:HD * h + HD],
                            fa[rows, bank, :].rearrange("p (w g d) -> p w g d", w=4, d=HD),
                            bv[rows, :].rearrange("p (g d) -> p g d", d=HD).unsqueeze(1)
                            .broadcast_to([64, 4, PAIRS, HD]), ALU.add)
                last.then_inc(v_kept, 1)

            keep_residual(0, 0)
            first_norm(0, 0)
            keep_k(0)
            keep_v(0)

            GROUP = 2 * HEADS

            def grid(v):
                return prob[:, 2 * v:2 * v + 2, :].rearrange("p u (h k) -> p (u h) k", k=WIN)

            def wide(a, v):
                return a[:, v * GROUP:(v + 1) * GROUP].unsqueeze(2).broadcast_to([P, GROUP, WIN])

            def shift(i, v):
                last_step = isinstance(i, int) and i % IMG_CHUNKS == IMG_CHUNKS - 1
                for u in (2 * v, 2 * v + 1):
                    dve.wait_ge(scored, i * SUBS + u + 1)
                    table = bias[:, int(last_step and u == SUBS - 1), :]
                    ins = dve.scalar_tensor_tensor(prob[:, u, :], ga[:, u % 2, :], SCALE, table, ALU.mult, ALU.add)
                backed(i, ins)
                backed(i, dve.tensor_reduce(top[:, v * GROUP:(v + 1) * GROUP], grid(v), AX_X, ALU.max))
                dve.tensor_tensor(grid(v), grid(v), wide(top, v), ALU.subtract).then_inc(shifted, 1)

            def divide(i, v):
                half = slice(v * GROUP, (v + 1) * GROUP)
                dve.wait_ge(exped, 2 * i + v + 1)
                backed(i, dve.tensor_reduce(total[:, half], grid(v), AX_X, ALU.add))
                backed(i, dve.reciprocal(inverse[:, half], total[:, half]))
                dve.tensor_tensor(grid(v), grid(v), wide(inverse, v), ALU.mult).then_inc(probs_ready, 1)

            def second_norm(i, par):
                dve.wait_ge(projected, i + 1)
                dve.wait_ge(bo_added, i + 1)
                flat = res[:, par, :, :].rearrange("p u c -> p (u c)")
                backed(i, dve.tensor_tensor(flat, ga_all, flat, ALU.add))
                norm_stats(1, i, par, backed)

            def route(i):
                dve.wait_ge(routed, i + 1)
                logits = pf[:, 128:128 + SUBS * E].rearrange("p (u e) -> p u e", e=E)

                def over_e(a):
                    return a[:, :].unsqueeze(2).broadcast_to([P, SUBS, E])

                backed(i, dve.tensor_reduce(rmax[:, :], logits, AX_X, ALU.max))
                dve.tensor_tensor(rexp[:, :, :], logits, over_e(rmax), ALU.subtract).then_inc(route_in, 1)
                dve.wait_ge(route_exp, i + 1)
                backed(i, dve.tensor_reduce(rsum[:, :], rexp[:, :, :], AX_X, ALU.add))
                backed(i, dve.reciprocal(rsum[:, :], rsum[:, :]))
                backed(i, dve.tensor_tensor(rprob[:, :, :], rexp[:, :, :], over_e(rsum), ALU.mult))
                mine = rprob[:, :, :].unsqueeze(3).broadcast_to([P, SUBS, E, E])
                other = rprob[:, :, :].unsqueeze(2).broadcast_to([P, SUBS, E, E])
                before_ = lower[:, :].rearrange("p (e f) -> p e f", f=E).unsqueeze(1).broadcast_to([P, SUBS, E, E])
                backed(i, dve.tensor_tensor(same[:, :, :, :], other, mine, ALU.is_equal))
                dve.tensor_tensor(more[:, :, :, :], other, mine, ALU.is_gt)
                backed(i, dve.tensor_tensor(same[:, :, :, :], same[:, :, :, :], before_, ALU.mult))
                backed(i, dve.tensor_tensor(more[:, :, :, :], more[:, :, :, :], same[:, :, :, :], ALU.add))
                backed(i, dve.tensor_reduce(rank[:, :, :], more[:, :, :, :], AX_X, ALU.add))
                backed(i, dve.tensor_scalar(sel[:, :, :], rank[:, :, :], 1.5, None, ALU.is_lt))
                backed(i, dve.tensor_tensor(chosen[:, :, :], sel[:, :, :], rprob[:, :, :], ALU.mult))
                backed(i, dve.tensor_reduce(rsum[:, :], chosen[:, :, :], AX_X, ALU.add))
                backed(i, dve.tensor_scalar(rsum[:, :], rsum[:, :], 1e-12, None, ALU.max))
                backed(i, dve.reciprocal(rsum[:, :], rsum[:, :]))
                dve.tensor_tensor(comb[:, :, :], chosen[:, :, :], over_e(rsum), ALU.mult).then_inc(comb_ready, 1)
                border.end()

            def step(i, par, img):
                att, exp, com = stages(img)
                front = att and has_front(i)
                m, c = i - IMG_CHUNKS, i - 2 * IMG_CHUNKS
                if att:
                    border.begin()
                    shift(i, 0)
                if front:
                    keep_residual(i + 1, 1 - par)
                if (att and not (isinstance(i, int) and i == 0)) or (isinstance(i, int) and i == STEPS):
                    new_image = isinstance(i, int) and i % IMG_CHUNKS == 0
                    places(i - 1, 1 - par, img - 1 if new_image else img)
                    if new_image:
                        tile_table(img - 1)
                if com:
                    which = c if isinstance(c, int) else upto(c, STEPS - 1)
                    dve.tensor_copy(cgate[:, par, :], gate_hist[:, which, :])
                    mine = (P, TOP_K * SUBS, E)
                    ins = dve.tensor_tensor(region_of[:, :, :], row_hist[:, which, :].unsqueeze(2).broadcast_to(mine),
                                            region[:, img % 2, :].unsqueeze(1).broadcast_to(mine), ALU.is_ge)
                    ins.then_inc(cidx_order, 1)
                    dve.wait_ge(cidx_order, 3 * c + 1)
                    dve.tensor_tensor(region_of[:, :, :], region_of[:, :, :],
                                      shrink[:, img % 2, :].unsqueeze(1).broadcast_to(mine), ALU.mult)\
                       .then_inc(cidx_order, 1)
                    dve.wait_ge(cidx_order, 3 * c + 2)
                    dve.tensor_reduce(shift_by[:, :], region_of[:, :, :], AX_X, ALU.add).then_inc(cidx_order, 1)
                    dve.wait_ge(cidx_order, 3 * c + 3)
                    dve.tensor_tensor(cidx[:, par, :], row_hist[:, which, :], shift_by[:, :], ALU.subtract)\
                       .then_inc(cidx_ready, 1)
                who = None
                if exp:
                    if isinstance(m, int) and m % IMG_CHUNKS == 0:
                        dve.wait_ge(table_ready, img)
                        dve.sem_inc(dve_gate, 1)
                    who = expert_of(dve, m)

                def slot(t):
                    if exp:
                        expert_slot(m, t, par, who)

                slot(0)
                if att:
                    shift(i, 1)
                if front:
                    first_norm(i + 1, 1 - par)
                slot(1)
                if att:
                    divide(i, 0)
                slot(2)
                if att:
                    divide(i, 1)
                slot(3)
                slot(4)
                if com:
                    dve.wait_ge(acc_in, (c + 1) * 16)
                    for u in range(SUBS):
                        dve.wait_ge(got_in[u], (c + 1) * 32)
                        dve.scalar_tensor_tensor(acc[:, u, :], got[:, 0, u, :], cgate[:, par, u:u + 1], acc[:, u, :],
                                                 ALU.mult, ALU.add).then_inc(acc_half, 1)
                    for u in range(SUBS):
                        dve.wait_ge(acc_half, c * SUBS + u + 1)
                        dve.scalar_tensor_tensor(acc[:, u, :], got[:, 1, u, :], cgate[:, par, SUBS + u:SUBS + u + 1],
                                                 acc[:, u, :], ALU.mult, ALU.add).then_inc(acc_done, 1)
                slot(5)
                if front:
                    keep_k(i + 1)
                slot(6)
                if att:
                    second_norm(i, par)
                if front:
                    keep_v(i + 1)
                slot(7)
                if att:
                    at_least(dve, scattered[par], half_of(i) * SCATTER)
                    normalize(1, i, par, lambda u: tok[:, par, u, :], n2_ready)
                slot(8)
                if att:
                    route(i)

            def flush():
                who = expert_of(dve, STEPS)
                for t in range(OUT_LAG):
                    expert_slot(STEPS, t, 0, who)

            steps(dve, step, flush)

        @block.tensor
        def _(pe):
            pe.wait_ge(weights_in, 16 * WEIGHTS)
            pe.matmul(ga[:, 0, :], flip, rel, start=True, stop=True).then_inc(bias_turned, 1)
            pe.wait_ge(tables, TABLES)
            pe.wait_ge(experts_in, 16 * EXPERTS)

            def turn(dst, src):
                return pe.matmul(dst, src, ident[:, :], is_transpose=True, start=True, stop=True)

            def expert_slot(m, t, par, who):
                g = tile(m, t, 0)
                if g is not None:
                    pe.wait_ge(xs_in[t % RING], (m * (T_STEP // RING) + t // RING + 1) * 16)
                    at_least(pe, xs_kept, g)
                    at_least(pe, hid_kept, g - TURN_LAG)
                    for h in range(HALVES):
                        last = turn(pt[:, 0, h, :], xs[:, t % RING, h * P:(h + 1) * P])
                    last.then_inc(xs_turned, 1)
                g = tile(m, t, HID_LAG)
                if g is not None:
                    at = (par + t + 1) % 2
                    pe.wait_ge(xs_kept, g + 1)
                    at_least(pe, hid_biased, g)
                    for h in range(HALVES):
                        last = pe.matmul(ph[:, 0:C], xs_t[:, at, h, :], w1[:, h, who(t, HID_LAG), :],
                                         start=(h == 0), stop=(h == HALVES - 1))
                    last.then_inc(hid_ready, 1)
                g = tile(m, t, TURN_LAG)
                if g is not None:
                    pe.wait_ge(hid_done, g + 1)
                    if tile(m, t, 0) is not None:
                        pe.wait_ge(xs_kept, g + TURN_LAG + 1)
                    at_least(pe, hid_kept, g)
                    for f in range(HALVES):
                        last = turn(pt[:, 1, f, :], hid[:, (par + t) % 2, f * P:(f + 1) * P])
                    last.then_inc(hid_turned, 1)
                g = tile(m, t, OUT_LAG)
                if g is not None:
                    at = (par + t + 1) % 2
                    pe.wait_ge(hid_kept, g + 1)
                    at_least(pe, y_kept, g)
                    for f in range(HALVES):
                        last = pe.matmul(py[:, 0:C], hid_t[:, at, f, :], w2[:, f, who(t, OUT_LAG), :],
                                         start=(f == 0), stop=(f == HALVES - 1))
                    last.then_inc(y_ready, 1)

            def turn_x(j, par):
                pe.wait_ge(summed, j + 1)
                at_least(pe, v_kept, j)
                for u in range(SUBS):
                    for h in range(HALVES):
                        at = (2 * (u % 2) + h) * P
                        last = turn(fa[:, u // 2, at:at + P], xl[:, par, h, u * P:(u + 1) * P])
                last.then_inc(x_turned, 1)

            def turn_normed(j):
                pe.wait_ge(n1_ready, j + 1)
                for h in range(HALVES):
                    for u in range(SUBS):
                        last = turn(fa[:, h, u * P:(u + 1) * P], nrm[:, u, h * P:(h + 1) * P])
                last.then_inc(n1_turned, 1)

            def make_qk(first_n, ready):
                for n in (0, 1):
                    cols = slice((first_n + n) * P, (first_n + n + 1) * P)
                    for h in range(HALVES):
                        last = pe.matmul(fa[:, n, :], wqk[:, h, cols], nrm_t[:, h, :],
                                         start=(h == 0), stop=(h == HALVES - 1))
                last.then_inc(ready, 1)

            def make_q(j):
                pe.wait_ge(n1_kept, j + 1)
                make_qk(0, q_ready)

            def make_k(j):
                pe.wait_ge(q_kept, j + 1)
                make_qk(2, k_ready)

            def make_v(j):
                pe.wait_ge(k_kept_act, j + 1)
                pe.wait_ge(k_kept_dve, j + 1)
                for w in range(WINS):
                    for parity in range(2):
                        for h in range(HALVES):
                            last = pe.matmul(fa[64 * parity:64 * parity + 64, w // 4, (w % 4) * P:(w % 4 + 1) * P],
                                             nrm_t[:, h, w * WIN:(w + 1) * WIN], wv[:, h, parity, :],
                                             start=(h == 0), stop=(h == HALVES - 1))
                last.then_inc(v_ready, 1)

            def score(i, v):
                for u in (2 * v, 2 * v + 1):
                    for side in range(2):
                        cols = slice((2 * u + side) * WIN, (2 * u + side + 1) * WIN)
                        for g in range(HALVES):
                            last = pe.matmul(ga[64 * side:64 * side + 64, u % 2, g * 256:g * 256 + 256],
                                             qt[:, g, cols], kdiag[:, g, :, cols], start=True, stop=True)
                    last.then_inc(scored, 1)

            def turn_probs(i, v):
                pe.wait_ge(probs_ready, 2 * i + v + 1)
                for u in (2 * v, 2 * v + 1):
                    for g in range(PAIRS):
                        last = turn(ga[:, u % 2, g * P:(g + 1) * P], prob[:, u, g * P:(g + 1) * P])
                    last.then_inc(p_turned, 1)

            turn_x(0, 0)
            turn_normed(0)
            make_q(0)
            make_k(0)
            make_v(0)

            def step(i, par, img):
                att, exp, com = stages(img)
                front = att and has_front(i)
                m, c = i - IMG_CHUNKS, i - 2 * IMG_CHUNKS
                if att:
                    pe.wait_ge(k_kept_act, i + 1)
                    pe.wait_ge(k_kept_dve, i + 1)
                    at_least(pe, n2_kept, i)
                    score(i, 0)
                if front:
                    turn_x(i + 1, 1 - par)
                if (att and not (isinstance(i, int) and i == 0)) or (isinstance(i, int) and i == STEPS):
                    pe.wait_ge(comb_ready, i)
                    chosen_by = sel[:, :, :].rearrange("p u e -> p (u e)")
                    pe.matmul(pf[:, 0:SUBS * E], strict[:, :], chosen_by, start=True, stop=False)
                    for u in range(1, SUBS):
                        pe.matmul(pf[:, u * E:SUBS * E], ones[:, :], chosen_by[:, 0:(SUBS - u) * E],
                                  start=False, stop=(u == SUBS - 1))
                    for u in range(SUBS):
                        last = pe.matmul(pf[:, 64:64 + E], ones[:, :], sel[:, u, :], start=(u == 0), stop=(u == SUBS - 1))
                    last.then_inc(ranked, 1)
                who = None
                if exp:
                    if isinstance(m, int) and m % IMG_CHUNKS == 0:
                        pe.wait_ge(table_ready, img)
                        pe.sem_inc(pe_gate, 1)
                    who = expert_of(pe, m)

                def slot(t):
                    if exp:
                        expert_slot(m, t, par, who)

                slot(0)
                if att:
                    pe.wait_ge(shifted, 2 * i + 1)
                    score(i, 1)
                slot(1)
                slot(2)
                if att:
                    pe.wait_ge(shifted, 2 * i + 2)
                    turn_probs(i, 0)
                if front:
                    turn_normed(i + 1)
                slot(3)
                if att:
                    pe.wait_ge(p_kept, i * SUBS + 2)
                    turn_probs(i, 1)
                if front:
                    make_q(i + 1)
                slot(4)
                if att:
                    pe.wait_ge(p_kept, (i + 1) * SUBS)
                    pe.wait_ge(v_kept, i + 1)
                    for w in range(WINS):
                        for g in range(PAIRS):
                            at = g * P + (w % 2) * WIN
                            rows = slice(64 * (g % 2), 64 * (g % 2) + 64)
                            last = pe.matmul(ga[rows, g // 2, w * WIN:(w + 1) * WIN], vdiag[:, w, g, :],
                                             prob_t[:, w // 2, at:at + WIN], start=True, stop=True)
                    last.then_inc(mixed_v, 1)
                if front:
                    make_k(i + 1)
                slot(5)
                if att:
                    pe.wait_ge(att_kept, i + 1)
                    for u in range(SUBS):
                        for h in range(HALVES):
                            last = pe.matmul(ga[:, u // 2, (u % 2) * C:(u % 2) * C + C],
                                             att_t[:, h, u * P:(u + 1) * P], wo[:, h, :],
                                             start=(h == 0), stop=(h == HALVES - 1))
                    last.then_inc(projected, 1)
                slot(6)
                if front:
                    make_v(i + 1)
                slot(7)
                if com:
                    for v in range(2):
                        pe.wait_ge(acc_done, c * SUBS + 2 * v + 2)
                        at_least(pe, out_kept, c * 2 + v)
                        if att or (isinstance(i, int) and i == STEPS):
                            at_least(pe, placed, i)
                        for h in range(HALVES):
                            for u in (2 * v, 2 * v + 1):
                                at = h * 256 + (u % 2) * P
                                last = turn(pf[:, at:at + P], acc[:, u, h * P:(h + 1) * P])
                        last.then_inc(out_turned, 1)
                if att:
                    pe.wait_ge(n2_ready, i + 1)
                    for h in range(HALVES):
                        for u in range(SUBS):
                            last = turn(ga[:, h, u * P:(u + 1) * P], tok[:, par, u, h * P:(h + 1) * P])
                    last.then_inc(n2_turned, 1)
                slot(8)
                if att:
                    pe.wait_ge(n2_kept, i + 1)
                    if com:
                        pe.wait_ge(out_kept, (c + 1) * 2)
                    for u in range(SUBS):
                        for h in range(HALVES):
                            last = pe.matmul(pf[:, 128 + u * E:128 + (u + 1) * E], tok_t[:, h, u * P:(u + 1) * P],
                                             wr[:, h, :], start=(h == 0), stop=(h == HALVES - 1))
                    last.then_inc(routed, 1)

            def flush():
                who = expert_of(pe, STEPS)
                for t in range(OUT_LAG):
                    expert_slot(STEPS, t, 0, who)

            steps(pe, step, flush)


def keep_buffers(nc, ctx):
    return {
        "ident": ctx.enter_context(nc.sbuf_tensor("ident", [P, P], F32)),
        "bn_scale": ctx.enter_context(nc.sbuf_tensor("bn_scale", [P, HALVES], F32)),
        "bn_shift": ctx.enter_context(nc.sbuf_tensor("bn_shift", [P, HALVES], F32)),
    }


def gather_buffers(nc, ctx):
    return {
        "idx_all": ctx.enter_context(nc.sbuf_tensor("idx_all", [P, B, 2, 4, PXT, TAPS], I32)),
        "wts_all": ctx.enter_context(nc.sbuf_tensor("wts_all", [P, B, 2, 4, PXT, TAPS, CORNERS], F32)),
    }


def constants():
    import numpy as np

    chan = np.arange(P)
    group = (chan[:, None] // (C // 32) == chan[None, :] // (C // 32)).astype(np.float32) / (C // 32)
    p, r, q, j, t = np.ogrid[0:P, 0:2, 0:PXT, 0:4, 0:TAPS]
    base = np.zeros((P, 2, PXT, 4, TAPS, 2), np.float32)
    base[..., 0] = 2 * (16 * r + 4 * j + q) + p // W + t // 3 - 1
    base[..., 1] = p % W + t % 3 - 1 + 0 * (r + q + j)
    here = np.zeros((P, HEADS, WIN), np.float32)
    first = np.arange(P)[:, None] % WIN < SHIFT
    apart = (first != (np.arange(WIN)[None, :] < SHIFT)) & (np.arange(P)[:, None] >= WIN)
    here[:] = np.where(apart, np.float32(-1e30), np.float32(0))[:, None, :]
    flip = (np.arange(WIN)[:, None] == WIN - 1 - np.arange(P)[None, :] % WIN).astype(np.float32)
    lower = (np.arange(E)[None, :] < np.arange(E)[:, None]).astype(np.float32)
    region_rows, octal = N + P, 8 ** np.arange(E)
    e = np.arange(E)
    return {
        "strict_c": (np.arange(P)[:, None] < np.arange(P)[None, :]).astype(np.float32),
        "region_c": np.broadcast_to(np.concatenate([e * region_rows, (E + e) * region_rows]).astype(np.float32) + 1,
                                    (P, 2 * E)).copy(),
        "row_id_c": (e[None, :] * region_rows + np.arange(P)[:, None]).astype(np.float32),
        "octal_c": octal.astype(np.float32)[None, :],
        "tile_id_c": np.arange(EXPERT_TILES, dtype=np.float32)[None, :],
        "ident_c": np.eye(P, dtype=np.float32),
        "group_c": group,
        "base_c": base.reshape(P, -1),
        "flip_c": flip,
        "apart_c": here.reshape(P, -1),
        "lower_c": np.broadcast_to(lower.reshape(1, -1), (P, E * E)).copy(),
    }


def build(nc, d, out):
    with ExitStack() as ctx:
        table = nc.dram_tensor("table", (B * ENTRIES, CORNERS * C), F32, kind="Internal").ap()
        conv = nc.dram_tensor("conv_raw", (C, B * N), F32, kind="Internal").ap()
        keep = keep_buffers(nc, ctx)
        with ExitStack() as inner:
            both = {**keep, **gather_buffers(nc, inner)}
            sample_table_stage(nc, d["x"], d["w_off"], d["b_off"], table, both, d)
            conv_stage(nc, d["w_conv"], d["gamma"], d["beta"], table, conv, both)
        token_stage(nc, d["x"], conv, d, out, keep)


def laid_out(inputs):
    import numpy as np

    def a(name):
        return np.asarray(inputs[name])

    w_qkv, b_qkv = a("L1_attn_w_qkv"), a("L1_attn_b_qkv")
    even_odd = (PAIRS, 2, HD)
    d = {
        "x": a("x"),
        "w_off": a("L0_conv_w_off").reshape(OFFS, C, TAPS).transpose(1, 2, 0),
        "b_off": a("L0_conv_b_off"),
        "w_conv": a("L0_conv_w_conv").reshape(C, C, TAPS).transpose(1, 2, 0),
        "gamma": a("L0_conv_gamma"),
        "beta": a("L0_conv_beta"),
        "w_qk": w_qkv[:2 * C].T,
        "w_v": w_qkv[2 * C:].T.reshape(C, *even_odd).transpose(0, 2, 1, 3).reshape(C, C),
        "b_qk": b_qkv[:2 * C].reshape(4, P).T,
        "b_v": b_qkv[2 * C:].reshape(even_odd).transpose(1, 0, 2).reshape(2, P),
        "rel_rev": a("L1_attn_rel_pos")[:, ::-1],
        "w_out": a("L1_attn_w_out").T,
        "b_out": a("L1_attn_b_out"),
        "w_router": a("L1_ffn_router_w").T,
        "w_1": a("L1_ffn_w1"),
        "b_1": a("L1_ffn_b1").reshape(E * C),
        "w_2": a("L1_ffn_w2"),
        "b_2": a("L1_ffn_b2").reshape(E * C),
        **constants(),
    }
    return {name: np.ascontiguousarray(v) for name, v in d.items()}


def kernel(**inputs):
    import concourse.bacc as bacc
    from concourse.bass_utils import run_bass_kernel_spmd

    nc = bacc.Bacc("TRN2", target_bir_lowering=False, num_devices=1)
    arrays = laid_out(inputs)
    d = {name: nc.dram_tensor("in_" + name, v.shape, mybir.dt.from_np(v.dtype), kind="ExternalInput").ap()
         for name, v in arrays.items()}
    out = nc.dram_tensor("out", (B, C, H, W), F32, kind="ExternalOutput").ap()
    build(nc, d, out)
    r = run_bass_kernel_spmd(nc, [{"in_" + name: v for name, v in arrays.items()}], core_ids=[0])
    return r.results[0]["out"]
```

```python
from contextlib import ExitStack

import concourse.bass as bass
from concourse import mybir

F32 = mybir.dt.float32
I32 = mybir.dt.int32
ALU = mybir.AluOpType
ACT = mybir.ActivationFunctionType
AX_X = mybir.AxisListType.X

P = 128
B, C, H, W = 4, 256, 64, 64
HALVES = C // P
N = H * W
TAPS = 9
OFFS = 2 * TAPS
OPAD = 32
PADW = W + 2
ENTRIES = PADW * PADW
CORNERS = 4
CHUNK = 512
IMG_CHUNKS = N // CHUNK
TILES = B * IMG_CHUNKS
PXT = CHUNK // P
GN_EPS, BN_EPS, LN_EPS = 1e-5, 1e-5, 1e-5

HEADS, HD, WIN = 8, 32, 64
WINS = CHUNK // WIN
SHIFT = WIN // 2
SCALE = float(HD) ** -0.5
E = 8
HG = 4
PAIRS = HEADS // 2
TOP_K = 2
STEP_TILES = -(-(TOP_K * N + E * (P - 1)) // (P * IMG_CHUNKS))
EXPERT_TILES = STEP_TILES * IMG_CHUNKS


def upto(value, top):
    return value if isinstance(value, int) else value.with_bounds(min_val=0, max_val=top)


def at_least(eng, semaphore, value):
    if not isinstance(value, int) or value > 0:
        eng.wait_ge(semaphore, value)


class Tally:

    def __init__(self, per):
        self.per, self.n = per, 0

    def begin(self):
        self.n = 0

    def next(self, i):
        self.n += 1
        return i * self.per + self.n

    def end(self):
        assert self.n == self.per, (self.n, self.per)


def sample_table_stage(nc, x, w_off, b_off, table, keep, const):
    ident, idx_all, wts_all = keep["ident"], keep["idx_all"], keep["wts_all"]
    GROUP_TILES = 8
    GROUPS = N // P // GROUP_TILES
    ROUNDS = 2
    STATS = N // CHUNK
    x_v = x.rearrange("b (h p) y x -> b p h (y x)", p=P)
    table_v = table.rearrange("(b y x) (s c) -> b y x s c", b=B, y=PADW, s=CORNERS)

    with ExitStack() as ctx:
        def sb(name, shape, dt=F32):
            return ctx.enter_context(nc.sbuf_tensor(name, shape, dt))

        def ps(name, shape):
            return ctx.enter_context(nc.psum_tensor(name, shape, F32))

        def sem(name):
            return ctx.enter_context(nc.semaphore(name))

        raw = sb("raw", [P, 2, HALVES, N])
        padded = sb("padded", [P, HALVES, PADW, PADW])
        tok = sb("tok", [P, 2, GROUP_TILES, C])
        zero = sb("zero", [P, CORNERS * C])
        group = sb("group", [P, P])
        base = sb("base", [P, ROUNDS, PXT, 4, OFFS])
        woff = sb("woff", [P, HALVES, TAPS, OPAD])
        boff = sb("boff", [P, 1])
        stats = sb("stats", [P, HALVES, STATS, 6])
        mv = sb("mv", [P, HALVES, 2])
        gmean = sb("gmean", [P, HALVES])
        dev = sb("dev", [P, HALVES])
        spread = sb("spread", [P, HALVES])
        gvar = sb("gvar", [P, HALVES])
        grs = sb("grs", [P, HALVES])
        power = sb("power", [P, HALVES])
        off = sb("off", [P, ROUNDS, CHUNK])
        image_base = sb("image_base", [P, 1])
        pos = sb("pos", [P, PXT, 4, OFFS])
        whole_i = sb("whole_i", [P, PXT, 4, OFFS], I32)
        whole = sb("whole", [P, PXT, 4, OFFS])
        above = sb("above", [P, PXT, 4, OFFS])
        floor = sb("floor", [P, PXT, 4, OFFS])
        frac = sb("frac", [P, 2, PXT, 4, OFFS])
        entry = sb("entry", [P, PXT, 4, TAPS])

        ps_group = ps("ps_group", [P, 2, CHUNK])
        ps_tok = ps("ps_tok", [P, 2, CHUNK])
        ps_off = ps("ps_off", [P, 2, CHUNK])
        ps_pos = ps("ps_pos", [P, 2, CHUNK])

        const_in = sem("const_in")
        boff_zero = sem("boff_zero")
        boff_in = sem("boff_in")
        set_up = sem("set_up")
        base_set = sem("base_set")
        dve_gate, pool_gate, sp_gate = sem("dve_gate"), sem("pool_gate"), sem("sp_gate")
        border_out = sem("border_out")
        raw_in = [[sem(f"raw_in{i}{h}") for h in range(HALVES)] for i in range(2)]
        stat_order = sem("stat_order")
        means_ready = sem("means_ready")
        grouped = sem("grouped")
        var_ready = sem("var_ready")
        rs_ready = sem("rs_ready")
        normed = sem("normed")
        padded_ready = sem("padded_ready")
        turned = sem("turned")
        tok_ready = sem("tok_ready")
        table_out = [sem(f"table_out{i}") for i in range(2)]
        off_ready = sem("off_ready")
        off_kept = sem("off_kept")
        off_turned = sem("off_turned")
        pos_order = sem("pos_order")
        pos_taken = sem("pos_taken")
        block = ctx.enter_context(nc.Block())
        STAT_K, POS_K = 4, 21

        def images(eng, body):
            with eng.Fori(0, B // 2 - 1) as pair:
                body(pair, 0, 2)
                body(pair, 1, 2)
            body(B // 2 - 1, 0, 1)
            body(B // 2 - 1, 1, 0)

        @block.sync
        def _(sp):
            sp.dma_start(ident[:, :], const["ident_c"]).then_inc(const_in, 16)
            sp.dma_start(group[:, :], const["group_c"]).then_inc(const_in, 16)
            sp.dma_start(base[:, :, :, :, :].rearrange("p a b c d -> p (a b c d)"),
                         const["base_c"]).then_inc(const_in, 16)
            for h in range(HALVES):
                sp.dma_start(woff[:, h, :, 0:OFFS], w_off[h * P:(h + 1) * P, :, :]).then_inc(const_in, 16)
                sp.dma_start(raw[:, 0, h, :], x_v[0, :, h, :]).then_inc(raw_in[0][h], 16)
            for h in range(HALVES):
                sp.dma_start(raw[:, 1, h, :], x_v[1, :, h, :]).then_inc(raw_in[1][h], 16)
            sp.wait_ge(boff_zero, 1)
            for j in range(4):
                sp.dma_start(boff[OPAD * j:OPAD * j + OFFS, :],
                             b_off.rearrange("(o a) -> o a", a=1)).then_inc(boff_in, 16)
            sp.wait_ge(set_up, 2)
            rows = ((PADW - 1, 0, 4), (0, 0, 2), (PADW - 2, 2, 4))
            tv = table_v.rearrange("b y x s c -> b y x (s c)")
            for y, s0, s1 in rows:
                for b in range(B):
                    sp.dma_start(tv[b, y, :, s0 * C:s1 * C],
                                 zero[0:PADW, 0:(s1 - s0) * C]).then_inc(border_out, 16)
            for dy in range(2):
                y0 = 1 - dy
                for xx, s0, s1 in ((PADW - 1, 2 * dy, 2 * dy + 2), (0, 2 * dy, 2 * dy + 1),
                                   (PADW - 2, 2 * dy + 1, 2 * dy + 2)):
                    for b in range(B):
                        sp.dma_start(tv[b, y0:y0 + H, xx, s0 * C:s1 * C],
                                     zero[0:H, 0:(s1 - s0) * C]).then_inc(border_out, 16)

            def write_image(pair, par, more):
                b = pair * 2 + par
                image = b if isinstance(b, int) else sp.snap(upto(b, B - 1))
                for g in range(GROUPS):
                    sp.wait_ge(tok_ready, b * (GROUPS * 4) + 4 * (g + 1))
                    sp.sem_inc(sp_gate, 1)
                    for r in range(2):
                        for s in range(CORNERS):
                            dy, dx = s // 2, s % 2
                            y0 = 2 * GROUP_TILES * g + r - dy + 1
                            sp.dma_start(
                                table_v[image, y0:y0 + 2 * GROUP_TILES - 1:2, 1 - dx:1 - dx + W, s, :]
                                .rearrange("y x c -> x y c"),
                                tok[W * r:W * r + W, g % 2, :, :]).then_inc(table_out[g % 2], 16)
                if more == 2:
                    sp.wait_ge(turned, b * 16 + 16)
                    sp.wait_ge(padded_ready, b * HALVES + HALVES)
                    sp.sem_inc(sp_gate, 1)
                    behind = b + 2 if isinstance(b, int) else sp.snap(upto(b + 2, B - 1))
                    for h in range(HALVES):
                        sp.dma_start(raw[:, par, h, :], x_v[behind, :, h, :]).then_inc(raw_in[par][h], 16)

            images(sp, write_image)
            for i in range(2):
                sp.wait_ge(table_out[i], 16 * 8 * 2 * B)
            sp.wait_ge(border_out, 16 * 9 * B)
            sp.wait_ge(boff_in, 64)

        @block.gpsimd
        def _(pool):
            pool.memset(boff[:, :], 0.0).then_inc(boff_zero, 1)
            pool.memset(power[:, :], -0.5).then_inc(set_up, 1)
            pool.memset(zero[:, :], 0.0).then_inc(set_up, 1)
            pool.memset(woff[:, :, :, OFFS:OPAD], 0.0).then_inc(set_up, 1)
            pool.memset(padded[:, :, :, :], 0.0).then_inc(set_up, 1)
            pool.wait_ge(set_up, 4)

            def inverse_root(b):
                pool.wait_ge(var_ready, b + 1)
                pool.tensor_tensor(grs[:, :], gvar[:, :], power[:, :], ALU.pow).then_inc(rs_ready, 1)

            def pad_image(pair, par, more):
                b = pair * 2 + par
                at_least(pool, off_ready, b * 2)
                for h in range(HALVES):
                    pool.wait_ge(normed, b * 2 + h + 1)
                    pool.sem_inc(pool_gate, 1)
                    pool.tensor_copy(padded[:, h, 1:H + 1, 1:W + 1],
                                     raw[:, par, h, :].rearrange("p (y x) -> p y x", x=W)).then_inc(padded_ready, 1)
                if more:
                    inverse_root(b + 1)

            inverse_root(0)
            images(pool, pad_image)

        @block.vector
        def _(dve):
            st, po = Tally(STAT_K), Tally(POS_K)
            dve.memset(image_base[:, :], float(PADW + 1 - ENTRIES)).then_inc(base_set, 1)
            dve.wait_ge(base_set, 1)
            dve.wait_ge(const_in, 80)

            def normalize(pair, par):
                b = pair * 2 + par
                st.begin()
                for h in range(HALVES):
                    dve.wait_ge(raw_in[par][h], (pair + 1) * 16)
                    for c in range(STATS):
                        last = dve.bn_stats(stats[:, h, c, :], raw[:, par, h, c * CHUNK:(c + 1) * CHUNK])
                last.then_inc(stat_order, 1)
                dve.wait_ge(stat_order, st.next(b))
                dve.sem_inc(dve_gate, 1)
                for h in range(HALVES):
                    last = dve.bn_aggr(mv[:, h, :], stats[:, h, :, :].rearrange("p a b -> p (a b)"))
                last.then_inc(means_ready, 1)
                dve.wait_ge(grouped, b * 2 + 1)
                dve.tensor_copy(gmean[:, :], ps_group[:, 0, 0:HALVES]).then_inc(stat_order, 1)
                dve.wait_ge(means_ready, b * 2 + 1)
                dve.wait_ge(stat_order, st.next(b))
                dve.tensor_tensor(dev[:, :], mv[:, :, 0], gmean[:, :], ALU.subtract).then_inc(stat_order, 1)
                dve.wait_ge(stat_order, st.next(b))
                dve.tensor_tensor(dev[:, :], dev[:, :], dev[:, :], ALU.mult).then_inc(stat_order, 1)
                dve.wait_ge(stat_order, st.next(b))
                dve.tensor_tensor(spread[:, :], dev[:, :], mv[:, :, 1], ALU.add).then_inc(means_ready, 1)
                dve.wait_ge(grouped, b * 2 + 2)
                dve.tensor_scalar(gvar[:, :], ps_group[:, 1, 0:HALVES], GN_EPS, None, ALU.add).then_inc(var_ready, 1)
                dve.wait_ge(rs_ready, b + 1)
                for h in range(HALVES):
                    dve.tensor_scalar(raw[:, par, h, :], raw[:, par, h, :], gmean[:, h:h + 1], grs[:, h:h + 1],
                                      ALU.subtract, ALU.mult).then_inc(normed, 1)
                st.end()

            def place_samples(pair, par, more):
                b = pair * 2 + par
                if more:
                    normalize(pair + par, 1 - par)
                po.begin()
                image = upto(b, B - 1)

                def chained(ins):
                    ins.then_inc(pos_order, 1)
                    dve.wait_ge(pos_order, po.next(b))

                chained(dve.tensor_scalar(image_base[:, :], image_base[:, :], float(ENTRIES), None, ALU.add))
                for r in range(ROUNDS):
                    here = ps_pos[:, r, :].rearrange("p (q j o) -> p q j o", q=PXT, j=4)[:, :, :, 0:OFFS]
                    dve.wait_ge(off_turned, b * 2 + r + 1)

                    dve.tensor_tensor(pos[:, :, :, :], here, base[:, r, :, :, :], ALU.add).then_inc(pos_taken, 1)
                    dve.wait_ge(pos_taken, b * 2 + r + 1)
                    chained(dve.tensor_scalar(pos[:, :, :, :], pos[:, :, :, :], -1.0, float(H),
                                              ALU.max, ALU.min))
                    chained(dve.tensor_copy(whole_i[:, :, :, :], pos[:, :, :, :]))
                    chained(dve.tensor_copy(whole[:, :, :, :], whole_i[:, :, :, :]))
                    chained(dve.tensor_tensor(above[:, :, :, :], whole[:, :, :, :], pos[:, :, :, :], ALU.is_gt))
                    chained(dve.tensor_tensor(floor[:, :, :, :], whole[:, :, :, :], above[:, :, :, :],
                                              ALU.subtract))
                    chained(dve.tensor_tensor(frac[:, 1, :, :, :], pos[:, :, :, :], floor[:, :, :, :],
                                              ALU.subtract))
                    chained(dve.tensor_scalar(frac[:, 0, :, :, :], frac[:, 1, :, :, :], -1.0, 1.0,
                                              ALU.mult, ALU.add))
                    f = floor[:, :, :, :].rearrange("p q j (t a) -> p q j t a", a=2)
                    for j in range(4):
                        last = dve.scalar_tensor_tensor(entry[:, :, j, :], f[:, :, j, :, 0], float(PADW),
                                                        f[:, :, j, :, 1], ALU.mult, ALU.add)
                    chained(last)
                    chained(dve.tensor_scalar(
                        idx_all[:, image, r, :, :, :].rearrange("p j q t -> p q j t"),
                        entry[:, :, :, :], image_base[:, 0:1], None, ALU.add))
                    fr = frac[:, :, :, :, :].rearrange("p n q j (t a) -> p n q j t a", a=2)
                    for s in range(CORNERS):
                        dy, dx = s // 2, s % 2
                        for j in range(4):
                            last = dve.tensor_tensor(wts_all[:, image, r, j, :, :, s],
                                                     fr[:, dy, :, j, :, 0], fr[:, dx, :, j, :, 1], ALU.mult)
                    chained(last)
                po.end()

            normalize(0, 0)
            images(dve, place_samples)

        @block.scalar
        def _(act):
            act.wait_ge(boff_in, 64)

            def copy_image(pair, par, more):
                b = pair * 2 + par
                for g in range(GROUPS):
                    at_least(act, table_out[g % 2], (b * 2 + g // 2) * 128)
                    for k in range(4):
                        n = 4 * g + k
                        act.wait_ge(turned, b * 16 + n + 1)
                        act.activation(tok[:, g % 2, 2 * k:2 * k + 2, :].rearrange("p t c -> p (t c)"),
                                       ps_tok[:, n % 2, :], ACT.Copy).then_inc(tok_ready, 1)
                for r in range(ROUNDS):
                    act.wait_ge(off_ready, b * 2 + r + 1)
                    act.activation(off[:, r, :], ps_off[:, r, :], ACT.Identity,
                                   bias=boff[:, 0:1]).then_inc(off_kept, 1)

            images(act, copy_image)

        @block.tensor
        def _(pe):
            pe.wait_ge(const_in, 80)
            pe.wait_ge(set_up, 4)

            def average(b):
                for k, src in enumerate((mv[:, :, 0], spread[:, :])):
                    pe.wait_ge(means_ready, b * 2 + k + 1)
                    pe.matmul(ps_group[:, k, 0:HALVES], group[:, :], src, start=True, stop=True).then_inc(grouped, 1)

            def image(pair, par, more):
                b = pair * 2 + par
                pe.wait_ge(normed, b * 2 + 2)
                for n in range(N // P // 2):
                    if n >= 2:
                        pe.wait_ge(tok_ready, b * 16 + n - 1)
                    else:
                        pe.wait_ge(tok_ready, b * 16)
                    for t in range(2):
                        px = P * (2 * n + t)
                        for h in range(HALVES):
                            at = (t * HALVES + h) * P
                            last = pe.matmul(ps_tok[:, n % 2, at:at + P], raw[:, par, h, px:px + P],
                                             ident[:, :], is_transpose=True, start=True, stop=True)
                    last.then_inc(turned, 1)
                if more:
                    average(b + 1)
                for r in range(ROUNDS):
                    pe.wait_ge(off_kept, b * 2)
                    pe.wait_ge(padded_ready, b * 2 + 2)
                    for h in range(HALVES):
                        for t in range(TAPS):
                            ky, kx = t // 3, t % 3
                            for j in range(4):
                                y = 8 * (4 * r + j) + ky
                                last = pe.matmul(ps_off[OPAD * j:OPAD * (j + 1), r, :], woff[:, h, t, :],
                                                 padded[:, h, y:y + 8, kx:kx + W],
                                                 start=(h == 0 and t == 0),
                                                 stop=(h == HALVES - 1 and t == TAPS - 1))
                    last.then_inc(off_ready, 1)
                for r in range(ROUNDS):
                    pe.wait_ge(off_kept, b * 2 + r + 1)
                    pe.wait_ge(pos_taken, b * 2)
                    for q in range(PXT):
                        last = pe.matmul(ps_pos[:, r, q * P:(q + 1) * P], off[:, r, q * P:(q + 1) * P],
                                         ident[:, :], is_transpose=True, start=True, stop=True)
                    last.then_inc(off_turned, 1)

            average(0)
            images(pe, image)


def conv_stage(nc, w_conv, gamma, beta, table, conv, keep):
    ident, idx_all, wts_all = keep["ident"], keep["idx_all"], keep["wts_all"]
    bn_scale, bn_shift = keep["bn_scale"], keep["bn_shift"]
    ROW = CORNERS * C
    GATHERS = PXT * TAPS
    NPAIR = GATHERS // 2
    RING = 12
    MIX = 3
    KC = TAPS * HALVES
    idx_v = idx_all[:, :, :, :, :, :].rearrange("p b r j q t -> p (b r j) (q t)")
    wts_v = wts_all[:, :, :, :, :, :, :].rearrange("p b r j q t s -> p (b r j) (q t s)")
    conv_v = conv.rearrange("(m p) n -> p m n", p=P)

    with ExitStack() as ctx:
        def sb(name, shape, dt=F32):
            return ctx.enter_context(nc.sbuf_tensor(name, shape, dt))

        def ps(name, shape):
            return ctx.enter_context(nc.psum_tensor(name, shape, F32))

        def sem(name):
            return ctx.enter_context(nc.semaphore(name))

        weights = sb("weights", [P, TAPS, HALVES, C])
        rows = sb("rows", [P, RING, ROW])
        mixed_sb = sb("mixed_sb", [P, 2 * MIX, C])
        sampled = sb("sampled", [P, 2, KC, CHUNK])
        conv_sb = sb("conv_sb", [P, 2, HALVES, CHUNK])
        idx = sb("idx", [P, 2, GATHERS], I32)
        wts = sb("wts", [P, 2, GATHERS * CORNERS])
        stats = sb("bn_stats", [P, HALVES, TILES, 6])
        mv = sb("bn_mv", [P, HALVES, 2])
        aff = sb("aff", [P, 2, HALVES])
        power = sb("bn_power", [P, HALVES])
        rs = sb("bn_rs", [P, HALVES])
        ps_turn = ps("ps_turn", [P, MIX, CHUNK])
        ps_conv = ps("ps_conv", [P, 2, HALVES, CHUNK])

        weights_in = sem("weights_in")
        sp_gate = sem("conv_sp_gate")
        pool_gate = sem("conv_pool_gate")
        idx_ready = sem("idx_ready")
        rows_in = [sem(f"rows_in{i}") for i in range(RING)]
        scaled = sem("scaled")
        mix_order = sem("mix_order")
        mixed = sem("mixed")
        turned = sem("pair_turned")
        filed = sem("filed")
        conv_ready = sem("conv_ready")
        conv_kept = sem("conv_kept")
        counted = sem("counted")
        conv_out = [sem(f"conv_out{i}") for i in range(2)]
        bn_step = sem("bn_step")
        pow_ready = sem("pow_ready")
        block = ctx.enter_context(nc.Block())

        def slot_of(g):
            pair, side = g // 2, g % 2
            return 2 * (pair // TAPS) + side, pair % TAPS

        def tiles(eng, step):
            step(0, 0, 0)
            step(1, 1, 0)
            with eng.Fori(1, TILES // 2) as k:
                step(k * 2, 0, k)
                step(k * 2 + 1, 1, k)

        @block.sync
        def _(sp):
            for t in range(TAPS):
                sp.dma_start(weights[:, t, :, :], w_conv[:, t, :].rearrange("(h p) o -> p h o", p=P))\
                  .then_inc(weights_in, 16)
            sp.dma_start(aff[:, 0, :], gamma.rearrange("(m p) -> p m", p=P),
                         allow_slow_non_contiguous=True).then_inc(weights_in, 16)
            sp.dma_start(aff[:, 1, :], beta.rearrange("(m p) -> p m", p=P),
                         allow_slow_non_contiguous=True).then_inc(weights_in, 16)
            with sp.Fori(0, TILES // 2) as k:
                for par in range(2):
                    at = sp.snap(k * (2 * CHUNK) + par * CHUNK)
                    sp.wait_ge(conv_kept, k * 2 + par + 1)
                    sp.sem_inc(sp_gate, 1)
                    sp.dma_start(conv_v[:, :, bass.ds(at, CHUNK)], conv_sb[:, par, :, :])\
                      .then_inc(conv_out[par], 16)
            for par in range(2):
                sp.wait_ge(conv_out[par], 16 * (TILES // 2))

        @block.gpsimd
        def _(pool):
            pool.memset(power[:, :], -0.5).then_inc(bn_step, 1)

            def step(s, par, k):
                pool.wait_ge(idx_ready, s + 1)
                for g in range(GATHERS):
                    if not isinstance(s, int) or s * GATHERS + g >= RING:
                        pool.wait_ge(mixed, s * GATHERS + g - RING + 1)
                        pool.sem_inc(pool_gate, 1)
                    q, t = slot_of(g)
                    pool.indirect_dma_start(rows[:, g % RING, :], None, table,
                                            bass.IndirectOffsetOnAxis(idx[:, par, q * TAPS + t:q * TAPS + t + 1], 0))\
                        .then_inc(rows_in[g % RING], 16)

            tiles(pool, step)
            pool.wait_ge(bn_step, 2)
            pool.tensor_tensor(rs[:, :], mv[:, :, 1], power[:, :], ALU.pow).then_inc(pow_ready, 1)

        @block.scalar
        def _(act):
            def conv_copy(par, n):
                act.wait_ge(conv_ready, n + 1)
                if not isinstance(n, int) or n >= 2:
                    act.wait_ge(conv_out[par], (n // 2) * 16 if isinstance(n, int) else upto(n >> 1, TILES) * 16)
                act.activation(conv_sb[:, par, :, :].rearrange("p m n -> p (m n)"),
                               ps_conv[:, par, :, :].rearrange("p m n -> p (m n)"), ACT.Copy).then_inc(conv_kept, 1)

            def step(s, par, k):
                act.wait_ge(idx_ready, s + 1)

                def file(n):
                    act.wait_ge(turned, s * NPAIR + n + 1)
                    half, t = n // TAPS, n % TAPS
                    if n == 0 and (not isinstance(s, int) or s >= 2):
                        act.wait_ge(conv_ready, s - 1)
                    act.activation(sampled[:, par, 2 * t:2 * t + 2, half * 256:half * 256 + 256],
                                   ps_turn[:, n % MIX, :].rearrange("p (h n) -> p h n", h=HALVES),
                                   ACT.Copy).then_inc(filed, 1)

                for n in range(NPAIR):
                    for g in (2 * n, 2 * n + 1):
                        q, t = slot_of(g)
                        act.wait_ge(rows_in[g % RING], (s * (GATHERS // RING) + g // RING + 1) * 16)
                        if not isinstance(s, int) or s * NPAIR + n >= MIX:
                            act.wait_ge(turned, s * NPAIR + n - MIX + 1)
                        at = (q * TAPS + t) * CORNERS
                        act.activation(mixed_sb[:, g % (2 * MIX), :], rows[:, g % RING, 0:C], ACT.Copy,
                                       scale=wts[:, par, at:at + 1]).then_inc(scaled, 1)
                    if n >= 2:
                        file(n - 2)
                    if n == 4 and (not isinstance(s, int) or s >= 2):
                        conv_copy(par, s - 2)
                file(NPAIR - 2)
                file(NPAIR - 1)

            tiles(act, step)
            conv_copy(0, TILES - 2)
            conv_copy(1, TILES - 1)

        @block.vector
        def _(dve):
            def load_indices(s, par):
                dve.tensor_copy(idx[:, par, :], idx_v[:, s, :])
                dve.tensor_copy(wts[:, par, :], wts_v[:, s, :]).then_inc(idx_ready, 1)

            def count(s, par, n):
                dve.wait_ge(conv_kept, s + 1)
                for m in range(HALVES):
                    last = dve.bn_stats(stats[:, m, n, :], conv_sb[:, par, m, :])
                last.then_inc(counted, 1)

            load_indices(0, 0)

            def step(s, par, k):
                for n in range(NPAIR):
                    for corner in range(1, CORNERS):
                        for side in range(2):
                            g = 2 * n + side
                            q, t = slot_of(g)
                            done = s * (4 * NPAIR) + 4 * n + 2 * (corner - 2) + side + 1
                            if corner == 1:
                                dve.wait_ge(rows_in[g % RING], (s * (GATHERS // RING) + g // RING + 1) * 16)
                                dve.wait_ge(scaled, s * GATHERS + g + 1)
                            else:
                                dve.wait_ge(mix_order, done)
                            at = (q * TAPS + t) * CORNERS + corner
                            ins = dve.scalar_tensor_tensor(
                                mixed_sb[:, g % (2 * MIX), :], rows[:, g % RING, corner * C:(corner + 1) * C],
                                wts[:, par, at:at + 1], mixed_sb[:, g % (2 * MIX), :], ALU.mult, ALU.add)
                            if corner < CORNERS - 1:
                                ins.then_inc(mix_order, 1)
                            else:
                                ins.then_inc(mixed, 1)
                    if n == 2:
                        load_indices(upto((s + 1) & (TILES - 1), TILES - 1) if not isinstance(s, int) else s + 1,
                                     1 - par)
                    if n == 6 and (not isinstance(s, int) or s >= 2):
                        count(s - 2, par, s - 2 if isinstance(s, int) else upto(s - 2, TILES - 1))

            tiles(dve, step)
            count(TILES - 2, 0, TILES - 2)
            count(TILES - 1, 1, TILES - 1)
            dve.wait_ge(counted, TILES)
            for m in range(HALVES):
                last = dve.bn_aggr(mv[:, m, :], stats[:, m, :, :].rearrange("p a b -> p (a b)"))
            last.then_inc(counted, 1)
            dve.wait_ge(counted, TILES + 1)
            dve.tensor_scalar(mv[:, :, 1], mv[:, :, 1], BN_EPS, None, ALU.add).then_inc(bn_step, 1)
            dve.wait_ge(weights_in, 16 * (TAPS + 2))
            dve.wait_ge(pow_ready, 1)
            dve.tensor_tensor(bn_scale[:, :], aff[:, 0, :], rs[:, :], ALU.mult).then_inc(bn_step, 1)
            dve.wait_ge(bn_step, 3)
            dve.tensor_tensor(mv[:, :, 0], mv[:, :, 0], bn_scale[:, :], ALU.mult).then_inc(bn_step, 1)
            dve.wait_ge(bn_step, 4)
            dve.tensor_tensor(bn_shift[:, :], aff[:, 1, :], mv[:, :, 0], ALU.subtract).then_inc(bn_step, 1)

        @block.tensor
        def _(pe):
            pe.wait_ge(weights_in, 16 * (TAPS + 2))

            def product(s, par, kc):
                t, h = kc // HALVES, kc % HALVES
                pe.wait_ge(filed, s * NPAIR + TAPS + t + 1)
                if kc == 0 and (not isinstance(s, int) or s >= 2):
                    pe.wait_ge(conv_kept, s - 1)
                for m in range(HALVES):
                    last = pe.matmul(ps_conv[:, par, m, :], weights[:, t, h, m * P:(m + 1) * P],
                                     sampled[:, par, kc, :], start=(kc == 0), stop=(kc == KC - 1))
                if kc == KC - 1:
                    last.then_inc(conv_ready, 1)

            def step(s, par, k):
                for n in range(NPAIR):
                    pe.wait_ge(mixed, s * GATHERS + 2 * n + 2)
                    if not isinstance(s, int) or s * NPAIR + n >= MIX:
                        pe.wait_ge(filed, s * NPAIR + n - MIX + 1)
                    for h in range(HALVES):
                        for side in range(2):
                            g = 2 * n + side
                            at = h * 256 + side * P
                            last = pe.matmul(ps_turn[:, n % MIX, at:at + P],
                                             mixed_sb[:, g % (2 * MIX), h * P:(h + 1) * P],
                                             ident[:, :], is_transpose=True, start=True, stop=True)
                    last.then_inc(turned, 1)
                    if not isinstance(s, int) or s >= 1:
                        product(s - 1, 1 - par, n)

            tiles(pe, step)
            for kc in range(KC):
                product(TILES - 1, 1, kc)


def token_stage(nc, x, conv, d, out, keep):
    ident, bn_scale, bn_shift = keep["ident"], keep["bn_scale"], keep["bn_shift"]
    SUBS = CHUNK // P
    STEPS = TILES
    T_STEP, T_IMG = STEP_TILES, EXPERT_TILES
    T_ALL = T_IMG * B
    AHEAD, RING = 3, 3
    assert T_STEP % AHEAD == 0 and T_STEP % RING == 0
    HID_LAG, OUT_LAG, STORE_LAG = 1, 2, 5
    SCATTER = 16 * TOP_K * SUBS
    REGION = N + P
    BUFFER = E * REGION
    x_v = x.rearrange("b (h p) y x -> b p h (y x)", p=P)
    conv_v = conv.rearrange("(h p) (b n) -> b p h n", p=P, b=B)
    out_v = out.rearrange("b (h p) y x -> b p h (y x)", p=P)
    w1_v = d["w_1"].rearrange("e (h p) n -> e p h n", p=P)
    BODY, REST = CHUNK - SHIFT, SHIFT
    slots = nc.dram_tensor("slots", (2 * BUFFER, C), F32, kind="Internal").ap()
    results = [nc.dram_tensor(f"results{i}", (T_IMG * P, C), F32, kind="Internal").ap() for i in range(2)]
    base = nc.dram_tensor("firsts", (STEPS, P, SUBS * C), F32, kind="Internal").ap()

    with ExitStack() as ctx:
        def sb(name, shape, dt=F32):
            return ctx.enter_context(nc.sbuf_tensor(name, shape, dt))

        def ps(name, shape):
            return ctx.enter_context(nc.psum_tensor(name, shape, F32))

        def sem(name):
            return ctx.enter_context(nc.semaphore(name))

        wqk = sb("wqk", [P, HALVES, 2 * C])
        wv = sb("wv", [P, HALVES, 2, P])
        wo = sb("wo", [P, HALVES, C])
        wr = sb("wr", [P, HALVES, E])
        w1 = sb("w1", [P, AHEAD, HALVES, C])
        w2 = sb("w2", [P, HALVES, E, C])
        b1 = sb("b1", [P, E, HALVES])
        b2 = sb("b2", [P, E, C])
        bqk = sb("bqk", [P, 4])
        bv = sb("bv", [P, P])
        bo = sb("bo", [P, C])
        bias = sb("bias", [P, 2, HEADS * WIN])
        lower = sb("lower", [P, E * E])
        strict = sb("strict", [P, P])
        ones = sb("ones", [P, P])
        region = sb("region", [P, 2, E])
        row_id = sb("row_id", [P, E])
        octal = sb("octal", [1, E])
        tile_id = sb("tile_id", [1, T_IMG])
        power = sb("c_power", [P, 4])
        zero = sb("c_zero", [P, C])
        xl = sb("xl", [P, 2, HALVES, CHUNK])
        yl = sb("yl", [P, 2, HALVES, CHUNK])
        xt = sb("xt", [P, SUBS, C])
        res = sb("res", [P, 2, SUBS, C])
        nrm = sb("nrm", [P, SUBS, C])
        tok = sb("ctok", [P, 2, SUBS, C])
        nrm_t = sb("nrm_t", [P, HALVES, CHUNK])
        qt = sb("qt", [P, HALVES, CHUNK])
        kdiag = sb("kdiag", [P, HALVES, HG, CHUNK])
        vdiag = sb("vdiag", [P, WINS, PAIRS, 2 * HD])
        prob = sb("prob", [P, SUBS, HEADS * WIN])
        prob_t = sb("prob_t", [P, SUBS, HEADS * WIN])
        att_t = sb("att_t", [P, HALVES, CHUNK])
        tok_t = sb("tok_t", [P, HALVES, CHUNK])
        first = sb("first", [P, SUBS * C])
        stats = sb("ln_stats", [P, SUBS, 6])
        mv = sb("ln_mv", [P, SUBS, 2])
        var = sb("ln_var", [P, SUBS])
        rs = sb("ln_rs", [P, SUBS])
        top = sb("top", [P, SUBS * HEADS])
        total = sb("total", [P, SUBS * HEADS])
        inverse = sb("inverse", [P, SUBS * HEADS])
        rmax = sb("rmax", [P, SUBS])
        rexp = sb("rexp", [P, SUBS, E])
        rsum = sb("rsum", [P, SUBS])
        rprob = sb("rprob", [P, SUBS, E])
        more = sb("more", [P, SUBS, E, E])
        same = sb("same", [P, SUBS, E, E])
        rank = sb("rank", [P, SUBS, E])
        sel = sb("sel", [P, SUBS, E])
        chosen = sb("chosen", [P, SUBS, E])
        comb = sb("comb", [P, SUBS, E])
        filled = sb("filled", [P, E])
        place = sb("place", [P, SUBS, E])
        high = sb("high", [P, SUBS])
        both = sb("both", [P, SUBS])
        is_high = sb("is_high", [P, SUBS, E])
        weighed = sb("weighed", [P, SUBS, E])
        scat_idx = sb("scat_idx", [P, 2, TOP_K, SUBS], I32)
        row_hist = sb("row_hist", [P, STEPS, TOP_K * SUBS])
        gate_hist = sb("gate_hist", [P, STEPS, TOP_K * SUBS])
        pad_f = sb("pad_f", [P, E])
        pad_idx = sb("pad_idx", [P, E], I32)
        need_i = sb("need_i", [P, E], I32)
        need = sb("need", [P, E])
        gap = sb("gap", [P, E])
        shrink = sb("shrink", [P, 2, E])
        start = sb("start", [1, 3, E])
        beyond = sb("beyond", [1, T_IMG, E])
        scratch = sb("scratch", [1, T_IMG, E])
        rows_f = sb("rows_f", [1, 3, T_IMG])
        ids = sb("ids", [1, OUT_LAG + T_ALL + T_STEP + E])
        packing = sb("packing", [1, 2, IMG_CHUNKS + 1, E])
        words_f = sb("words_f", [1, 2, IMG_CHUNKS + 1])
        words = sb("words", [1, 2, STEPS + 1], I32)
        row_in = sb("row_in", [1, T_ALL], I32)
        w1_of = sb("w1_of", [1, T_ALL], I32)
        xs = sb("xs", [P, AHEAD, C])
        xs_t = sb("xs_t", [P, 2, HALVES, P])
        hid_t = sb("hid_t", [P, 2, HALVES, P])
        ys = sb("ys", [P, RING, C])
        region_of = sb("region_of", [P, TOP_K * SUBS, E])
        shift_by = sb("shift_by", [P, TOP_K * SUBS])
        cidx = sb("cidx", [P, 2, TOP_K * SUBS], I32)
        cgate = sb("cgate", [P, 2, TOP_K * SUBS])
        got = sb("got", [P, TOP_K, SUBS, C])
        acc = sb("acc", [P, SUBS, C])
        final = sb("final", [P, HALVES, CHUNK])
        rel, flip = final[0:WIN, 0, :], final[0:WIN, 1, 0:P]

        fa = ps("fa", [P, 2, CHUNK])
        ga = ps("ga", [P, 2, CHUNK])
        pt = ps("pt", [P, CHUNK])
        ph = ps("ph", [P, CHUNK])
        py = ps("py", [P, CHUNK])
        pf = ps("pf", [P, CHUNK])
        fa_all = fa[:, :, :].rearrange("p a n -> p (a n)")
        ga_all = ga[:, :, :].rearrange("p a n -> p (a n)")

        weights_in = sem("c_weights_in")
        experts_in = sem("experts_in")
        tables = sem("tables")
        bias_turned = sem("bias_turned")
        bias_kept = sem("bias_kept")
        loads_in = [sem(f"loads_in{i}") for i in range(2)]
        relued = sem("relued")
        summed = sem("summed")
        x_turned = sem("x_turned")
        x_kept = sem("x_kept")
        front_order = sem("front_order")
        back_order = sem("back_order")
        var_ready = [sem(f"var_ready{n}") for n in (1, 2)]
        rs_ready = [sem(f"rs_ready{n}") for n in (1, 2)]
        n1_ready = sem("n1_ready")
        bo_added = sem("bo_added")
        n1_turned = sem("n1_turned")
        n1_kept = sem("n1_kept")
        q_ready = sem("q_ready")
        k_ready = sem("k_ready")
        q_kept = sem("q_kept")
        k_kept_act = sem("k_kept_act")
        k_kept_dve = sem("k_kept_dve")
        v_ready = sem("v_ready")
        v_kept = sem("v_kept")
        scored = sem("scored")
        shifted = sem("shifted")
        exped = sem("exped")
        probs_ready = sem("probs_ready")
        p_turned = sem("p_turned")
        p_kept = sem("p_kept")
        mixed_v = sem("mixed_v")
        att_kept = sem("att_kept")
        projected = sem("projected")
        n2_ready = sem("n2_ready")
        first_ready = sem("first_ready")
        first_out = sem("first_out")
        n2_turned = sem("n2_turned")
        n2_kept = sem("n2_kept")
        routed = sem("routed")
        route_in = sem("route_in")
        route_exp = sem("route_exp")
        route_order = sem("route_order")
        comb_ready = sem("comb_ready")
        ranked = sem("ranked")
        place_order = sem("place_order")
        placed = sem("placed")
        scattered = [sem(f"scattered{i}") for i in range(2)]
        padded = sem("padded")
        pads_out = sem("pads_out")
        table_order = sem("table_order")
        table_ready = sem("table_ready")
        xs_in = [sem(f"xs_in{i}") for i in range(AHEAD)]
        xs_turned = sem("xs_turned")
        xs_kept = sem("xs_kept")
        hid_ready = sem("hid_ready")
        hid_kept = sem("hid_kept")
        y_ready = sem("y_ready")
        y_kept = sem("y_kept")
        ys_out = [sem(f"ys_out{i}") for i in range(RING)]
        cidx_order = sem("cidx_order")
        cidx_ready = sem("cidx_ready")
        got_in = [sem(f"got_in{u}") for u in range(SUBS)]
        acc_in = sem("acc_in")
        acc_half = sem("acc_half")
        acc_done = sem("acc_done")
        out_turned = sem("out_turned")
        out_kept = sem("out_kept")
        stored = sem("stored")
        sp_gate, dve_gate, pool_gate = sem("c_sp_gate"), sem("c_dve_gate"), sem("c_pool_gate")
        pe_gate, act_gate = sem("c_pe_gate"), sem("c_act_gate")
        block = ctx.enter_context(nc.Block())
        WEIGHTS, TABLES, EXPERTS = 21, 8, 4
        FRONT_K, BACK_K, ROUTE_K, PLACE_K, TABLE_K = 2, 11, 13, 7, 15

        def steps(eng, step, flush=None):
            for img in range(B + 2):
                i0 = img * IMG_CHUNKS
                if img == B + 1 and flush is not None:
                    flush()
                step(i0, 0, img)
                with eng.Fori(0, IMG_CHUNKS // 2 - 1) as k:
                    step(k * 2 + (i0 + 1), 1, img)
                    step(k * 2 + (i0 + 2), 0, img)
                step(i0 + IMG_CHUNKS - 1, 1, img)

        def has_front(i):
            return not isinstance(i, int) or i + 1 < STEPS

        def has_input(i):
            return not isinstance(i, int) or i + 2 < STEPS

        def has_routes(i, att):
            return not (isinstance(i, int) and i == 0) if att else isinstance(i, int) and i == STEPS

        def starts_image(i):
            return isinstance(i, int) and i % IMG_CHUNKS == 0

        def expert_of(eng, m):
            at = m if isinstance(m, int) else upto(m, STEPS)
            loaded = {}

            def who(t, lag):
                w, j = divmod(t - lag + OUT_LAG, E)
                if w not in loaded:
                    at_ap = words[0:1, w, at:at + 1] if isinstance(at, int) else words[0:1, w, bass.ds(at, 1)]
                    loaded[w] = eng.value_load(at_ap, min_val=0, max_val=8 ** E - 1)
                return upto((loaded[w] >> (3 * j)) & (E - 1), E - 1)

            return who

        def stages(img):
            return img < B, 1 <= img <= B, img >= 2

        def columns(eng, i):
            if isinstance(i, int):
                return i % IMG_CHUNKS * CHUNK + SHIFT, (i + 1) % IMG_CHUNKS * CHUNK
            return (eng.snap(upto((i & (IMG_CHUNKS - 1)) * CHUNK + SHIFT, N - BODY)),
                    eng.snap(upto(((i + 1) & (IMG_CHUNKS - 1)) * CHUNK, N - REST)))

        def half_of(i):
            return i // 2 if isinstance(i, int) else upto(i >> 1, STEPS)

        def tile(m, t, lag):
            g = m * T_STEP + t - lag
            if isinstance(m, int) and not 0 <= g < T_ALL:
                return None
            return g

        @block.sync
        def _(sp):
            def load(nxt, par, turned):
                body, rest = columns(sp, nxt)
                image = nxt // IMG_CHUNKS if isinstance(nxt, int) else sp.snap(upto(nxt >> 3, B - 1))
                at_least(sp, x_turned, turned)
                sp.sem_inc(sp_gate, 1)
                for src, dst in ((x_v, xl), (conv_v, yl)):
                    sp.dma_start(dst[:, par, :, 0:BODY], src[image, :, :, bass.ds(body, BODY)])\
                      .then_inc(loads_in[par], 16)
                    sp.dma_start(dst[:, par, :, BODY:CHUNK], src[image, :, :, bass.ds(rest, REST)])\
                      .then_inc(loads_in[par], 16)

            load(0, 0, 0)
            for h in range(HALVES):
                rows = slice(h * P, (h + 1) * P)
                sp.dma_start(wqk[:, h, :], d["w_qk"][rows, :]).then_inc(weights_in, 16)
                sp.dma_start(wv[:, h, :, :].rearrange("p a n -> p (a n)"), d["w_v"][rows, :]).then_inc(weights_in, 16)
                sp.dma_start(wo[:, h, :], d["w_out"][rows, :]).then_inc(weights_in, 16)
                sp.dma_start(wr[:, h, :], d["w_router"][rows, :]).then_inc(weights_in, 16)
                sp.dma_start(bv[64 * h:64 * h + 64, :], d["b_v"][h:h + 1, :].partition_broadcast(64)
                             .rearrange("p a n -> p (a n)")).then_inc(weights_in, 16)
            sp.dma_start(rel.rearrange("p (h k) -> p h k", k=WIN),
                         bass.AP(d["rel_rev"].tensor, 0, [[1, WIN], [2 * WIN - 1, HEADS], [1, WIN]]))\
              .then_inc(weights_in, 16)
            sp.dma_start(flip, d["flip_c"]).then_inc(weights_in, 16)
            sp.dma_start(bqk[:, :], d["b_qk"]).then_inc(weights_in, 16)
            sp.dma_start(bo[:, :], d["b_out"].partition_broadcast(P)).then_inc(weights_in, 16)
            sp.dma_start(lower[:, :], d["lower_c"]).then_inc(weights_in, 16)
            sp.dma_start(bias[:, 1, :], d["apart_c"]).then_inc(weights_in, 16)
            sp.dma_start(strict[:, :], d["strict_c"]).then_inc(weights_in, 16)
            sp.dma_start(region[:, :, :].rearrange("p a e -> p (a e)"), d["region_c"]).then_inc(weights_in, 16)
            sp.dma_start(row_id[:, :], d["row_id_c"]).then_inc(weights_in, 16)
            sp.dma_start(octal[:, :], d["octal_c"]).then_inc(weights_in, 16)
            sp.dma_start(tile_id[:, :], d["tile_id_c"]).then_inc(weights_in, 16)
            load(1, 1, 0)
            for h in range(HALVES):
                rows = slice(h * P, (h + 1) * P)
                sp.dma_start(w2[:, h, :, :], d["w_2"][:, rows, :].rearrange("e p n -> p e n")).then_inc(experts_in, 16)
            sp.dma_start(b1[:, :, :].rearrange("p e h -> p (e h)"), d["b_1"])\
              .then_inc(experts_in, 16)
            sp.dma_start(b2[:, :, :].rearrange("p e n -> p (e n)"), d["b_2"].partition_broadcast(P))\
              .then_inc(experts_in, 16)

            load(2, 0, 1)

            def expert_slot(m, t, img):
                g = tile(m, t, 0)
                if g is not None:
                    entry = slice(g, g + 1) if isinstance(g, int) else bass.ds(upto(g, T_ALL - 1), 1)
                    row = sp.value_load(row_in[0:1, entry], min_val=0, max_val=2 * BUFFER - P)
                    e = sp.value_load(w1_of[0:1, entry], min_val=0, max_val=E - 1)
                    at_least(sp, hid_ready, g - AHEAD + 1)
                    sp.sem_inc(sp_gate, 1)
                    sp.dma_start(xs[:, t % AHEAD, :], slots[bass.ds(row, P), :]).then_inc(xs_in[t % AHEAD], 16)
                    sp.dma_start(w1[:, t % AHEAD, :, :], w1_v[e, :, :, :]).then_inc(xs_in[t % AHEAD], 16)
                g = tile(m, t, STORE_LAG)
                if g is not None:
                    if isinstance(g, int):
                        image, row = g // T_IMG, g % T_IMG * P
                    else:
                        image = img - 1
                        row = sp.snap(upto((g - image * T_IMG) * P, (T_IMG - 1) * P))
                    sp.wait_ge(y_kept, g + 1)
                    sp.sem_inc(sp_gate, 1)
                    r = (t - STORE_LAG) % RING
                    sp.dma_start(results[image % 2][bass.ds(row, P), :], ys[:, r, :]).then_inc(ys_out[r], 16)

            def step(i, par, img):
                att, exp, com = stages(img)
                m, c = i - IMG_CHUNKS, i - 2 * IMG_CHUNKS
                if exp and starts_image(m):
                    sp.wait_ge(table_ready, img)
                    for half in range(2):
                        sp.wait_ge(scattered[half], SCATTER * (IMG_CHUNKS // 2) * img)
                    sp.wait_ge(pads_out, 16 * E * img)
                    sp.sem_inc(sp_gate, 1)
                if com:
                    which = c if isinstance(c, int) else sp.snap(upto(c, STEPS - 1))
                    at_least(sp, out_turned, c * 2)
                    sp.sem_inc(sp_gate, 1)
                    sp.dma_start(acc[:, :, :].rearrange("p u c -> p (u c)"), base[which, :, :]).then_inc(acc_in, 16)
                for t in range(T_STEP):
                    if exp:
                        expert_slot(m, t, img)
                    if t == 1 and att and has_input(i):
                        load((i + 3) & (STEPS - 1), 1 - par, i + 2)
                if att:
                    which = i if isinstance(i, int) else sp.snap(upto(i, STEPS - 1))
                    sp.wait_ge(first_ready, i + 1)
                    sp.sem_inc(sp_gate, 1)
                    sp.dma_start(base[which, :, :], first[:, :]).then_inc(first_out, 16)
                if com:
                    body, rest = columns(sp, c)
                    sp.wait_ge(out_kept, (c + 1) * 2)
                    sp.sem_inc(sp_gate, 1)
                    sp.dma_start(out_v[img - 2, :, :, bass.ds(body, BODY)], final[:, :, 0:BODY]).then_inc(stored, 16)
                    sp.dma_start(out_v[img - 2, :, :, bass.ds(rest, REST)], final[:, :, BODY:CHUNK]).then_inc(stored, 16)

            def flush():
                for t in range(STORE_LAG):
                    expert_slot(STEPS, t, B + 1)

            steps(sp, step, flush)
            sp.wait_ge(stored, 32 * STEPS)
            for par in range(2):
                sp.wait_ge(loads_in[par], 64 * (STEPS // 2 + 1))
            sp.wait_ge(first_out, 16 * STEPS)
            for r in range(RING):
                sp.wait_ge(ys_out[r], 16 * (T_ALL // RING))

        @block.gpsimd
        def _(pool):
            pool.memset(power[:, :], -0.5).then_inc(tables, 1)
            pool.memset(kdiag[:, :, :, :], 0.0).then_inc(tables, 1)
            pool.memset(vdiag[:, :, :, :], 0.0).then_inc(tables, 1)
            pool.memset(ones[:, :], 1.0).then_inc(tables, 1)
            pool.memset(zero[:, :], 0.0).then_inc(tables, 1)
            pool.memset(ids[:, :], 0.0).then_inc(tables, 1)
            pool.memset(filled[:, :], 0.0).then_inc(tables, 1)
            pool.wait_ge(tables, TABLES - 1)

            def add_x(i, par):
                pool.wait_ge(relued, i + 1)
                pool.tensor_tensor(xl[:, par, :, :], xl[:, par, :, :], yl[:, par, :, :], ALU.add).then_inc(summed, 1)

            def scatter(i, par):
                pool.wait_ge(placed, i + 1)
                pool.sem_inc(pool_gate, 1)
                for u in range(SUBS):
                    for k in range(TOP_K):
                        pool.indirect_dma_start(
                            slots, bass.IndirectOffsetOnAxis(scat_idx[:, par, k, u:u + 1], 0),
                            tok[:, par, u, :], None).then_inc(scattered[par], 16)

            def all_results(images):
                for r in range(RING):
                    pool.wait_ge(ys_out[r], 16 * (T_IMG // RING) * images)

            def inverse_root(nth, j):
                pool.wait_ge(var_ready[nth], j + 1)
                pool.tensor_tensor(rs[:, :], var[:, :], power[:, :], ALU.pow).then_inc(rs_ready[nth], 1)

            def add_bo(j, par):
                pool.wait_ge(n1_ready, j + 1)
                for u in range(SUBS):
                    last = pool.tensor_tensor(res[:, par, u, :], xt[:, u, :], bo[:, :], ALU.add)
                last.then_inc(bo_added, 1)

            add_x(0, 0)
            inverse_root(0, 0)
            pool.wait_ge(weights_in, 16 * WEIGHTS)
            pool.wait_ge(bias_kept, 1)
            pool.tensor_tensor(bias[:, 1, :], bias[:, 1, :], bias[:, 0, :], ALU.add).then_inc(tables, 1)
            add_x(1, 1)
            add_bo(0, 0)
            inverse_root(0, 1)

            def step(i, par, img):
                att, exp, com = stages(img)
                c = i - 2 * IMG_CHUNKS
                new_image = starts_image(i)
                if new_image and exp:
                    scatter(i - 1, 1 - par)
                if exp and starts_image(i):
                    pool.wait_ge(padded, img)
                    for e in range(E):
                        pool.indirect_dma_start(slots, bass.IndirectOffsetOnAxis(pad_idx[:, e:e + 1], 0),
                                                zero[:, :], None).then_inc(pads_out, 16)
                if att and has_front(i):
                    add_bo(i + 1, 1 - par)
                if att and has_input(i):
                    add_x(i + 2, par)
                if com:
                    if starts_image(c):
                        all_results(img - 1)
                    pool.wait_ge(cidx_ready, c + 1)
                    pool.sem_inc(pool_gate, 1)
                    for u in range(SUBS):
                        for k in range(TOP_K):
                            pool.indirect_dma_start(got[:, k, u, :], None, results[img % 2],
                                                    bass.IndirectOffsetOnAxis(cidx[:, par, k * SUBS + u:k * SUBS + u + 1], 0))\
                                .then_inc(got_in[u], 16)
                if att:
                    inverse_root(1, i)
                    pool.wait_ge(n2_ready, i + 1)
                    at_least(pool, first_out, i * 16)
                    pool.tensor_tensor(first[:, :], res[:, par, :, :].rearrange("p u c -> p (u c)"),
                                       tok[:, par, :, :].rearrange("p u c -> p (u c)"), ALU.add)\
                        .then_inc(first_ready, 1)
                    if has_input(i):
                        inverse_root(0, i + 2)
                    if not new_image:
                        scatter(i - 1, 1 - par)

            steps(pool, step)
            for par in range(2):
                pool.wait_ge(scattered[par], SCATTER * (STEPS // 2))
            pool.wait_ge(pads_out, 16 * E * B)

        @block.scalar
        def _(act):
            def relu(i, par):
                act.wait_ge(loads_in[par], (half_of(i) + 1) * 64)
                for h in range(HALVES):
                    last = act.activation(yl[:, par, h, :], yl[:, par, h, :], ACT.Relu,
                                          bias=bn_shift[:, h:h + 1], scale=bn_scale[:, h:h + 1])
                last.then_inc(relued, 1)

            def expert_slot(m, t, par, who):
                g = tile(m, t, 0)
                if g is not None:
                    act.wait_ge(xs_turned, g + 1)
                    at_least(act, hid_ready, g - 1)
                    act.activation(xs_t[:, (par + t) % 2, :, :].rearrange("p h n -> p (h n)"), pt[:, 0:C],
                                   ACT.Copy).then_inc(xs_kept, 1)
                g = tile(m, t, HID_LAG)
                if g is not None:
                    act.wait_ge(hid_ready, g + 1)
                    at_least(act, y_ready, g - 1)
                    e = who(t, HID_LAG)
                    for f in range(HALVES):
                        last = act.activation(hid_t[:, (par + t + 1) % 2, f, :], ph[:, f * P:(f + 1) * P], ACT.Gelu,
                                              bias=b1[:, e, f:f + 1])
                    last.then_inc(hid_kept, 1)

            def keep_x(j):
                act.wait_ge(x_turned, j + 1)
                at_least(act, bo_added, j)
                act.activation(xt[:, :, :].rearrange("p u c -> p (u c)"), fa_all, ACT.Copy).then_inc(x_kept, 1)

            def keep_normed(j):
                act.wait_ge(n1_turned, j + 1)
                act.activation(nrm_t[:, :, :].rearrange("p h n -> p (h n)"), fa_all, ACT.Copy).then_inc(n1_kept, 1)

            def keep_q(j):
                act.wait_ge(q_ready, j + 1)
                at_least(act, scored, j * SUBS)
                for h in range(HALVES):
                    last = act.activation(qt[:, h, :], fa[:, h, :], ACT.Identity, bias=bqk[:, h:h + 1])
                last.then_inc(q_kept, 1)

            def keep_k(j):
                act.wait_ge(k_ready, j + 1)
                for n in range(HG):
                    rows = slice(HD * n, HD * (n + 1))
                    last = act.activation(kdiag[rows, 0, n, :], fa[rows, 0, :], ACT.Identity, bias=bqk[rows, 2:3])
                last.then_inc(k_kept_act, 1)

            def exp_scores(i, v):
                act.wait_ge(shifted, 2 * i + v + 1)
                act.activation(prob[:, 2 * v:2 * v + 2, :], prob[:, 2 * v:2 * v + 2, :], ACT.Exp).then_inc(exped, 1)

            def keep_probs(i, v):
                for u in (2 * v, 2 * v + 1):
                    act.wait_ge(p_turned, i * SUBS + u + 1)
                    act.activation(prob_t[:, u, :], ga[:, u % 2, :], ACT.Copy).then_inc(p_kept, 1)

            def exp_logits(i):
                act.wait_ge(route_in, i + 1)
                act.activation(rexp[:, :, :], rexp[:, :, :], ACT.Exp).then_inc(route_exp, 1)

            relu(0, 0)
            keep_x(0)
            keep_normed(0)
            act.wait_ge(weights_in, 16 * WEIGHTS)
            act.wait_ge(bias_turned, 1)
            act.activation(bias[:, 0, :], ga[:, 0, :], ACT.Copy).then_inc(bias_kept, 1)
            keep_q(0)
            relu(1, 1)
            act.wait_ge(tables, TABLES)
            keep_k(0)
            keep_x(1)

            def step(i, par, img):
                att, exp, com = stages(img)
                front = att and has_front(i)
                m, c = i - IMG_CHUNKS, i - 2 * IMG_CHUNKS

                if front:
                    keep_normed(i + 1)
                if att:
                    exp_scores(i, 0)
                if has_routes(i, att):
                    exp_logits(i - 1)
                if att and has_input(i):
                    relu(i + 2, par)
                if front:
                    keep_q(i + 1)
                who = None
                if exp:
                    if starts_image(m):
                        act.wait_ge(experts_in, 16 * EXPERTS)
                        act.wait_ge(table_ready, img)
                        act.sem_inc(act_gate, 1)
                    who = expert_of(act, m)

                def slot(t):
                    if exp:
                        expert_slot(m, t, par, who)

                slot(0)
                if att:
                    exp_scores(i, 1)
                if front:
                    keep_k(i + 1)
                slot(1)
                if att:
                    keep_probs(i, 0)
                slot(2)
                if att:
                    keep_probs(i, 1)
                slot(3)
                if att:
                    act.wait_ge(mixed_v, i + 1)
                    act.activation(att_t[:, :, :].rearrange("p h n -> p (h n)"), ga_all, ACT.Copy).then_inc(att_kept, 1)
                slot(4)
                slot(5)
                slot(6)
                if com:
                    for v in range(2):
                        act.wait_ge(out_turned, c * 2 + v + 1)
                        at_least(act, stored, c * 32)
                        act.activation(final[:, :, 256 * v:256 * v + 256],
                                       pf[:, :].rearrange("p (h n) -> p h n", h=HALVES), ACT.Copy)\
                           .then_inc(out_kept, 1)
                if att and has_input(i):
                    keep_x(i + 2)
                slot(7)
                if att:
                    act.wait_ge(n2_turned, i + 1)
                    act.activation(tok_t[:, :, :].rearrange("p h n -> p (h n)"), ga_all, ACT.Copy).then_inc(n2_kept, 1)
                slot(8)

            def flush():
                who = expert_of(act, STEPS)
                for t in range(OUT_LAG):
                    expert_slot(STEPS, t, 0, who)

            steps(act, step, flush)

        @block.vector
        def _(dve):
            forder, border = Tally(FRONT_K), Tally(BACK_K)
            rorder, porder, torder = Tally(ROUTE_K), Tally(PLACE_K), Tally(TABLE_K)

            def expert_slot(m, t, par, who):
                g = tile(m, t, OUT_LAG)
                if g is not None:
                    dve.wait_ge(y_ready, g + 1)
                    r = (t - OUT_LAG) % RING
                    at_least(dve, ys_out[r], (m * (T_STEP // RING) + (t - OUT_LAG) // RING) * 16)
                    dve.tensor_tensor(ys[:, r, :], py[:, 0:C], b2[:, who(t, OUT_LAG), :], ALU.add)\
                       .then_inc(y_kept, 1)

            def places(i, par, img):
                def chained(ins):
                    ins.then_inc(place_order, 1)
                    dve.wait_ge(place_order, porder.next(i))

                def over_u(a):
                    return a.unsqueeze(1).broadcast_to([P, SUBS, E])

                def over_e(a):
                    return a[:, :].unsqueeze(2).broadcast_to([P, SUBS, E])

                porder.begin()
                dve.wait_ge(ranked, i + 1)
                before_ = pf[:, 0:SUBS * E].rearrange("p (u e) -> p u e", e=E)
                chained(dve.tensor_tensor(place[:, :, :], before_, over_u(filled[:, :]), ALU.add))
                dve.tensor_tensor(filled[:, :], filled[:, :], pf[:, 64:64 + E], ALU.add)
                chained(dve.tensor_tensor(place[:, :, :], place[:, :, :], over_u(region[:, img % 2, :]), ALU.add))
                chained(dve.tensor_tensor(place[:, :, :], place[:, :, :], sel[:, :, :], ALU.mult))
                dve.tensor_reduce(high[:, :], place[:, :, :], AX_X, ALU.max)
                chained(dve.tensor_reduce(both[:, :], place[:, :, :], AX_X, ALU.add))
                dve.tensor_tensor(is_high[:, :, :], place[:, :, :], over_e(high), ALU.is_equal)
                chained(dve.tensor_tensor(both[:, :], both[:, :], high[:, :], ALU.subtract))
                chained(dve.tensor_tensor(sel[:, :, :], sel[:, :, :], is_high[:, :, :], ALU.subtract))
                hist = i if isinstance(i, int) else upto(i, STEPS - 1)
                dve.tensor_tensor(weighed[:, :, :], is_high[:, :, :], comb[:, :, :], ALU.mult)
                chained(dve.tensor_tensor(comb[:, :, :], sel[:, :, :], comb[:, :, :], ALU.mult))
                dve.tensor_reduce(gate_hist[:, hist, 0:SUBS], weighed[:, :, :], AX_X, ALU.add)
                dve.tensor_reduce(gate_hist[:, hist, SUBS:2 * SUBS], comb[:, :, :], AX_X, ALU.add)
                at_least(dve, scattered[par], half_of(i) * SCATTER)
                for k, rows in enumerate((high, both)):
                    dve.tensor_copy(row_hist[:, hist, k * SUBS:(k + 1) * SUBS], rows[:, :])
                    last = dve.tensor_scalar(scat_idx[:, par, k, :], rows[:, :], -1.0, None, ALU.add)
                last.then_inc(placed, 1)
                porder.end()

            def tile_table(img):
                def chained(ins):
                    ins.then_inc(table_order, 1)
                    dve.wait_ge(table_order, torder.next(img))

                torder.begin()
                one = slice(0, 1)
                first_row = float((img % 2) * BUFFER)
                at_least(dve, pads_out, 16 * E * img)
                dve.tensor_tensor(pad_f[:, :], filled[:, :], row_id[:, :], ALU.add)
                chained(dve.tensor_scalar(gap[:, :], filled[:, :], float(P - 1), None, ALU.add))
                dve.tensor_scalar(pad_idx[:, :], pad_f[:, :], first_row, None, ALU.add).then_inc(padded, 1)
                dve.memset(filled[:, :], 0.0)
                chained(dve.tensor_copy(need_i[:, :], gap[:, :]))
                chained(dve.tensor_scalar(need_i[:, :], need_i[:, :], 7, None, ALU.arith_shift_right))
                chained(dve.tensor_copy(need[:, :], need_i[:, :]))
                dve.tensor_scalar(gap[:, :], need[:, :], -float(P), float(REGION), ALU.mult, ALU.add)
                chained(dve.tensor_copy(start[:, 0, :], need[one, :]))
                src = 0
                for n, dist in enumerate((1, 2, 4)):
                    dst = n + 1 if n < 2 else 0
                    dve.tensor_copy(start[:, dst, 0:dist], start[:, src, 0:dist])
                    chained(dve.tensor_tensor(start[:, dst, dist:E], start[:, src, dist:E],
                                              start[:, src, 0:E - dist], ALU.add))
                    src = dst
                dve.memset(shrink[:, img % 2, 0:1], first_row + 1)
                dve.tensor_copy(shrink[:, img % 2, 1:E], gap[:, 0:E - 1])
                upto_e = start[:, src, :].unsqueeze(1).broadcast_to([1, T_IMG, E])
                t_of = tile_id[:, :].unsqueeze(2).broadcast_to([1, T_IMG, E])
                chained(dve.tensor_tensor(beyond[:, :, :], t_of, upto_e, ALU.is_ge))
                own = ids[:, OUT_LAG + img * T_IMG:OUT_LAG + (img + 1) * T_IMG]
                dve.tensor_reduce(own, beyond[:, :, 0:E - 1], AX_X, ALU.add)
                chained(dve.tensor_tensor(scratch[:, :, :], beyond[:, :, :],
                                          gap[one, :].unsqueeze(1).broadcast_to([1, T_IMG, E]), ALU.mult))
                dve.tensor_reduce(rows_f[:, 0, :], scratch[:, :, 0:E - 1], AX_X, ALU.add)
                chained(dve.tensor_scalar(rows_f[:, 1, :], beyond[:, :, E - 1], -1.0, 1.0, ALU.mult, ALU.add))
                chained(dve.scalar_tensor_tensor(rows_f[:, 2, :], tile_id[:, :], float(P), rows_f[:, 0, :],
                                                 ALU.mult, ALU.add))
                chained(dve.tensor_tensor(rows_f[:, 2, :], rows_f[:, 2, :], rows_f[:, 1, :], ALU.mult))
                at = slice(img * T_IMG, (img + 1) * T_IMG)
                dve.tensor_scalar(row_in[:, at], rows_f[:, 2, :], first_row, None, ALU.add)
                dve.tensor_copy(w1_of[:, at], own)
                for w in range(2):
                    for j in range(IMG_CHUNKS + 1):
                        a = img * T_IMG + j * T_STEP + E * w
                        last = dve.tensor_tensor(packing[:, w, j, :], ids[:, a:a + E], octal[:, :], ALU.mult)
                chained(last)
                chained(dve.tensor_reduce(words_f[:, :, :], packing[:, :, :, :], AX_X, ALU.add))
                n = img * IMG_CHUNKS
                dve.tensor_copy(words[:, :, n:n + IMG_CHUNKS + 1], words_f[:, :, :]).then_inc(table_ready, 1)
                torder.end()

            def fronted(j, ins):
                ins.then_inc(front_order, 1)
                dve.wait_ge(front_order, forder.next(j))

            def backed(i, ins):
                ins.then_inc(back_order, 1)
                dve.wait_ge(back_order, border.next(i))

            def norm_stats(nth, j, rows, ordered):
                for u in range(SUBS):
                    last = dve.bn_stats(stats[:, u, :], rows[:, u, :])
                ordered(j, last)
                dve.sem_inc(dve_gate, 1)
                for u in range(SUBS):
                    last = dve.bn_aggr(mv[:, u, :], stats[:, u, :])
                ordered(j, last)
                dve.tensor_scalar(var[:, :], mv[:, :, 1], LN_EPS, None, ALU.add).then_inc(var_ready[nth], 1)

            def normalize(nth, j, rows, dst, done):
                dve.wait_ge(rs_ready[nth], j + 1)
                for u in range(SUBS):
                    last = dve.tensor_scalar(dst(u), rows[:, u, :], mv[:, u, 0:1], rs[:, u:u + 1],
                                             ALU.subtract, ALU.mult)
                last.then_inc(done, 1)

            def first_stats(j):
                forder.begin()
                dve.wait_ge(x_kept, j + 1)
                norm_stats(0, j, xt, fronted)
                forder.end()

            def first_norm(j):
                normalize(0, j, xt, lambda u: nrm[:, u, :], n1_ready)

            def keep_k(j):
                dve.wait_ge(k_ready, j + 1)
                for n in range(HG):
                    rows = slice(HD * n, HD * (n + 1))
                    last = dve.tensor_scalar(kdiag[rows, 1, n, :], fa[rows, 1, :], bqk[rows, 3:4], None, ALU.add)
                last.then_inc(k_kept_dve, 1)

            def keep_v(j):
                dve.wait_ge(v_ready, j + 1)
                for h in range(2):
                    rows = slice(64 * h, 64 * h + 64)
                    for bank in range(2):
                        ws = slice(4 * bank, 4 * bank + 4)
                        last = dve.tensor_tensor(
                            vdiag[rows, ws, :, HD * h:HD * h + HD],
                            fa[rows, bank, :].rearrange("p (w g d) -> p w g d", w=4, d=HD),
                            bv[rows, :].rearrange("p (g d) -> p g d", d=HD).unsqueeze(1)
                            .broadcast_to([64, 4, PAIRS, HD]), ALU.add)
                last.then_inc(v_kept, 1)

            first_stats(0)
            first_norm(0)
            dve.wait_ge(weights_in, 16 * WEIGHTS)
            dve.wait_ge(tables, TABLES)
            keep_k(0)
            keep_v(0)
            first_stats(1)
            first_norm(1)

            GROUP = 2 * HEADS

            def grid(v):
                return prob[:, 2 * v:2 * v + 2, :].rearrange("p u (h k) -> p (u h) k", k=WIN)

            def wide(a, v):
                return a[:, v * GROUP:(v + 1) * GROUP].unsqueeze(2).broadcast_to([P, GROUP, WIN])

            def shift(i, v):
                last_step = isinstance(i, int) and i % IMG_CHUNKS == IMG_CHUNKS - 1
                for u in (2 * v, 2 * v + 1):
                    dve.wait_ge(scored, i * SUBS + u + 1)
                    table = bias[:, int(last_step and u == SUBS - 1), :]
                    ins = dve.scalar_tensor_tensor(prob[:, u, :], ga[:, u % 2, :], SCALE, table, ALU.mult, ALU.add)
                backed(i, ins)
                backed(i, dve.tensor_reduce(top[:, v * GROUP:(v + 1) * GROUP], grid(v), AX_X, ALU.max))
                dve.tensor_tensor(grid(v), grid(v), wide(top, v), ALU.subtract).then_inc(shifted, 1)

            def divide(i, v):
                half = slice(v * GROUP, (v + 1) * GROUP)
                dve.wait_ge(exped, 2 * i + v + 1)
                backed(i, dve.tensor_reduce(total[:, half], grid(v), AX_X, ALU.add))
                backed(i, dve.reciprocal(inverse[:, half], total[:, half]))
                dve.tensor_tensor(grid(v), grid(v), wide(inverse, v), ALU.mult).then_inc(probs_ready, 1)

            def second_norm(i, par):
                dve.wait_ge(projected, i + 1)
                dve.wait_ge(bo_added, i + 1)
                flat = res[:, par, :, :].rearrange("p u c -> p (u c)")
                backed(i, dve.tensor_tensor(flat, ga_all, flat, ALU.add))
                norm_stats(1, i, res[:, par, :, :], backed)

            def routed_on(i, ins):
                ins.then_inc(route_order, 1)
                dve.wait_ge(route_order, rorder.next(i))

            def over_e(a):
                return a[:, :].unsqueeze(2).broadcast_to([P, SUBS, E])

            def take_logits(i):
                rorder.begin()
                dve.wait_ge(routed, i + 1)
                logits = pf[:, 128:128 + SUBS * E].rearrange("p (u e) -> p u e", e=E)
                routed_on(i, dve.tensor_reduce(rmax[:, :], logits, AX_X, ALU.max))
                dve.tensor_tensor(rexp[:, :, :], logits, over_e(rmax), ALU.subtract).then_inc(route_in, 1)

            def route(i):
                dve.wait_ge(route_exp, i + 1)
                routed_on(i, dve.tensor_reduce(rsum[:, :], rexp[:, :, :], AX_X, ALU.add))
                routed_on(i, dve.reciprocal(rsum[:, :], rsum[:, :]))
                routed_on(i, dve.tensor_tensor(rprob[:, :, :], rexp[:, :, :], over_e(rsum), ALU.mult))
                mine = rprob[:, :, :].unsqueeze(3).broadcast_to([P, SUBS, E, E])
                other = rprob[:, :, :].unsqueeze(2).broadcast_to([P, SUBS, E, E])
                before_ = lower[:, :].rearrange("p (e f) -> p e f", f=E).unsqueeze(1).broadcast_to([P, SUBS, E, E])
                routed_on(i, dve.tensor_tensor(same[:, :, :, :], other, mine, ALU.is_equal))
                dve.tensor_tensor(more[:, :, :, :], other, mine, ALU.is_gt)
                routed_on(i, dve.tensor_tensor(same[:, :, :, :], same[:, :, :, :], before_, ALU.mult))
                routed_on(i, dve.tensor_tensor(more[:, :, :, :], more[:, :, :, :], same[:, :, :, :], ALU.add))
                routed_on(i, dve.tensor_reduce(rank[:, :, :], more[:, :, :, :], AX_X, ALU.add))
                routed_on(i, dve.tensor_scalar(sel[:, :, :], rank[:, :, :], 1.5, None, ALU.is_lt))
                routed_on(i, dve.tensor_tensor(chosen[:, :, :], sel[:, :, :], rprob[:, :, :], ALU.mult))
                routed_on(i, dve.tensor_reduce(rsum[:, :], chosen[:, :, :], AX_X, ALU.add))
                routed_on(i, dve.tensor_scalar(rsum[:, :], rsum[:, :], 1e-12, None, ALU.max))
                routed_on(i, dve.reciprocal(rsum[:, :], rsum[:, :]))
                dve.tensor_tensor(comb[:, :, :], chosen[:, :, :], over_e(rsum), ALU.mult).then_inc(comb_ready, 1)
                rorder.end()

            def step(i, par, img):
                att, exp, com = stages(img)
                front = att and has_front(i)
                m, c = i - IMG_CHUNKS, i - 2 * IMG_CHUNKS
                if att:
                    border.begin()
                    shift(i, 0)
                routes, new_image = has_routes(i, att), starts_image(i)
                if routes:
                    take_logits(i - 1)
                if routes and new_image:
                    route(i - 1)
                    places(i - 1, 1 - par, img - 1)
                    tile_table(img - 1)
                if att:
                    divide(i, 0)
                    shift(i, 1)
                if com:
                    which = c if isinstance(c, int) else upto(c, STEPS - 1)
                    dve.tensor_copy(cgate[:, par, :], gate_hist[:, which, :])
                    mine = (P, TOP_K * SUBS, E)
                    ins = dve.tensor_tensor(region_of[:, :, :], row_hist[:, which, :].unsqueeze(2).broadcast_to(mine),
                                            region[:, img % 2, :].unsqueeze(1).broadcast_to(mine), ALU.is_ge)
                    ins.then_inc(cidx_order, 1)
                    dve.wait_ge(cidx_order, 3 * c + 1)
                    dve.tensor_tensor(region_of[:, :, :], region_of[:, :, :],
                                      shrink[:, img % 2, :].unsqueeze(1).broadcast_to(mine), ALU.mult)\
                       .then_inc(cidx_order, 1)
                    dve.wait_ge(cidx_order, 3 * c + 2)
                    dve.tensor_reduce(shift_by[:, :], region_of[:, :, :], AX_X, ALU.add).then_inc(cidx_order, 1)
                    dve.wait_ge(cidx_order, 3 * c + 3)
                    dve.tensor_tensor(cidx[:, par, :], row_hist[:, which, :], shift_by[:, :], ALU.subtract)\
                       .then_inc(cidx_ready, 1)
                who = None
                if exp:
                    if starts_image(m):
                        dve.wait_ge(experts_in, 16 * EXPERTS)
                        dve.wait_ge(table_ready, img)
                        dve.sem_inc(dve_gate, 1)
                    who = expert_of(dve, m)

                def slot(t):
                    if exp:
                        expert_slot(m, t, par, who)

                slot(0)
                if att:
                    divide(i, 1)
                if front:
                    keep_k(i + 1)
                slot(1)
                slot(2)
                if routes and not new_image:
                    route(i - 1)
                slot(3)
                slot(4)
                if com:
                    dve.wait_ge(acc_in, (c + 1) * 16)
                    for u in range(SUBS):
                        dve.wait_ge(got_in[u], (c + 1) * 32)
                        dve.scalar_tensor_tensor(acc[:, u, :], got[:, 0, u, :], cgate[:, par, u:u + 1], acc[:, u, :],
                                                 ALU.mult, ALU.add).then_inc(acc_half, 1)
                    for u in range(SUBS):
                        dve.wait_ge(acc_half, c * SUBS + u + 1)
                        dve.scalar_tensor_tensor(acc[:, u, :], got[:, 1, u, :], cgate[:, par, SUBS + u:SUBS + u + 1],
                                                 acc[:, u, :], ALU.mult, ALU.add).then_inc(acc_done, 1)
                slot(5)
                if front:
                    keep_v(i + 1)
                if att:
                    second_norm(i, par)
                slot(6)
                if att:
                    at_least(dve, scattered[par], half_of(i) * SCATTER)
                    normalize(1, i, res[:, par, :, :], lambda u: tok[:, par, u, :], n2_ready)
                    border.end()
                slot(7)
                if routes and not new_image:
                    places(i - 1, 1 - par, img)
                if att and has_input(i):
                    first_stats(i + 2)
                if att and has_input(i):
                    first_norm(i + 2)
                slot(8)

            def flush():
                who = expert_of(dve, STEPS)
                for t in range(OUT_LAG):
                    expert_slot(STEPS, t, 0, who)

            steps(dve, step, flush)

        @block.tensor
        def _(pe):
            def turn(dst, src):
                return pe.matmul(dst, src, ident[:, :], is_transpose=True, start=True, stop=True)

            def expert_slot(m, t, par, who):
                g = tile(m, t, 0)
                if g is not None:
                    pe.wait_ge(xs_in[t % AHEAD], (m * (T_STEP // AHEAD) + t // AHEAD + 1) * 32)
                    at_least(pe, xs_kept, g)
                    for h in range(HALVES):
                        last = turn(pt[:, h * P:(h + 1) * P], xs[:, t % AHEAD, h * P:(h + 1) * P])
                    last.then_inc(xs_turned, 1)
                g = tile(m, t, HID_LAG)
                if g is not None:
                    pe.wait_ge(xs_kept, g + 1)
                    at_least(pe, hid_kept, g)
                    r = (t - HID_LAG) % AHEAD
                    for f in range(HALVES):
                        for h in range(HALVES):
                            last = pe.matmul(ph[:, f * P:(f + 1) * P], w1[:, r, h, f * P:(f + 1) * P],
                                             xs_t[:, (par + t + 1) % 2, h, :], start=(h == 0), stop=(h == HALVES - 1))
                    last.then_inc(hid_ready, 1)
                g = tile(m, t, OUT_LAG)
                if g is not None:
                    pe.wait_ge(hid_kept, g + 1)
                    at_least(pe, y_kept, g)
                    e = who(t, OUT_LAG)
                    for f in range(HALVES):
                        last = pe.matmul(py[:, 0:C], hid_t[:, (par + t) % 2, f, :], w2[:, f, e, :],
                                         start=(f == 0), stop=(f == HALVES - 1))
                    last.then_inc(y_ready, 1)

            def turn_x(j, par):
                pe.wait_ge(summed, j + 1)
                at_least(pe, v_kept, j)
                for u in range(SUBS):
                    for h in range(HALVES):
                        at = (2 * (u % 2) + h) * P
                        last = turn(fa[:, u // 2, at:at + P], xl[:, par, h, u * P:(u + 1) * P])
                last.then_inc(x_turned, 1)

            def turn_normed(j):
                pe.wait_ge(n1_ready, j + 1)
                for h in range(HALVES):
                    for u in range(SUBS):
                        last = turn(fa[:, h, u * P:(u + 1) * P], nrm[:, u, h * P:(h + 1) * P])
                last.then_inc(n1_turned, 1)

            def make_qk(first_n, ready):
                for n in (0, 1):
                    cols = slice((first_n + n) * P, (first_n + n + 1) * P)
                    for h in range(HALVES):
                        last = pe.matmul(fa[:, n, :], wqk[:, h, cols], nrm_t[:, h, :],
                                         start=(h == 0), stop=(h == HALVES - 1))
                last.then_inc(ready, 1)

            def make_q(j):
                pe.wait_ge(n1_kept, j + 1)
                make_qk(0, q_ready)

            def make_k(j):
                pe.wait_ge(q_kept, j + 1)
                make_qk(2, k_ready)

            def make_v(j):
                pe.wait_ge(k_kept_act, j + 1)
                pe.wait_ge(k_kept_dve, j + 1)
                for w in range(WINS):
                    for parity in range(2):
                        for h in range(HALVES):
                            last = pe.matmul(fa[64 * parity:64 * parity + 64, w // 4, (w % 4) * P:(w % 4 + 1) * P],
                                             nrm_t[:, h, w * WIN:(w + 1) * WIN], wv[:, h, parity, :],
                                             start=(h == 0), stop=(h == HALVES - 1))
                last.then_inc(v_ready, 1)

            def score(i, v):
                for u in (2 * v, 2 * v + 1):
                    for side in range(2):
                        cols = slice((2 * u + side) * WIN, (2 * u + side + 1) * WIN)
                        for g in range(HALVES):
                            last = pe.matmul(ga[64 * side:64 * side + 64, u % 2, g * 256:g * 256 + 256],
                                             qt[:, g, cols], kdiag[:, g, :, cols], start=True, stop=True)
                    last.then_inc(scored, 1)

            def turn_probs(i, v):
                pe.wait_ge(probs_ready, 2 * i + v + 1)
                for u in (2 * v, 2 * v + 1):
                    for g in range(PAIRS):
                        last = turn(ga[:, u % 2, g * P:(g + 1) * P], prob[:, u, g * P:(g + 1) * P])
                    last.then_inc(p_turned, 1)

            def count_before(i):
                pe.wait_ge(comb_ready, i + 1)
                chosen_by = sel[:, :, :].rearrange("p u e -> p (u e)")
                pe.matmul(pf[:, 0:SUBS * E], strict[:, :], chosen_by, start=True, stop=False)
                for u in range(1, SUBS):
                    pe.matmul(pf[:, u * E:SUBS * E], ones[:, :], chosen_by[:, 0:(SUBS - u) * E],
                              start=False, stop=(u == SUBS - 1))
                for u in range(SUBS):
                    last = pe.matmul(pf[:, 64:64 + E], ones[:, :], sel[:, u, :], start=(u == 0), stop=(u == SUBS - 1))
                last.then_inc(ranked, 1)

            turn_x(0, 0)
            turn_normed(0)
            pe.wait_ge(weights_in, 16 * WEIGHTS)
            pe.matmul(ga[:, 0, :], flip, rel, start=True, stop=True).then_inc(bias_turned, 1)
            make_q(0)
            make_k(0)
            pe.wait_ge(tables, TABLES)
            make_v(0)
            turn_x(1, 1)

            def step(i, par, img):
                att, exp, com = stages(img)
                front = att and has_front(i)
                m, c = i - IMG_CHUNKS, i - 2 * IMG_CHUNKS
                if att:
                    pe.wait_ge(k_kept_act, i + 1)
                    pe.wait_ge(k_kept_dve, i + 1)
                    at_least(pe, n2_kept, i)
                    score(i, 0)
                if front:
                    turn_normed(i + 1)
                    make_q(i + 1)
                if att:
                    pe.wait_ge(shifted, 2 * i + 1)
                    score(i, 1)
                routes, new_image = has_routes(i, att), starts_image(i)
                if routes and new_image:
                    count_before(i - 1)
                who = None
                if exp:
                    if starts_image(m):
                        pe.wait_ge(experts_in, 16 * EXPERTS)
                        pe.wait_ge(table_ready, img)
                        pe.sem_inc(pe_gate, 1)
                    who = expert_of(pe, m)

                def slot(t):
                    if exp:
                        expert_slot(m, t, par, who)

                slot(0)
                if front:
                    make_k(i + 1)
                slot(1)
                if att:
                    pe.wait_ge(shifted, 2 * i + 2)
                    turn_probs(i, 0)
                slot(2)
                if att:
                    pe.wait_ge(p_kept, i * SUBS + 2)
                    turn_probs(i, 1)
                slot(3)
                if att:
                    pe.wait_ge(p_kept, (i + 1) * SUBS)
                    pe.wait_ge(v_kept, i + 1)
                    for w in range(WINS):
                        for g in range(PAIRS):
                            at = g * P + (w % 2) * WIN
                            rows = slice(64 * (g % 2), 64 * (g % 2) + 64)
                            last = pe.matmul(ga[rows, g // 2, w * WIN:(w + 1) * WIN], vdiag[:, w, g, :],
                                             prob_t[:, w // 2, at:at + WIN], start=True, stop=True)
                    last.then_inc(mixed_v, 1)
                slot(4)
                if front:
                    make_v(i + 1)
                slot(5)
                if att:
                    pe.wait_ge(att_kept, i + 1)
                    for u in range(SUBS):
                        for h in range(HALVES):
                            last = pe.matmul(ga[:, u // 2, (u % 2) * C:(u % 2) * C + C],
                                             att_t[:, h, u * P:(u + 1) * P], wo[:, h, :],
                                             start=(h == 0), stop=(h == HALVES - 1))
                    last.then_inc(projected, 1)
                slot(6)
                if com:
                    for v in range(2):
                        pe.wait_ge(acc_done, c * SUBS + 2 * v + 2)
                        at_least(pe, out_kept, c * 2 + v)
                        if routes:
                            pe.wait_ge(placed if new_image else route_in, i)
                        for h in range(HALVES):
                            for u in (2 * v, 2 * v + 1):
                                at = h * 256 + (u % 2) * P
                                last = turn(pf[:, at:at + P], acc[:, u, h * P:(h + 1) * P])
                        last.then_inc(out_turned, 1)
                if att and has_input(i):
                    turn_x(i + 2, par)
                slot(7)
                if routes and not new_image:
                    if com:
                        pe.wait_ge(out_kept, (c + 1) * 2)
                    count_before(i - 1)
                if att:
                    pe.wait_ge(n2_ready, i + 1)
                    for h in range(HALVES):
                        for u in range(SUBS):
                            last = turn(ga[:, h, u * P:(u + 1) * P], tok[:, par, u, h * P:(h + 1) * P])
                    last.then_inc(n2_turned, 1)
                slot(8)
                if att:
                    pe.wait_ge(n2_kept, i + 1)
                    if com:
                        pe.wait_ge(out_kept, (c + 1) * 2)
                    if routes:
                        pe.wait_ge(placed, i)
                    for u in range(SUBS):
                        for h in range(HALVES):
                            last = pe.matmul(pf[:, 128 + u * E:128 + (u + 1) * E], tok_t[:, h, u * P:(u + 1) * P],
                                             wr[:, h, :], start=(h == 0), stop=(h == HALVES - 1))
                    last.then_inc(routed, 1)

            def flush():
                who = expert_of(pe, STEPS)
                for t in range(OUT_LAG):
                    expert_slot(STEPS, t, 0, who)

            steps(pe, step, flush)


def keep_buffers(nc, ctx):
    return {
        "ident": ctx.enter_context(nc.sbuf_tensor("ident", [P, P], F32)),
        "bn_scale": ctx.enter_context(nc.sbuf_tensor("bn_scale", [P, HALVES], F32)),
        "bn_shift": ctx.enter_context(nc.sbuf_tensor("bn_shift", [P, HALVES], F32)),
    }


def gather_buffers(nc, ctx):
    return {
        "idx_all": ctx.enter_context(nc.sbuf_tensor("idx_all", [P, B, 2, 4, PXT, TAPS], I32)),
        "wts_all": ctx.enter_context(nc.sbuf_tensor("wts_all", [P, B, 2, 4, PXT, TAPS, CORNERS], F32)),
    }


def constants():
    import numpy as np

    chan = np.arange(P)
    group = (chan[:, None] // (C // 32) == chan[None, :] // (C // 32)).astype(np.float32) / (C // 32)
    p, r, q, j, t = np.ogrid[0:P, 0:2, 0:PXT, 0:4, 0:TAPS]
    base = np.zeros((P, 2, PXT, 4, TAPS, 2), np.float32)
    base[..., 0] = 2 * (16 * r + 4 * j + q) + p // W + t // 3 - 1
    base[..., 1] = p % W + t % 3 - 1 + 0 * (r + q + j)
    here = np.zeros((P, HEADS, WIN), np.float32)
    first = np.arange(P)[:, None] % WIN < SHIFT
    apart = (first != (np.arange(WIN)[None, :] < SHIFT)) & (np.arange(P)[:, None] >= WIN)
    here[:] = np.where(apart, np.float32(-1e30), np.float32(0))[:, None, :]
    flip = (np.arange(WIN)[:, None] == WIN - 1 - np.arange(P)[None, :] % WIN).astype(np.float32)
    lower = (np.arange(E)[None, :] < np.arange(E)[:, None]).astype(np.float32)
    region_rows, octal = N + P, 8 ** np.arange(E)
    e = np.arange(E)
    return {
        "strict_c": (np.arange(P)[:, None] < np.arange(P)[None, :]).astype(np.float32),
        "region_c": np.broadcast_to(np.concatenate([e * region_rows, (E + e) * region_rows]).astype(np.float32) + 1,
                                    (P, 2 * E)).copy(),
        "row_id_c": (e[None, :] * region_rows + np.arange(P)[:, None]).astype(np.float32),
        "octal_c": octal.astype(np.float32)[None, :],
        "tile_id_c": np.arange(EXPERT_TILES, dtype=np.float32)[None, :],
        "ident_c": np.eye(P, dtype=np.float32),
        "group_c": group,
        "base_c": base.reshape(P, -1),
        "flip_c": flip,
        "apart_c": here.reshape(P, -1),
        "lower_c": np.broadcast_to(lower.reshape(1, -1), (P, E * E)).copy(),
    }


def build(nc, d, out):
    with ExitStack() as ctx:
        table = nc.dram_tensor("table", (B * ENTRIES, CORNERS * C), F32, kind="Internal").ap()
        conv = nc.dram_tensor("conv_raw", (C, B * N), F32, kind="Internal").ap()
        keep = keep_buffers(nc, ctx)
        with ExitStack() as inner:
            both = {**keep, **gather_buffers(nc, inner)}
            sample_table_stage(nc, d["x"], d["w_off"], d["b_off"], table, both, d)
            conv_stage(nc, d["w_conv"], d["gamma"], d["beta"], table, conv, both)
        token_stage(nc, d["x"], conv, d, out, keep)


def laid_out(inputs):
    import numpy as np

    def a(name):
        return np.asarray(inputs[name])

    w_qkv, b_qkv = a("L1_attn_w_qkv"), a("L1_attn_b_qkv")
    even_odd = (PAIRS, 2, HD)
    d = {
        "x": a("x"),
        "w_off": a("L0_conv_w_off").reshape(OFFS, C, TAPS).transpose(1, 2, 0),
        "b_off": a("L0_conv_b_off"),
        "w_conv": a("L0_conv_w_conv").reshape(C, C, TAPS).transpose(1, 2, 0),
        "gamma": a("L0_conv_gamma"),
        "beta": a("L0_conv_beta"),
        "w_qk": w_qkv[:2 * C].T,
        "w_v": w_qkv[2 * C:].T.reshape(C, *even_odd).transpose(0, 2, 1, 3).reshape(C, C),
        "b_qk": b_qkv[:2 * C].reshape(4, P).T,
        "b_v": b_qkv[2 * C:].reshape(even_odd).transpose(1, 0, 2).reshape(2, P),
        "rel_rev": a("L1_attn_rel_pos")[:, ::-1],
        "w_out": a("L1_attn_w_out").T,
        "b_out": a("L1_attn_b_out"),
        "w_router": a("L1_ffn_router_w").T,
        "w_1": a("L1_ffn_w1"),
        "b_1": a("L1_ffn_b1").reshape(E, HALVES, P).transpose(2, 0, 1).reshape(P, E * HALVES),
        "w_2": a("L1_ffn_w2"),
        "b_2": a("L1_ffn_b2").reshape(E * C),
        **constants(),
    }
    return {name: np.ascontiguousarray(v) for name, v in d.items()}


def kernel(**inputs):
    import concourse.bacc as bacc
    from concourse.bass_utils import run_bass_kernel_spmd

    nc = bacc.Bacc("TRN2", target_bir_lowering=False, num_devices=1)
    arrays = laid_out(inputs)
    d = {name: nc.dram_tensor("in_" + name, v.shape, mybir.dt.from_np(v.dtype), kind="ExternalInput").ap()
         for name, v in arrays.items()}
    out = nc.dram_tensor("out", (B, C, H, W), F32, kind="ExternalOutput").ap()
    build(nc, d, out)
    r = run_bass_kernel_spmd(nc, [{"in_" + name: v for name, v in arrays.items()}], core_ids=[0])
    return r.results[0]["out"]
```
